# Optimizing a Trainium2 kernel written in Bass

```python
import numpy as np
import jax
import jax.numpy as jnp

def _softmax(x, axis=-1):
    return jax.nn.softmax(x, axis=axis)

def _gelu(x):
    return jax.nn.gelu(x, approximate=True)

def _silu(x):
    return jax.nn.silu(x)

def _sigmoid(x):
    return jax.nn.sigmoid(x)

def _layernorm(x, axis=-1, eps=1e-05):
    m = jnp.mean(x, axis=axis, keepdims=True)
    v = jnp.var(x, axis=axis, keepdims=True)
    return (x - m) / jnp.sqrt(v + eps)

def _scatter_add(tgt, idx, src, axis=0):
    return tgt.at[idx].add(src)

def _segment_sum(src, seg, n):
    return jax.ops.segment_sum(src, seg, n)
kernel_name = 'mk_gnn_ffn_d2_gnn_r32_d1532f'

def setup_inputs(seed: int=0):
    np.random.seed(seed)
    _w = jnp.asarray

    def _rec_inputs():
        import jax
        import jax.numpy as jnp
        _gk = jax.random.key(seed)
        x = -0.0003713 + 1 * jax.random.normal(jax.random.fold_in(_gk, 1), (3125, 256), jnp.float32)
        src = jax.random.randint(jax.random.fold_in(_gk, 2), (50000,), 0, 3125, jnp.int32)
        dst = jnp.minimum((3125 * jax.random.uniform(jax.random.fold_in(_gk, 3), (50000,)) ** 2.0).astype(jnp.int32), 99999)
        _o = jnp.argsort(dst, stable=True)
        src = src[_o]
        dst = dst[_o]
        edge_type_8 = jax.random.randint(jax.random.fold_in(_gk, 12), (50000,), 0, 8, jnp.int32)
        node_type_4 = jax.random.randint(jax.random.fold_in(_gk, 13), (3125,), 0, 4, jnp.int32)
        return (x, src, dst, edge_type_8, node_type_4)
    x, src, dst, edge_type_8, node_type_4 = _rec_inputs()

    def _L0_gnn_setup():
        import jax, jax.numpy as jnp
        import numpy as np
        N, E = (50000, 25000)
        IN_DIM = OUT_DIM = 256
        T, R, H = (4, 8, 8)
        DK = OUT_DIM // H

        def typed_linear(x, node_type, W, b):
            out = jnp.zeros((x.shape[0], W.shape[2]), dtype=x.dtype)
            for t in range(W.shape[0]):
                y = x @ W[t] + b[t]
                out = jnp.where((node_type == t)[:, None], y, out)
            return out
        key = jax.random.key(seed)
        ks = jax.random.split(key, 16)
        x = jax.random.normal(ks[0], (N, IN_DIM), dtype=jnp.float32)
        node_type = jax.random.randint(ks[1], (N,), 0, T, dtype=jnp.int32)
        src = jax.random.randint(ks[2], (E,), 0, N, dtype=jnp.int32)
        dst = jnp.arange(E, dtype=jnp.int32) % N
        etype = jax.random.randint(ks[3], (E,), 0, R, dtype=jnp.int32)
        w_scale = np.sqrt(2.0 / (IN_DIM + OUT_DIM)).astype(np.float32)
        r_scale = np.sqrt(2.0 / (DK + DK)).astype(np.float32)

        def lin(k):
            return jax.random.normal(k, (T, IN_DIM, OUT_DIM), dtype=jnp.float32) * w_scale
        return {'x': x, 'node_type': node_type, 'src': src, 'dst': dst, 'etype': etype, 'Wk': lin(ks[4]), 'bk': jnp.zeros((T, OUT_DIM), jnp.float32), 'Wq': lin(ks[5]), 'bq': jnp.zeros((T, OUT_DIM), jnp.float32), 'Wv': lin(ks[6]), 'bv': jnp.zeros((T, OUT_DIM), jnp.float32), 'Wa': lin(ks[7]), 'ba': jnp.zeros((T, OUT_DIM), jnp.float32), 'rel_att': jax.random.normal(ks[8], (R, H, DK, DK), jnp.float32) * r_scale, 'rel_msg': jax.random.normal(ks[9], (R, H, DK, DK), jnp.float32) * r_scale, 'rel_pri': jnp.ones((R, H), jnp.float32), 'skip': jnp.ones((T,), jnp.float32)}
    _L0_gnn_all = _L0_gnn_setup()
    _L0_gnn_in = {k: v for k, v in _L0_gnn_all.items() if k in ('Wk', 'bk', 'Wq', 'bq', 'Wv', 'bv', 'Wa', 'ba', 'rel_att', 'rel_msg', 'rel_pri', 'skip')}
    del _L0_gnn_all

    def _L0_ffn_setup():
        import jax, jax.numpy as jnp
        import numpy as np
        TOP_K = 2
        LN_EPS = 1e-05
        key = jax.random.key(seed)
        ks = jax.random.split(key, 8)
        B, S, D, E, H = (16, 1024, 256, 8, 1024)
        x = jax.random.normal(ks[0], (B, S, D), dtype=jnp.float32)
        Wr = jax.random.normal(ks[1], (D, E), dtype=jnp.float32) * 0.1
        br = jnp.zeros((E,), dtype=jnp.float32)
        ln_g = jnp.ones((E, D), dtype=jnp.float32)
        ln_b = jnp.zeros((E, D), dtype=jnp.float32)
        W1 = jax.random.normal(ks[2], (E, D, H), dtype=jnp.float32) * (1.0 / np.sqrt(D))
        b1 = jnp.zeros((E, H), dtype=jnp.float32)
        W2 = jax.random.normal(ks[3], (E, H, D), dtype=jnp.float32) * (1.0 / np.sqrt(H))
        b2 = jnp.zeros((E, D), dtype=jnp.float32)
        return {'x': x, 'Wr': Wr, 'br': br, 'ln_g': ln_g, 'ln_b': ln_b, 'W1': W1, 'b1': b1, 'W2': W2, 'b2': b2}
    _L0_ffn_all = _L0_ffn_setup()
    _L0_ffn_in = {k: v for k, v in _L0_ffn_all.items() if k in ('Wr', 'br', 'ln_g', 'ln_b', 'W1', 'b1', 'W2', 'b2')}
    del _L0_ffn_all

    def _L1_gnn_setup():
        import jax, jax.numpy as jnp
        import numpy as np
        N_NODES = 50000
        N_EDGES = 25000
        D = 256
        NUM_STEPS = 6
        key = jax.random.key(seed)
        ks = jax.random.split(key, 12)
        s = 1.0 / np.sqrt(D)
        return {'node_feats': jax.random.normal(ks[0], (N_NODES, D), jnp.float32), 'W1': jax.random.normal(ks[1], (D, D), jnp.float32) * s, 'b1': jax.random.normal(ks[2], (D,), jnp.float32) * s, 'W2': jax.random.normal(ks[3], (D, D), jnp.float32) * s, 'b2': jax.random.normal(ks[4], (D,), jnp.float32) * s, 'W_ih': jax.random.normal(ks[5], (3 * D, D), jnp.float32) * s, 'b_ih': jax.random.normal(ks[6], (3 * D,), jnp.float32) * s, 'W_hh': jax.random.normal(ks[7], (3 * D, D), jnp.float32) * s, 'b_hh': jax.random.normal(ks[8], (3 * D,), jnp.float32) * s, 'src': jax.random.randint(ks[9], (N_EDGES,), 0, N_NODES, jnp.int32), 'dst': jax.random.randint(ks[10], (N_EDGES,), 0, N_NODES, jnp.int32)}
    _L1_gnn_all = _L1_gnn_setup()
    _L1_gnn_in = {k: v for k, v in _L1_gnn_all.items() if k in ('W1', 'b1', 'W2', 'b2', 'W_ih', 'b_ih', 'W_hh', 'b_hh')}
    del _L1_gnn_all

    def _L1_ffn_setup():
        import jax, jax.numpy as jnp
        import numpy as np
        B, N, D = (16, 128, 256)
        NUM_EXPERTS, TOP_K, HEADS = (4, 2, 4)
        N_EDGES = 32768
        LN_EPS = 1e-05

        def _layernorm(x, g, b):
            mu = x.mean(-1, keepdims=True)
            var = ((x - mu) ** 2).mean(-1, keepdims=True)
            return (x - mu) * jax.lax.rsqrt(var + LN_EPS) * g + b

        def _forward(x, edge_index, W_gat, att_src, att_dst, b_gat, ln_gamma, ln_beta, W1, b1, W2, b2):
            Bc, Nc, Dc = x.shape
            M = Bc * Nc
            x_flat = x.reshape(M, Dc)
            h = (x_flat @ W_gat).reshape(M, HEADS, NUM_EXPERTS)
            loops = jnp.arange(M, dtype=edge_index.dtype)
            src = jnp.concatenate([edge_index[0], loops])
            dst = jnp.concatenate([edge_index[1], loops])
            a_src = (h * att_src).sum(-1)
            a_dst = (h * att_dst).sum(-1)
            e = jax.nn.leaky_relu(a_src[src] + a_dst[dst], negative_slope=0.2)
            e_max = jax.ops.segment_max(e, dst, num_segments=M)
            ee = jnp.exp(e - e_max[dst])
            denom = jax.ops.segment_sum(ee, dst, num_segments=M)
            alpha = ee / (denom[dst] + 1e-16)
            msg = h[src] * alpha[:, :, None]
            agg = jax.ops.segment_sum(msg, dst, num_segments=M).reshape(M, HEADS * NUM_EXPERTS) + b_gat
            scores = _layernorm(agg, ln_gamma, ln_beta).reshape(M, HEADS, NUM_EXPERTS).mean(1)
            scores = scores.reshape(Bc, Nc, NUM_EXPERTS)
            topk_s, topk_i = jax.lax.top_k(scores, TOP_K)
            w = jax.nn.softmax(topk_s, axis=-1)
            out = jnp.zeros_like(x)
            for ei in range(NUM_EXPERTS):
                g = jnp.where(topk_i == ei, w, 0.0).sum(-1)
                hh = jax.nn.gelu(x @ W1[ei] + b1[ei], approximate=False)
                out = out + g[..., None] * (hh @ W2[ei] + b2[ei])
            return out
        key = jax.random.key(seed)
        ks = jax.random.split(key, 8)
        s = 0.05
        return {'x': jax.random.normal(ks[0], (B, N, D), jnp.float32), 'W_gat': jax.random.normal(ks[1], (D, HEADS * NUM_EXPERTS), jnp.float32) * s, 'att_src': jax.random.normal(ks[2], (HEADS, NUM_EXPERTS), jnp.float32) * s, 'att_dst': jax.random.normal(ks[3], (HEADS, NUM_EXPERTS), jnp.float32) * s, 'b_gat': jnp.zeros((HEADS * NUM_EXPERTS,), jnp.float32), 'ln_gamma': jnp.ones((HEADS * NUM_EXPERTS,), jnp.float32), 'ln_beta': jnp.zeros((HEADS * NUM_EXPERTS,), jnp.float32), 'W1': jax.random.normal(ks[4], (NUM_EXPERTS, D, 2 * D), jnp.float32) * s, 'b1': jnp.zeros((NUM_EXPERTS, 2 * D), jnp.float32), 'W2': jax.random.normal(ks[5], (NUM_EXPERTS, 2 * D, D), jnp.float32) * s, 'b2': jnp.zeros((NUM_EXPERTS, D), jnp.float32), 'edge_index': jax.random.randint(ks[6], (2, N_EDGES), 0, B * N, jnp.int32)}
    _L1_ffn_all = _L1_ffn_setup()
    _L1_ffn_in = {k: v for k, v in _L1_ffn_all.items() if k in ('W_gat', 'att_src', 'att_dst', 'b_gat', 'ln_gamma', 'ln_beta', 'W1', 'b1', 'W2', 'b2', 'edge_index')}
    del _L1_ffn_all
    return {'x': x, 'src': src, 'dst': dst, 'edge_type_8': edge_type_8, 'node_type_4': node_type_4, 'L0_gnn_Wk': _L0_gnn_in['Wk'], 'L0_gnn_bk': _L0_gnn_in['bk'], 'L0_gnn_Wq': _L0_gnn_in['Wq'], 'L0_gnn_bq': _L0_gnn_in['bq'], 'L0_gnn_Wv': _L0_gnn_in['Wv'], 'L0_gnn_bv': _L0_gnn_in['bv'], 'L0_gnn_Wa': _L0_gnn_in['Wa'], 'L0_gnn_ba': _L0_gnn_in['ba'], 'L0_gnn_rel_att': _L0_gnn_in['rel_att'], 'L0_gnn_rel_msg': _L0_gnn_in['rel_msg'], 'L0_gnn_rel_pri': _L0_gnn_in['rel_pri'], 'L0_gnn_skip': _L0_gnn_in['skip'], 'L0_ffn_Wr': _L0_ffn_in['Wr'], 'L0_ffn_br': _L0_ffn_in['br'], 'L0_ffn_ln_g': _L0_ffn_in['ln_g'], 'L0_ffn_ln_b': _L0_ffn_in['ln_b'], 'L0_ffn_W1': _L0_ffn_in['W1'], 'L0_ffn_b1': _L0_ffn_in['b1'], 'L0_ffn_W2': _L0_ffn_in['W2'], 'L0_ffn_b2': _L0_ffn_in['b2'], 'L1_gnn_W1': _L1_gnn_in['W1'], 'L1_gnn_b1': _L1_gnn_in['b1'], 'L1_gnn_W2': _L1_gnn_in['W2'], 'L1_gnn_b2': _L1_gnn_in['b2'], 'L1_gnn_W_ih': _L1_gnn_in['W_ih'], 'L1_gnn_b_ih': _L1_gnn_in['b_ih'], 'L1_gnn_W_hh': _L1_gnn_in['W_hh'], 'L1_gnn_b_hh': _L1_gnn_in['b_hh'], 'L1_ffn_W_gat': _L1_ffn_in['W_gat'], 'L1_ffn_att_src': _L1_ffn_in['att_src'], 'L1_ffn_att_dst': _L1_ffn_in['att_dst'], 'L1_ffn_b_gat': _L1_ffn_in['b_gat'], 'L1_ffn_ln_gamma': _L1_ffn_in['ln_gamma'], 'L1_ffn_ln_beta': _L1_ffn_in['ln_beta'], 'L1_ffn_W1': _L1_ffn_in['W1'], 'L1_ffn_b1': _L1_ffn_in['b1'], 'L1_ffn_W2': _L1_ffn_in['W2'], 'L1_ffn_b2': _L1_ffn_in['b2'], 'L1_ffn_edge_index': _L1_ffn_in['edge_index']}

def reference(x, src, dst, edge_type_8, node_type_4, L0_gnn_Wk, L0_gnn_bk, L0_gnn_Wq, L0_gnn_bq, L0_gnn_Wv, L0_gnn_bv, L0_gnn_Wa, L0_gnn_ba, L0_gnn_rel_att, L0_gnn_rel_msg, L0_gnn_rel_pri, L0_gnn_skip, L0_ffn_Wr, L0_ffn_br, L0_ffn_ln_g, L0_ffn_ln_b, L0_ffn_W1, L0_ffn_b1, L0_ffn_W2, L0_ffn_b2, L1_gnn_W1, L1_gnn_b1, L1_gnn_W2, L1_gnn_b2, L1_gnn_W_ih, L1_gnn_b_ih, L1_gnn_W_hh, L1_gnn_b_hh, L1_ffn_W_gat, L1_ffn_att_src, L1_ffn_att_dst, L1_ffn_b_gat, L1_ffn_ln_gamma, L1_ffn_ln_beta, L1_ffn_W1, L1_ffn_b1, L1_ffn_W2, L1_ffn_b2, L1_ffn_edge_index):
    import jax
    import jax.numpy as jnp

    def _L0_gnn_ref(x, node_type, src, dst, etype, Wk, bk, Wq, bq, Wv, bv, Wa, ba, rel_att, rel_msg, rel_pri, skip):
        import jax, jax.numpy as jnp
        import numpy as np
        N, E = (50000, 25000)
        IN_DIM = OUT_DIM = 256
        T, R, H = (4, 8, 8)
        DK = OUT_DIM // H

        def typed_linear(x, node_type, W, b):
            out = jnp.zeros((x.shape[0], W.shape[2]), dtype=x.dtype)
            for t in range(W.shape[0]):
                y = x @ W[t] + b[t]
                out = jnp.where((node_type == t)[:, None], y, out)
            return out
        n = x.shape[0]
        r = rel_att.shape[0]
        h, dk = (rel_att.shape[1], rel_att.shape[2])
        sqrt_dk = jnp.asarray(np.sqrt(dk), x.dtype)
        k = typed_linear(x, node_type, Wk, bk).reshape(n, h, dk)
        q = typed_linear(x, node_type, Wq, bq).reshape(n, h, dk)
        v = typed_linear(x, node_type, Wv, bv).reshape(n, h, dk)
        k_r = jnp.einsum('nhd,rhde->rnhe', k, rel_att)
        v_r = jnp.einsum('nhd,rhde->rnhe', v, rel_msg)
        key_e = k_r[etype, src]
        val_e = v_r[etype, src]
        att = (q[dst] * key_e).sum(-1) * rel_pri[etype] / sqrt_dk
        seg = dst * r + etype
        s = n * r
        m = jax.ops.segment_max(att, seg, num_segments=s)
        ex = jnp.exp(att - m[seg])
        den = jax.ops.segment_sum(ex, seg, num_segments=s)
        alpha = ex / den[seg]
        hmsg = jax.ops.segment_sum(alpha[..., None] * val_e, seg, num_segments=s)
        hmsg = hmsg.reshape(n, r, h * dk)
        cnt = jax.ops.segment_sum(jnp.ones((att.shape[0],), x.dtype), seg, num_segments=s)
        present = (cnt.reshape(n, r) > 0).astype(x.dtype)
        t = hmsg.sum(1) / jnp.maximum(present.sum(1, keepdims=True), 1.0)
        trans = typed_linear(t, node_type, Wa, ba)
        a = jax.nn.sigmoid(skip)[node_type][:, None]
        return trans * a + x * (1.0 - a)

    def _L0_ffn_ref(x, Wr, br, ln_g, ln_b, W1, b1, W2, b2):
        import jax, jax.numpy as jnp
        import numpy as np
        TOP_K = 2
        LN_EPS = 1e-05
        B, S, D = x.shape
        N = B * S
        xt = x.reshape(N, D)
        logits = xt @ Wr + br
        probs = jax.nn.softmax(logits, axis=-1)
        top_p, top_idx = jax.lax.top_k(probs, TOP_K)
        weights = top_p / top_p.sum(axis=-1, keepdims=True)
        mu = xt.mean(axis=-1, keepdims=True)
        var = ((xt - mu) ** 2).mean(axis=-1, keepdims=True)
        xn = (xt - mu) * jax.lax.rsqrt(var + LN_EPS)
        xe = xn[None, :, :] * ln_g[:, None, :] + ln_b[:, None, :]
        h = jax.nn.gelu(jnp.einsum('end,edh->enh', xe, W1) + b1[:, None, :], approximate=False)
        y = jnp.einsum('enh,ehd->end', h, W2) + b2[:, None, :]
        y_tok = jnp.transpose(y, (1, 0, 2))
        sel = jnp.take_along_axis(y_tok, top_idx[:, :, None], axis=1)
        out = (weights[:, :, None] * sel).sum(axis=1)
        return out.reshape(B, S, D)

    def _L1_gnn_ref(node_feats, W1, b1, W2, b2, W_ih, b_ih, W_hh, b_hh, src, dst):
        import jax, jax.numpy as jnp
        import numpy as np
        N_NODES = 50000
        N_EDGES = 25000
        D = 256
        NUM_STEPS = 6
        n_nodes = node_feats.shape[0]
        for _ in range(NUM_STEPS):
            h = jnp.maximum(node_feats @ W1.T + b1, 0.0) @ W2.T + b2
            msg = jax.ops.segment_sum(h[src], dst, num_segments=n_nodes)
            gx = msg @ W_ih.T + b_ih
            gh = node_feats @ W_hh.T + b_hh
            xr, xz, xn = jnp.split(gx, 3, axis=-1)
            hr, hz, hn = jnp.split(gh, 3, axis=-1)
            r = jax.nn.sigmoid(xr + hr)
            z = jax.nn.sigmoid(xz + hz)
            n = jnp.tanh(xn + r * hn)
            node_feats = (1.0 - z) * n + z * node_feats
        return node_feats

    def _L1_ffn_ref(x, W_gat, att_src, att_dst, b_gat, ln_gamma, ln_beta, W1, b1, W2, b2, edge_index):
        import jax, jax.numpy as jnp
        import numpy as np
        B, N, D = (16, 128, 256)
        NUM_EXPERTS, TOP_K, HEADS = (4, 2, 4)
        N_EDGES = 32768
        LN_EPS = 1e-05

        def _layernorm(x, g, b):
            mu = x.mean(-1, keepdims=True)
            var = ((x - mu) ** 2).mean(-1, keepdims=True)
            return (x - mu) * jax.lax.rsqrt(var + LN_EPS) * g + b

        def _forward(x, edge_index, W_gat, att_src, att_dst, b_gat, ln_gamma, ln_beta, W1, b1, W2, b2):
            Bc, Nc, Dc = x.shape
            M = Bc * Nc
            x_flat = x.reshape(M, Dc)
            h = (x_flat @ W_gat).reshape(M, HEADS, NUM_EXPERTS)
            loops = jnp.arange(M, dtype=edge_index.dtype)
            src = jnp.concatenate([edge_index[0], loops])
            dst = jnp.concatenate([edge_index[1], loops])
            a_src = (h * att_src).sum(-1)
            a_dst = (h * att_dst).sum(-1)
            e = jax.nn.leaky_relu(a_src[src] + a_dst[dst], negative_slope=0.2)
            e_max = jax.ops.segment_max(e, dst, num_segments=M)
            ee = jnp.exp(e - e_max[dst])
            denom = jax.ops.segment_sum(ee, dst, num_segments=M)
            alpha = ee / (denom[dst] + 1e-16)
            msg = h[src] * alpha[:, :, None]
            agg = jax.ops.segment_sum(msg, dst, num_segments=M).reshape(M, HEADS * NUM_EXPERTS) + b_gat
            scores = _layernorm(agg, ln_gamma, ln_beta).reshape(M, HEADS, NUM_EXPERTS).mean(1)
            scores = scores.reshape(Bc, Nc, NUM_EXPERTS)
            topk_s, topk_i = jax.lax.top_k(scores, TOP_K)
            w = jax.nn.softmax(topk_s, axis=-1)
            out = jnp.zeros_like(x)
            for ei in range(NUM_EXPERTS):
                g = jnp.where(topk_i == ei, w, 0.0).sum(-1)
                hh = jax.nn.gelu(x @ W1[ei] + b1[ei], approximate=False)
                out = out + g[..., None] * (hh @ W2[ei] + b2[ei])
            return out
        return _forward(x, edge_index, W_gat, att_src, att_dst, b_gat, ln_gamma, ln_beta, W1, b1, W2, b2)
    x = x + _L0_gnn_ref(_layernorm(x, axis=-1), node_type_4, src, dst, edge_type_8, L0_gnn_Wk, L0_gnn_bk, L0_gnn_Wq, L0_gnn_bq, L0_gnn_Wv, L0_gnn_bv, L0_gnn_Wa, L0_gnn_ba, L0_gnn_rel_att, L0_gnn_rel_msg, L0_gnn_rel_pri, L0_gnn_skip)
    x = x + _L0_ffn_ref(_layernorm(x, axis=-1)[None], L0_ffn_Wr, L0_ffn_br, L0_ffn_ln_g, L0_ffn_ln_b, L0_ffn_W1, L0_ffn_b1, L0_ffn_W2, L0_ffn_b2)[0]
    x = x + _L1_gnn_ref(_layernorm(x, axis=-1), L1_gnn_W1, L1_gnn_b1, L1_gnn_W2, L1_gnn_b2, L1_gnn_W_ih, L1_gnn_b_ih, L1_gnn_W_hh, L1_gnn_b_hh, src, dst)
    x = x + _L1_ffn_ref(_layernorm(x, axis=-1)[None], L1_ffn_W_gat, L1_ffn_att_src, L1_ffn_att_dst, L1_ffn_b_gat, L1_ffn_ln_gamma, L1_ffn_ln_beta, L1_ffn_W1, L1_ffn_b1, L1_ffn_W2, L1_ffn_b2, L1_ffn_edge_index)[0]
    return x

_drawn_inputs = setup_inputs


def setup_inputs(seed=0):
    import zlib

    import numpy as np

    out = dict(_drawn_inputs(seed))
    spreads = {'L0_gnn_bk': (0.0, 0.326),
     'L0_gnn_bq': (0.0, 0.325),
     'L0_gnn_bv': (0.0, 0.1),
     'L0_gnn_ba': (0.0, 0.1),
     'L0_gnn_rel_pri': (1.0, 0.57),
     'L0_gnn_skip': (1.0, 0.2),
     'L0_ffn_br': (0.0, 0.1),
     'L0_ffn_ln_g': (1.0, 0.2),
     'L0_ffn_ln_b': (0.0, 0.1),
     'L0_ffn_b1': (0.0, 0.1),
     'L0_ffn_b2': (0.0, 0.1),
     'L1_ffn_b_gat': (0.0, 0.1),
     'L1_ffn_ln_gamma': (1.0, 0.2),
     'L1_ffn_ln_beta': (0.0, 0.1),
     'L1_ffn_b1': (0.0, 0.1),
     'L1_ffn_b2': (0.0, 0.1)}
    factors = {'L1_ffn_att_src': 6.701, 'L1_ffn_att_dst': 70.648}
    for name, (base, spread) in spreads.items():
        noise = np.random.default_rng([zlib.crc32(name.encode()), seed]).standard_normal(out[name].shape)
        drawn = base * np.exp(spread * noise) if base else spread * noise
        out[name] = jnp.asarray(drawn.astype(out[name].dtype))
    for name, factor in factors.items():
        out[name] = (out[name] * factor).astype(out[name].dtype)
    return out
```

```python
from contextlib import ExitStack, contextmanager

import numpy as np

import concourse.bass as bass
import concourse.mybir as mybir

F32 = mybir.dt.float32
BF16 = mybir.dt.bfloat16
I32 = mybir.dt.int32
U16 = mybir.dt.uint16
ALU = mybir.AluOpType
ACT = mybir.ActivationFunctionType
AX = mybir.AxisListType.X

P = 128
EPS = 1e-5
BIG = 1e30
PAD_NODE = 4095
NODE_BITS = 12
NODE_MASK = (1 << NODE_BITS) - 1
PAD_WORD = PAD_NODE << NODE_BITS
SLOTS = 8
HALF = SLOTS // 2


class Program:
    pass


class Graph:
    pass


def cdiv(a, b):
    return -(-a // b)


class Chain:

    def __init__(self, eng, sem, base=0):
        self.eng, self.sem, self.base, self.n = eng, sem, base, 0

    def inc(self, ins):
        ins.then_inc(self.sem, 1)
        self.n += 1

    def wait(self):
        self.eng.wait_ge(self.sem, self.base + self.n)

    def step(self, ins):
        self.inc(ins)
        self.wait()


def peeled(eng, n, body):
    body(0, True, n == 1)
    if n > 2:
        with eng.Fori(1, n - 1, 1) as i:
            body(i, False, False)
    if n > 1:
        body(n - 1, False, True)


def led(eng, n, body):
    body(0, True)
    if n > 1:
        with eng.Fori(1, n, 1) as i:
            body(i, False)


def gate(eng, g, sem, value):
    eng.wait_ge(sem, value)
    eng.sem_inc(g.passed[eng.engine], 1)


def phase(make):
    def run(g, *args):
        if g.shared:
            make(g, *args)
        else:
            with together(g):
                make(g, *args)
    return run


@contextmanager
def together(g):
    used = []

    def sem(name):
        used.append(g.nc.alloc_semaphore(name))
        return used[-1]

    with ExitStack() as scope, g.nc.Block() as block:
        g.shared, g.block, g.scope, outer, g.sem = True, block, scope, g.sem, sem
        yield
    g.shared, g.sem = False, outer
    g.nc.clear_and_free_semaphores(used)
    g.nc.all_engine_barrier()


@phase
def make_constants(g):
    nc = g.nc
    g.ident = g.sb("ident", [P, P])
    g.ones = g.sb("ones", [P, 256])
    g.ones_bf = g.sb("ones_bf", [P, P], BF16)
    g.before_bf = g.sb("before_bf", [P, P], BF16)
    g.from_bf = g.sb("from_bf", [P, P], BF16)
    g.count_f = g.sb("count_f", [P, 256])
    g.count_bf = g.sb("count_bf", [P, 256], BF16)
    count_i = g.sb("count_i", [P, 256], I32)
    blank = g.sem("blank")
    shaped = g.sem("shaped")
    counted = g.sem("counted")
    converted = g.sem("converted")
    block = g.block
    @block.gpsimd
    def _(pool):
        pool.memset(g.ident[:, :], 0.0).then_inc(blank, 1)
        pool.memset(g.ones[:, :], 1.0).then_inc(blank, 1)
        pool.memset(g.ones_bf[:, :], 1.0).then_inc(blank, 1)
        pool.iota(count_i[:, :], pattern=[[1, 256]], base=0, channel_multiplier=0).then_inc(counted, 1)
        pool.wait_ge(blank, 3)
        pool.affine_select(out=g.ident[:, :], in_=g.ident[:, :], compare_op=ALU.not_equal, fill=1.0,
                           base=0, pattern=[[-1, P]], channel_multiplier=1).then_inc(shaped, 1)
        pool.affine_select(out=g.before_bf[:, :], in_=g.ones_bf[:, :], compare_op=ALU.is_gt, fill=0.0,
                           base=0, pattern=[[1, P]], channel_multiplier=-1).then_inc(shaped, 1)
        pool.affine_select(out=g.from_bf[:, :], in_=g.ones_bf[:, :], compare_op=ALU.is_ge, fill=0.0,
                           base=0, pattern=[[-1, P]], channel_multiplier=1).then_inc(shaped, 1)
        pool.wait_ge(counted, 1)
        pool.wait_ge(shaped, 3)

    @block.vector
    def _(dve):
        dve.wait_ge(counted, 1)
        dve.tensor_copy(g.count_f[:, :], count_i[:, :]).then_inc(converted, 1)
        dve.tensor_copy(g.count_bf[:, :], count_i[:, :]).then_inc(converted, 1)
        dve.wait_ge(converted, 2)


@phase
def rank_words(g, tag, words, place_at, words_in, out_dram, chunks, out_chunks, digits, digit_ops, per_tile):
    nc = g.nc
    lanes = 4
    runs = chunks // lanes
    assert chunks % (2 * lanes) == 0 and chunks % SLOTS == 0 and digits <= 256
    ctx = g.scope
    def sb(name, shape, dt=F32):
        return ctx.enter_context(nc.sbuf_tensor(f"{tag}_{name}", shape, dt))

    t0 = place_at
    t1 = sb("t1", [P, chunks], I32)
    digit = sb("digit", [P, chunks], BF16)
    hot = sb("hot", [P, 2, lanes, digits], BF16)
    prod = sb("prod", [P, 2, lanes, digits])
    place = sb("place", [P, chunks])
    total = sb("total", [P, digits])
    incl = sb("incl", [P, digits])
    excl = sb("excl", [P, digits])
    start = sb("start", [P, lanes, digits])
    tiles = (digits - 1) // per_tile if per_tile else 1
    tile_total = sb("tile_total", [P, tiles])
    tile_int = sb("tile_int", [P, tiles], I32)
    tile_room = sb("tile_room", [P, tiles])
    tile_end = sb("tile_end", [P, tiles])
    tile_start = sb("tile_start", [P, tiles])
    fill = sb("fill", [P, out_chunks], I32)
    hist = ctx.enter_context(nc.psum_tensor(f"{tag}_hist", [P, lanes, 512], F32))
    rank = ctx.enter_context(nc.psum_tensor(f"{tag}_rank", [P, lanes, 512], F32))

    loaded = g.sem(f"{tag}_loaded")
    dchain = g.sem(f"{tag}_dchain")
    hot_ready = g.sem(f"{tag}_hot_ready")
    hist_done = g.sem(f"{tag}_hist_done")
    start_ready = g.sem(f"{tag}_start_ready")
    rank_ready = g.sem(f"{tag}_rank_ready")
    prod_ready = g.sem(f"{tag}_prod_ready")
    rank_moved = g.sem(f"{tag}_rank_moved")
    reduced = g.sem(f"{tag}_reduced")
    filled = g.sem(f"{tag}_filled")
    padded = g.sem(f"{tag}_padded")

    by_lane = digit[:, :].rearrange("p (q j) -> p q j", q=lanes)
    place_lane = place[:, :].rearrange("p (q j) -> p q j", q=lanes)
    count = g.count_bf[:, 0:digits].unsqueeze(1).to_broadcast([P, lanes, digits])

    block = g.block
    @block.sync
    def _(sp):
        sp.dma_start(words[:, :], words_in).then_inc(loaded, 16)
        sp.wait_ge(filled, 1)
        sp.dma_start(out_dram.rearrange("(p c) o -> p (c o)", p=P), fill[:, :]).then_inc(padded, 16)
        sp.wait_ge(padded, 16)

    @block.vector
    def _(dve):
        ch = Chain(dve, dchain)
        dve.wait_ge(loaded, 16)
        digit_ops(ch, words, t0, t1)
        ch.step(dve.tensor_copy(digit[:, :], t0[:, :]))

        def one_hot(j, b):
            dve.tensor_tensor(hot[:, b, :, :], by_lane[:, :, bass.ds(j, 1)].to_broadcast([P, lanes, digits]),
                              count, ALU.is_equal).then_inc(hot_ready, 1)

        def hist_body(i, first, last):
            for b in range(2):
                if not first:
                    dve.wait_ge(hist_done, i * 2 + (b - 1))
                one_hot(i * 2 + b, b)

        peeled(dve, runs // 2, hist_body)

        dve.wait_ge(hist_done, runs)
        ch.step(dve.tensor_reduce(total[:, :], hist[:, :, 0:digits].rearrange("p q d -> p d q"), AX, ALU.add))
        ch.step(dve.tensor_tensor_scan(incl[:, :], g.ones[:, 0:digits], total[:, :], 0.0, ALU.mult, ALU.add))
        ch.step(dve.tensor_tensor(excl[:, :], incl[:, :], total[:, :], ALU.subtract))
        if per_tile:
            real = tiles * per_tile
            by_tile = [P, tiles, per_tile]
            ch.step(dve.tensor_reduce(tile_total[:, :], total[:, 0:real].rearrange(
                "p (t d) -> p t d", d=per_tile), AX, ALU.add))
            ch.step(dve.tensor_scalar(tile_int[:, :], tile_total[:, :], float(P - 1), None, ALU.add))
            ch.step(dve.tensor_scalar(tile_int[:, :], tile_int[:, :], 7, 7, ALU.logical_shift_right,
                                      ALU.logical_shift_left))
            ch.step(dve.tensor_copy(tile_room[:, :], tile_int[:, :]))
            ch.step(dve.tensor_tensor_scan(tile_end[:, :], g.ones[:, 0:tiles], tile_room[:, :], 0.0,
                                           ALU.mult, ALU.add))
            ch.step(dve.tensor_tensor(tile_start[:, :], tile_end[:, :], tile_room[:, :], ALU.subtract))
            ex = excl[:, 0:real].rearrange("p (t d) -> p t d", d=per_tile)
            st = start[:, 0, 0:real].rearrange("p (t d) -> p t d", d=per_tile)
            ch.step(dve.tensor_tensor(st, ex, ex[:, :, 0:1].to_broadcast(by_tile), ALU.subtract))
            ch.step(dve.tensor_tensor(st, st, tile_start[:, :].unsqueeze(2).to_broadcast(by_tile), ALU.add))
            ch.step(dve.tensor_copy(start[:, 0, real:digits], tile_end[:, tiles - 1:tiles]))
        else:
            ch.step(dve.tensor_copy(start[:, 0, :], excl[:, :]))
        for q in range(1, lanes):
            ch.step(dve.tensor_tensor(start[:, q, :], start[:, q - 1, :], hist[:, q - 1, 0:digits], ALU.add))
        dve.sem_inc(start_ready, 1)

        def rank_body(i, first, last):
            for b in range(2):
                j = i * 2 + b
                if not (last and b == 1):
                    if not (first and b == 0):
                        dve.wait_ge(rank_moved, j)
                    one_hot(j + 1, 1 - b)
                dve.wait_ge(rank_ready, j + 1)
                dve.tensor_tensor(prod[:, b, :, :], rank[:, :, 0:digits], hot[:, b, :, :],
                                  ALU.mult).then_inc(prod_ready, 1)
                gate(dve, g, prod_ready, j + 1)
                dve.tensor_reduce(place_lane[:, :, bass.ds(j, 1)], prod[:, b, :, :].unsqueeze(2), AX,
                                  ALU.add).then_inc(reduced, 1)

        one_hot(0, 0)
        peeled(dve, runs // 2, rank_body)

        dve.wait_ge(reduced, runs)
        ch.step(dve.tensor_copy(t0[:, :], place[:, :]))
        ch.inc(dve.tensor_scalar(t1[:, :], t0[:, :], P - 1, None, ALU.bitwise_and))
        ch.wait()
        ch.step(dve.tensor_scalar(t0[:, :], t0[:, :], 7, None, ALU.logical_shift_right))
        ch.step(dve.scalar_tensor_tensor(out=t0[:, :], in0=t1[:, :], scalar=float(out_chunks), in1=t0[:, :],
                                         op0=ALU.mult, op1=ALU.add))

    @block.tensor
    def _(pe):
        def hist_body(i, first, last):
            for b in range(2):
                pe.wait_ge(hot_ready, i * 2 + (b + 1))
                for q in range(lanes):
                    mm = pe.matmul(hist[:, q, 0:digits], g.ones_bf[:, :], hot[:, b, q, :],
                                   start=first and b == 0, stop=last and b == 1)
                mm.then_inc(hist_done, 1)

        peeled(pe, runs // 2, hist_body)
        pe.wait_ge(start_ready, 1)
        for q in range(lanes):
            pe.matmul(rank[:, q, 0:digits], g.ones[0:1, 0:P], start[0:1, q, :], start=True, stop=True)

        def rank_body(i, first, last):
            for b in range(2):
                pe.wait_ge(hot_ready, i * 2 + (b + 1 + runs))
                for q in range(lanes):
                    mm = pe.matmul(rank[:, q, 0:digits], g.before_bf[:, :], hot[:, b, q, :],
                                   start=False, stop=True, skip_group_check=True)
                mm.then_inc(rank_ready, 1)
                pe.wait_ge(prod_ready, i * 2 + (b + 1))
                for q in range(lanes):
                    mm = pe.matmul(rank[:, q, 0:digits], g.from_bf[:, :], hot[:, b, q, :],
                                   start=False, stop=True, skip_group_check=True)
                mm.then_inc(rank_moved, 1)

        peeled(pe, runs // 2, rank_body)

    @block.gpsimd
    def _(pool):
        pool.memset(fill[:, :], PAD_WORD).then_inc(filled, 1)


@phase
def scatter_words(g, tag, words, place_at, out_dram, chunks):
    ctx = g.scope
    at = ctx.enter_context(g.nc.sbuf_tensor(f"{tag}_at", [P, SLOTS], I32))
    what = ctx.enter_context(g.nc.sbuf_tensor(f"{tag}_what", [P, SLOTS], I32))
    staged = g.sem(f"{tag}_staged")
    scattered = [g.sem(f"{tag}_scattered{b}") for b in range(SLOTS)]
    block = g.block

    @block.gpsimd
    def _(pool):
        def body(i, first):
            for h in range(2):
                half = slice(h * HALF, (h + 1) * HALF)
                if not first:
                    for b in range(h * HALF, (h + 1) * HALF):
                        pool.wait_ge(scattered[b], i * 16)
                now = bass.ds(i * SLOTS + h * HALF, HALF)
                pool.tensor_copy(at[:, half].bitcast(U16), place_at[:, now].bitcast(U16)).then_inc(staged, 1)
                pool.tensor_copy(what[:, half].bitcast(U16), words[:, now].bitcast(U16)).then_inc(staged, 1)
                gate(pool, g, staged, i * 4 + (h * 2 + 2))
                for b in range(h * HALF, (h + 1) * HALF):
                    pool.indirect_dma_start(
                        out=out_dram, out_offset=bass.IndirectOffsetOnAxis(ap=at[:, b:b + 1], axis=0),
                        in_=what[:, b:b + 1], in_offset=None).then_inc(scattered[b], 16)

        led(pool, chunks // SLOTS, body)
        for b in range(SLOTS):
            pool.wait_ge(scattered[b], 16 * (chunks // SLOTS))


def sort_plan(g, e):
    def bits(ch, out, a, shift, mask):
        ch.step(ch.eng.tensor_scalar(out[:, :], a[:, :], shift, mask, ALU.logical_shift_right, ALU.bitwise_and))

    if e.typed:
        def low_digit(ch, words, t0, t1):
            bits(ch, t0, words, NODE_BITS - 3, 0x78)
            bits(ch, t1, words, 2 * NODE_BITS, 7)
            ch.step(ch.eng.tensor_tensor(t0[:, :], t0[:, :], t1[:, :], ALU.bitwise_or))
        low, shift = 128, 4
    else:
        def low_digit(ch, words, t0, t1):
            bits(ch, t0, words, NODE_BITS, 63)
        low, shift = 64, 6
    high = g.tiles * P >> shift

    def high_digit(ch, words, t0, t1):
        bits(ch, t0, words, NODE_BITS + shift, NODE_MASK >> shift)
        ch.step(ch.eng.tensor_scalar(t0[:, :], t0[:, :], float(high), None, ALU.min))

    return ((low, low_digit, None), (high + 1, high_digit, P >> shift))


def rank_edges(g, e, n):
    digits, digit_ops, per_tile = sort_plan(g, e)[n]
    words_in = e.once.rearrange("(p c) o -> p (c o)", p=P) if n else e.packed[:, :]
    rank_words(g, f"{e.tag}_rank{n}", e.words, e.place, words_in, e.sorted if n else e.once, e.raw_chunks,
               e.room if n else e.raw_chunks, digits, digit_ops, per_tile)


def scatter_edges(g, e, n):
    scatter_words(g, f"{e.tag}_scatter{n}", e.words, e.place, e.sorted if n else e.once, e.raw_chunks)


@phase
def pack_typed(g, e, src, dst, etype):
    nc = g.nc
    edges = src.shape[0]
    rows = edges // e.raw_chunks
    assert rows * e.raw_chunks == edges and rows <= P
    ctx = g.scope
    def sb(name):
        return ctx.enter_context(nc.sbuf_tensor(f"{e.tag}_{name}", [P, e.raw_chunks], I32))

    s, d, t = sb("src"), sb("dst"), sb("typ")
    blank = g.sem(f"{e.tag}_blank")
    loaded = g.sem(f"{e.tag}_in")
    chain = g.sem(f"{e.tag}_pack")
    block = g.block
    @block.sync
    def _(sp):
        sp.wait_ge(blank, 3)
        for to, of in ((s, src), (d, dst), (t, etype)):
            sp.dma_start(to[0:rows, :], of.rearrange("(p c) -> p c", p=rows)).then_inc(loaded, 16)

    @block.vector
    def _(dve):
        dve.memset(s[:, :], 0).then_inc(blank, 1)
        dve.memset(d[:, :], PAD_NODE).then_inc(blank, 1)
        dve.memset(t[:, :], 0).then_inc(blank, 1)
        dve.wait_ge(loaded, 48)
        ch = Chain(dve, chain)
        ch.inc(dve.tensor_scalar(d[:, :], d[:, :], NODE_BITS, None, ALU.logical_shift_left))
        ch.inc(dve.tensor_scalar(t[:, :], t[:, :], 2 * NODE_BITS, None, ALU.logical_shift_left))
        ch.wait()
        ch.step(dve.tensor_tensor(s[:, :], s[:, :], d[:, :], ALU.bitwise_or))
        ch.step(dve.tensor_tensor(e.packed[:, :], s[:, :], t[:, :], ALU.bitwise_or))


@phase
def pack_looped(g, e, edge_index):
    nc = g.nc
    edges = edge_index.shape[1]
    cols = edges // P
    assert cols * P == edges and cols + g.tiles <= e.raw_chunks
    ctx = g.scope
    def sb(name):
        return ctx.enter_context(nc.sbuf_tensor(f"{e.tag}_{name}", [P, e.raw_chunks], I32))

    s, d = sb("src"), sb("dst")
    blank = g.sem(f"{e.tag}_blank")
    loaded = g.sem(f"{e.tag}_in")
    looped = g.sem(f"{e.tag}_looped")
    chain = g.sem(f"{e.tag}_pack")
    block = g.block
    @block.sync
    def _(sp):
        sp.wait_ge(blank, 2)
        for to, k in ((s, 0), (d, 1)):
            sp.dma_start(to[:, 0:cols], edge_index[k, :].rearrange("(p c) -> p c", p=P)).then_inc(loaded, 16)

    @block.gpsimd
    def _(pool):
        pool.wait_ge(blank, 2)
        for x in (s, d):
            pool.iota(x[:, cols:cols + g.tiles], pattern=[[1, g.tiles]], base=0,
                      channel_multiplier=g.tiles).then_inc(looped, 1)

    @block.vector
    def _(dve):
        dve.memset(s[:, :], 0).then_inc(blank, 1)
        dve.memset(d[:, :], PAD_NODE).then_inc(blank, 1)
        dve.wait_ge(loaded, 32)
        dve.wait_ge(looped, 2)
        ch = Chain(dve, chain)
        ch.step(dve.tensor_scalar(d[:, :], d[:, :], NODE_BITS, None, ALU.logical_shift_left))
        ch.step(dve.tensor_tensor(e.packed[:, :], s[:, :], d[:, :], ALU.bitwise_or))


def make_graph(g, tag, edges, raw_chunks, typed):
    nc = g.nc
    e = Graph()
    e.tag, e.typed, e.raw_chunks = tag, typed, raw_chunks
    used = (edges + g.tiles * (P - 1)) // P
    heads_step = 2 * SLOTS if typed else 4 * SLOTS
    e.chunks = cdiv(used, heads_step) * heads_step
    pads = raw_chunks * P - edges
    e.room = max(e.chunks, cdiv(edges + pads + g.tiles * (P - 1), P))
    e.room = cdiv(e.room, 16) * 16
    e.once = nc.dram_tensor(f"{tag}_once", [P * raw_chunks, 1], I32).ap()
    e.sorted = nc.dram_tensor(f"{tag}_sorted", [P * e.room, 1], I32).ap()
    return e


def build(nc, ins, out):
    nodes, dim = ins["x"].shape
    g = Program()
    g.shared = False
    g.nc, g.nodes, g.dim, g.tiles = nc, nodes, dim, cdiv(nodes, P)
    with ExitStack() as ctx:
        g.sb = lambda name, shape, dt=F32: ctx.enter_context(nc.sbuf_tensor(name, shape, dt))
        g.sem = lambda name: ctx.enter_context(nc.semaphore(name))
        g.passed = {nc.vector.engine: g.sem("passed_dve"), nc.gpsimd.engine: g.sem("passed_pool"),
                    nc.scalar.engine: g.sem("passed_act"), nc.tensor.engine: g.sem("passed_pe")}
        make_constants(g)

        hgt = make_graph(g, "hgt", ins["src"].shape[0], 400, True)
        gat = make_graph(g, "gat", ins["L1_ffn_edge_index"].shape[1] + g.tiles * P, 288, False)
        build_rest(g, ins, out, hgt, gat)


def edge_memory(g, e):
    n = e.chunks
    e.src_row = g.sb(f"{e.tag}_src_row", [P, n], I32)
    e.dst_row = g.sb(f"{e.tag}_dst_row", [P, n], I32)
    e.table_row = g.sb(f"{e.tag}_table_row", [P, n], I32) if e.typed else e.src_row
    e.local = g.sb(f"{e.tag}_local", [P, n])
    e.keep_f = g.sb(f"{e.tag}_keep_f", [P, n])
    e.keep_b = g.sb(f"{e.tag}_keep_b", [P, n])
    e.tile = g.sb(f"{e.tag}_tile", [1, n], I32)


@phase
def derive_edges(g, e):
    nc = g.nc
    n = e.chunks
    words = e.sorted.rearrange("(p c) o -> p (c o)", p=P)
    ctx = g.scope
    def sb(name):
        return ctx.enter_context(nc.sbuf_tensor(f"{e.tag}_{name}", [P, n], I32))

    w, before, after, dst, t0 = sb("w"), sb("before"), sb("after"), sb("dsts"), sb("dt0")
    far = ctx.enter_context(nc.sbuf_tensor(f"{e.tag}_far", [P, n], F32))
    blank = g.sem(f"{e.tag}_edge_blank")
    loaded = g.sem(f"{e.tag}_edge_loaded")
    chain = g.sem(f"{e.tag}_derive")
    block = g.block
    @block.sync
    def _(sp):
        sp.dma_start(w[:, :], words[:, 0:n]).then_inc(loaded, 16)
        sp.wait_ge(blank, 2)
        sp.dma_start(before[1:P, :], words[0:P - 1, 0:n]).then_inc(loaded, 16)
        sp.dma_start(before[0:1, 1:n], words[P - 1:P, 0:n - 1]).then_inc(loaded, 16)
        sp.dma_start(after[0:P - 1, :], words[1:P, 0:n]).then_inc(loaded, 16)
        sp.dma_start(after[P - 1:P, 0:n - 1], words[0:1, 1:n]).then_inc(loaded, 16)

    @block.vector
    def _(dve):
        dve.memset(before[:, :], 0x7fff0000).then_inc(blank, 1)
        dve.memset(after[:, :], 0x7fff0000).then_inc(blank, 1)
        dve.wait_ge(loaded, 80)
        ch = Chain(dve, chain)
        ch.inc(dve.tensor_scalar(e.src_row[:, :], w[:, :], NODE_MASK, None, ALU.bitwise_and))
        ch.inc(dve.tensor_scalar(dst[:, :], w[:, :], NODE_BITS, NODE_MASK, ALU.logical_shift_right,
                                 ALU.bitwise_and))
        for x in (w, before, after):
            ch.inc(dve.tensor_scalar(x[:, :], x[:, :], NODE_BITS, None, ALU.logical_shift_right))
        ch.wait()
        ch.inc(dve.tensor_tensor(e.keep_f[:, :], w[:, :], before[:, :], ALU.is_equal))
        ch.inc(dve.tensor_tensor(e.keep_b[:, :], w[:, :], after[:, :], ALU.is_equal))
        if e.typed:
            ch.step(dve.tensor_scalar(t0[:, :], w[:, :], NODE_BITS, None, ALU.logical_shift_right))
            ch.step(dve.scalar_tensor_tensor(out=e.table_row[:, :], in0=t0[:, :], scalar=float(g.tiles * P),
                                             in1=e.src_row[:, :], op0=ALU.mult, op1=ALU.add))
        ch.step(dve.tensor_scalar(e.dst_row[:, :], dst[:, :], float(g.tiles * P - 1), None, ALU.min))
        ch.step(dve.tensor_scalar(far[:, :], dst[:, :], float(g.tiles * P), 1024.0, ALU.is_ge, ALU.mult))
        ch.step(dve.tensor_scalar(t0[:, :], dst[:, :], P - 1, None, ALU.bitwise_and))
        ch.step(dve.tensor_tensor(e.local[:, :], t0[:, :], far[:, :], ALU.add))
        ch.step(dve.tensor_scalar(t0[:, :], dst[:, :], 7, None, ALU.logical_shift_right))
        ch.step(dve.tensor_scalar(e.tile[:, :], t0[0:1, :], float(g.tiles - 1), None, ALU.min))


@phase
def load_nodes(g, x, to):
    nc = g.nc
    whole = g.nodes // P
    blank = g.sem("x_blank")
    loaded = g.sem("x_loaded")
    block = g.block
    @block.vector
    def _(dve):
        dve.memset(to[:, whole:g.tiles, :], 0.0).then_inc(blank, 1)

    @block.sync
    def _(sp):
        sp.dma_start(to[:, 0:whole, :], x[0:whole * P, :].rearrange("(t p) d -> p t d", p=P)).then_inc(loaded, 16)
        sp.wait_ge(blank, 1)
        sp.dma_start(to[0:g.nodes - whole * P, whole, :], x[whole * P:g.nodes, :]).then_inc(loaded, 16)
        sp.wait_ge(loaded, 32)


@phase
def layernorm(g, tag, src, dst):
    nc = g.nc
    tiles = g.tiles
    ctx = g.scope
    def sb(name, shape):
        return ctx.enter_context(nc.sbuf_tensor(f"{tag}_{name}", shape, F32))

    stats = sb("stats", [P, tiles, 6])
    mean, diff, var, std, rstd = (sb(n, [P, tiles, 1]) for n in ("mean", "diff", "var", "std", "rstd"))
    counted = g.sem(f"{tag}_stats")
    chain = g.sem(f"{tag}_chain")
    var_ready = g.sem(f"{tag}_var_ready")
    std_ready = g.sem(f"{tag}_std_ready")
    done = g.sem(f"{tag}_done")
    block = g.block
    @block.vector
    def _(dve):
        with dve.Fori(0, tiles, 1) as t:
            dve.bn_stats(stats[:, bass.ds(t, 1), :], src[:, bass.ds(t, 1), :]).then_inc(counted, 1)
        dve.wait_ge(counted, tiles)
        ch = Chain(dve, chain)
        even, odd = stats[:, :, 1:2], stats[:, :, 4:5]
        ch.inc(dve.tensor_tensor(mean[:, :, :], even, odd, ALU.add))
        ch.inc(dve.tensor_tensor(diff[:, :, :], even, odd, ALU.subtract))
        ch.step(dve.tensor_tensor(var[:, :, :], stats[:, :, 2:3], stats[:, :, 5:6], ALU.add))
        ch.inc(dve.tensor_scalar(mean[:, :, :], mean[:, :, :], 0.5, None, ALU.mult))
        ch.step(dve.scalar_tensor_tensor(out=diff[:, :, :], in0=diff[:, :, :], scalar=0.25,
                                         in1=diff[:, :, :], op0=ALU.mult, op1=ALU.mult))
        ch.step(dve.scalar_tensor_tensor(out=var[:, :, :], in0=var[:, :, :], scalar=1.0 / g.dim,
                                         in1=diff[:, :, :], op0=ALU.mult, op1=ALU.add))
        dve.tensor_scalar(var[:, :, :], var[:, :, :], EPS, None, ALU.add).then_inc(var_ready, 1)
        dve.wait_ge(std_ready, 1)
        ch.step(dve.reciprocal(rstd[:, :, :], std[:, :, :]))
        with dve.Fori(0, tiles, 1) as t:
            dve.tensor_scalar(dst[:, bass.ds(t, 1), :], src[:, bass.ds(t, 1), :],
                              mean[:, bass.ds(t, 1), 0], rstd[:, bass.ds(t, 1), 0],
                              ALU.subtract, ALU.mult).then_inc(done, 1)
        dve.wait_ge(done, tiles)

    @block.scalar
    def _(act):
        act.wait_ge(var_ready, 1)
        act.activation(std[:, :, :], var[:, :, :], ACT.Sqrt).then_inc(std_ready, 1)


@phase
def load_types(g, node_type, type_hot):
    nc = g.nc
    types = type_hot.shape[2]
    whole = g.nodes // P
    ctx = g.scope
    kind = ctx.enter_context(nc.sbuf_tensor("kind", [P, g.tiles], I32))
    blank, loaded, made = g.sem("kind_blank"), g.sem("kind_loaded"), g.sem("kind_made")
    shape = [P, g.tiles, types]
    block = g.block
    @block.sync
    def _(sp):
        sp.wait_ge(blank, 1)
        with nc.allow_non_contiguous_dma("one word per node"):
            sp.dma_start(kind[:, 0:whole], node_type[0:whole * P].rearrange("(t p) -> p t", p=P)).then_inc(
                loaded, 16)
            sp.dma_start(kind[0:g.nodes - whole * P, whole:whole + 1],
                         node_type[whole * P:g.nodes].rearrange("(p o) -> p o", o=1)).then_inc(loaded, 16)

    @block.vector
    def _(dve):
        dve.memset(kind[:, :], 0).then_inc(blank, 1)
        dve.wait_ge(loaded, 32)
        dve.tensor_tensor(type_hot[:, :, :], kind[:, :].unsqueeze(2).to_broadcast(shape),
                          g.count_f[:, 0:types].unsqueeze(1).to_broadcast(shape),
                          ALU.is_equal).then_inc(made, 1)
        dve.wait_ge(made, 1)


@phase
def hgt_project(g, ins, y, type_hot, q, k_table, v_table):
    nc = g.nc
    types, dim, _ = ins["L0_gnn_Wk"].shape
    rels, heads, dk, _ = ins["L0_gnn_rel_att"].shape
    halves = dim // P
    hh = heads // halves
    wide = 3 * dim
    ctx = g.scope
    def sb(name, shape, dt=F32):
        return ctx.enter_context(nc.sbuf_tensor(f"hp_{name}", shape, dt))

    def psum(name, shape):
        return ctx.enter_context(nc.psum_tensor(f"hp_{name}", shape, F32))

    w = sb("w", [P, types, halves, wide])
    bias = sb("bias", [types, wide])
    rel = sb("rel", [P, 2, halves, rels, P])
    pri = sb("pri", [P, rels * heads])
    masked = sb("masked", [P, types, dim])
    hot = sb("hot", [P, types])
    xt = sb("xt", [P, types * halves, P])
    hot_t = sb("hot_t", [types, P])
    kv = sb("kv", [P, 2 * dim])
    kvt = sb("kvt", [P, 2 * halves, P])
    kr = sb("kr", [P, 2, rels, dim])
    p_xt = psum("p_xt", [P, types * halves, P])
    p_qkv = psum("p_qkv", [P, 1024])
    p_hot = p_qkv[0:types, wide:wide + P]
    p_kvt = psum("p_kvt", [P, 2 * halves, P])
    p_rel = psum("p_rel", [P, 2, 512])

    names = ("w_loaded", "rel_blank", "rel_loaded", "rel_ready", "chain", "masked_ready", "xt_done", "xt_copied",
             "qkv_done", "qkv_copied", "kvt_done", "kvt_copied", "rel_done", "rel_even", "rel_odd",
             "kv_stored")
    s = {n: g.sem(f"hp_{n}") for n in names}
    steps = 2 * halves * 2
    half_rels = rels // 2

    def rel_out(i):
        return kr[:, i // (2 * halves), (i % 2) * half_rels:(i % 2 + 1) * half_rels,
                  (i // 2 % halves) * P:(i // 2 % halves + 1) * P]

    block = g.block
    @block.sync
    def _(sp):
        for n, (wt, b) in enumerate(((ins["L0_gnn_Wq"], ins["L0_gnn_bq"]), (ins["L0_gnn_Wk"], ins["L0_gnn_bk"]),
                                     (ins["L0_gnn_Wv"], ins["L0_gnn_bv"]))):
            for t in range(types):
                sp.dma_start(w[:, t, :, n * dim:(n + 1) * dim],
                             wt[t].rearrange("(h p) n -> p h n", p=P)).then_inc(s["w_loaded"], 16)
            sp.dma_start(bias[:, n * dim:(n + 1) * dim], b).then_inc(s["w_loaded"], 16)
        sp.dma_start(pri[:, :], ins["L0_gnn_rel_pri"].rearrange("(o r) h -> o (r h)", o=1).to_broadcast(
            [P, rels * heads])).then_inc(s["w_loaded"], 16)
        sp.wait_ge(s["rel_blank"], 1)
        for n, m in enumerate((ins["L0_gnn_rel_att"], ins["L0_gnn_rel_msg"])):
            for h in range(heads):
                at = h % hh * dk
                sp.dma_start(rel[at:at + dk, n, h // hh, :, at:at + dk],
                             m[:, h].rearrange("r d e -> d r e")).then_inc(s["rel_loaded"], 16)

        def body(t, first):
            sp.wait_ge(s["rel_even"], t * (steps // 2) + steps // 2)
            sp.wait_ge(s["rel_odd"], t * (steps // 2) + steps // 2)
            for n, table in enumerate((k_table, v_table)):
                sp.dma_start(table.rearrange("(r n) d -> n r d", r=rels)[bass.ds(t * P, P), :, :],
                             kr[:, n, :, :]).then_inc(s["kv_stored"], 16)

        led(sp, g.tiles, body)
        sp.wait_ge(s["kv_stored"], 32 * g.tiles)

    @block.vector
    def _(dve):
        dve.memset(rel[:, :, :, :, :], 0.0).then_inc(s["rel_blank"], 1)
        dve.wait_ge(s["w_loaded"], 16 * (3 * (types + 1) + 1))
        dve.wait_ge(s["rel_loaded"], 16 * 2 * heads)
        ch = Chain(dve, s["chain"])
        ch.step(dve.tensor_scalar(pri[:, :], pri[:, :], float(1.0 / np.sqrt(dk)), None, ALU.mult))
        pr = pri[:, :].rearrange("p (r h) -> p r h", h=heads)
        for k in range(halves):
            for h in range(hh):
                block_cols = rel[:, 0, k, :, h * dk:(h + 1) * dk]
                ch.inc(dve.tensor_tensor(block_cols, block_cols,
                                         pr[:, :, k * hh + h:k * hh + h + 1].to_broadcast([P, rels, dk]),
                                         ALU.mult))
        ch.wait()
        dve.sem_inc(s["rel_ready"], 1)

        def body(t, first):
            if not first:
                dve.wait_ge(s["xt_done"], t)
            dve.tensor_tensor(masked[:, :, :], y[:, bass.ds(t, 1), :].to_broadcast([P, types, dim]),
                              type_hot[:, bass.ds(t, 1), :].rearrange("p o k -> p (o k)").unsqueeze(2)
                              .to_broadcast([P, types, dim]), ALU.mult).then_inc(s["masked_ready"], 1)
            dve.tensor_scalar(hot[:, :].unsqueeze(1), type_hot[:, bass.ds(t, 1), :], 1.0, None,
                              ALU.mult).then_inc(s["masked_ready"], 1)
            dve.wait_ge(s["qkv_done"], t + 1)
            if not first:
                dve.wait_ge(s["kvt_done"], t)
            dve.tensor_copy(kv[:, :], p_qkv[:, dim:wide]).then_inc(s["qkv_copied"], 1)
            dve.tensor_scalar(q[:, bass.ds(t, 1), :], p_qkv[:, 0:dim].unsqueeze(1), 1.0, None,
                              ALU.mult).then_inc(s["qkv_copied"], 1)
            if not first:
                dve.wait_ge(s["kv_stored"], t * 32)
            for i in range(0, steps, 2):
                dve.wait_ge(s["rel_done"], t * steps + (i + 1))
                dve.tensor_copy(rel_out(i), p_rel[:, 0, :].rearrange("p (r e) -> p r e", e=P)).then_inc(
                    s["rel_even"], 1)

        led(dve, g.tiles, body)
        dve.wait_ge(s["qkv_copied"], 2 * g.tiles)

    @block.scalar
    def _(act):
        def body(t, first):
            act.wait_ge(s["xt_done"], t + 1)
            if not first:
                act.wait_ge(s["qkv_done"], t)
            act.copy(xt[:, :, :], p_xt[:, :, :]).then_inc(s["xt_copied"], 1)
            act.copy(hot_t[:, :], p_hot).then_inc(s["xt_copied"], 1)
            act.wait_ge(s["kvt_done"], t + 1)
            act.copy(kvt[:, :, :], p_kvt[:, :, :]).then_inc(s["kvt_copied"], 1)
            if not first:
                act.wait_ge(s["kv_stored"], t * 32)
            for i in range(1, steps, 2):
                act.wait_ge(s["rel_done"], t * steps + (i + 1))
                act.copy(rel_out(i), p_rel[:, 1, :].rearrange("p (r e) -> p r e", e=P)).then_inc(s["rel_odd"], 1)

        led(act, g.tiles, body)

    @block.tensor
    def _(pe):
        pe.wait_ge(s["rel_ready"], 1)

        def body(t, first):
            pe.wait_ge(s["masked_ready"], t * 2 + 2)
            if not first:
                pe.wait_ge(s["xt_copied"], t * 2)
                pe.wait_ge(s["qkv_copied"], t * 2)
            for k in range(types):
                for h in range(halves):
                    pe.transpose(p_xt[:, k * halves + h, :], masked[:, k, h * P:(h + 1) * P], g.ident[:, :])
            pe.transpose(p_hot, hot[:, :], g.ident[:, :]).then_inc(s["xt_done"], 1)
            pe.wait_ge(s["xt_copied"], t * 2 + 2)
            for c0, c1 in ((0, 512), (512, wide)):
                pe.matmul(p_qkv[:, c0:c1], hot_t[:, :], bias[:, c0:c1], start=True, stop=False)
                for k in range(types):
                    for h in range(halves):
                        last = k == types - 1 and h == halves - 1
                        mm = pe.matmul(p_qkv[:, c0:c1], xt[:, k * halves + h, :], w[:, k, h, c0:c1],
                                       start=False, stop=last)
            mm.then_inc(s["qkv_done"], 1)
            pe.wait_ge(s["qkv_copied"], t * 2 + 1)
            if not first:
                pe.wait_ge(s["kvt_copied"], t)
            for k in range(2 * halves):
                mm = pe.transpose(p_kvt[:, k, :], kv[:, k * P:(k + 1) * P], g.ident[:, :])
            mm.then_inc(s["kvt_done"], 1)
            pe.wait_ge(s["kvt_copied"], t + 1)
            for i in range(steps):
                m, h, r = i // (2 * halves), i // 2 % halves, i % 2
                seen = s["rel_odd"] if i % 2 else s["rel_even"]
                if not (first and i < 2):
                    pe.wait_ge(seen, t * (steps // 2) + i // 2)
                pe.matmul(p_rel[:, i % 2, :], kvt[:, m * halves + h, :],
                          rel[:, m, h, r * half_rels:(r + 1) * half_rels, :],
                          start=True, stop=True).then_inc(s["rel_done"], 1)

        led(pe, g.tiles, body)


def gather_rows(pool, g, chunks, sources, staged, used, stage_base=0, used_base=0):
    k = len(sources)

    def body(i, first):
        for h in range(2):
            if not first:
                gate(pool, g, used, i * SLOTS + (used_base + (h + 1) * HALF - SLOTS))
            for rows, stage, _, _, _ in sources:
                pool.tensor_copy(stage[:, h * HALF:(h + 1) * HALF].bitcast(U16),
                                 rows[:, bass.ds(i * SLOTS + h * HALF, HALF)].bitcast(U16)).then_inc(staged, 1)
            gate(pool, g, staged, i * (2 * k) + (stage_base + (h + 1) * k))
            for b in range(h * HALF, (h + 1) * HALF):
                for _, stage, table, slots, gathered in sources:
                    pool.indirect_dma_start(
                        out=slots[:, b, :], out_offset=None, in_=table,
                        in_offset=bass.IndirectOffsetOnAxis(ap=stage[:, b:b + 1], axis=0)).then_inc(gathered[b], 16)

    return body


def dst_rows(g, tag, e, values, width):
    deep = 4
    ctx = g.scope
    hot = ctx.enter_context(g.nc.sbuf_tensor(f"{tag}_hot", [P, deep, P], F32))
    hot_t = ctx.enter_context(g.nc.sbuf_tensor(f"{tag}_hot_t", [P, deep, P], F32))
    p_hot = ctx.enter_context(g.nc.psum_tensor(f"{tag}_p_hot", [P, 2, 512], F32))
    p_rows = ctx.enter_context(g.nc.psum_tensor(f"{tag}_p_rows", [P, 2, 512], F32))
    hot_made, turned, copied, found = (g.sem(f"{tag}_{k}") for k in ("hot_made", "turned", "copied", "found"))

    def make_hot(dve, c, k, first):
        if not (first and k < deep):
            dve.wait_ge(turned, c + (1 - deep))
        dve.tensor_scalar(hot[:, k % deep, :], g.count_f[:, 0:P], e.local[:, bass.ds(c, 1)], None,
                          ALU.is_equal).then_inc(hot_made, 1)

    def turn(pe, c, k, first):
        pe.wait_ge(hot_made, c + 1)
        if not (first and k < 2):
            pe.wait_ge(copied, c - 1)
        pe.transpose(p_hot[:, k % 2, 0:P], hot[:, k % deep, :], g.ident[:, :]).then_inc(turned, 1)

    def copy(act, c, k, first):
        act.wait_ge(turned, c + 1)
        if not (first and k < deep):
            act.wait_ge(found, c + (1 - deep))
        act.copy(hot_t[:, k % deep, :], p_hot[:, k % 2, 0:P]).then_inc(copied, 1)

    def find(pe, c, k, first, read):
        tile = pe.value_load(e.tile[0:1, bass.ds(c, 1)], min_val=0, max_val=g.tiles - 1)
        pe.wait_ge(copied, c + 1)
        if not (first and k < 2):
            pe.wait_ge(read, c - 1)
        pe.matmul(p_rows[:, k % 2:k % 2 + 1, 0:width], hot_t[:, k % deep, :], values[:, bass.ds(tile, 1), :],
                  start=True, stop=True).then_inc(found, 1)

    return make_hot, turn, copy, find, found, p_rows


def ahead(step, eng, c, b, lead, first, last):
    for n in (range(lead + 1) if first and b == 0 else (lead,)):
        if not (last and b + n >= SLOTS):
            step(eng, c + n, b + n, first)


@phase
def hgt_scores(g, e, q, k_table, att):
    nc = g.nc
    heads = att.shape[2]
    dk = g.dim // heads
    ctx = g.scope
    keys = ctx.enter_context(nc.sbuf_tensor("hs_keys", [P, SLOTS, g.dim], F32))
    key_rows = ctx.enter_context(nc.sbuf_tensor("hs_key_rows", [P, SLOTS], I32))
    prod = ctx.enter_context(nc.sbuf_tensor("hs_prod", [P, 2, g.dim], F32))
    staged, used, scored = g.sem("hs_staged"), g.sem("hs_used"), g.sem("hs_scored")
    got = [g.sem(f"hs_got{b}") for b in range(SLOTS)]
    make_hot, turn, copy, find, found, p_rows = dst_rows(g, "hq", e, q, g.dim)
    loops = e.chunks // SLOTS
    block = g.block

    @block.gpsimd
    def _(pool):
        led(pool, loops, gather_rows(pool, g, e.chunks, [(e.table_row, key_rows, k_table, keys, got)], staged, used))

    @block.vector
    def _(dve):
        def body(i, first, last):
            for b in range(SLOTS):
                c = i * SLOTS + b
                ahead(make_hot, dve, c, b, 3, first, last)
                dve.wait_ge(got[b], i * 16 + 16)
                dve.wait_ge(found, c + 1)
                if not (first and b < 2):
                    dve.wait_ge(scored, c - 1)
                dve.tensor_tensor(prod[:, b % 2, :], keys[:, b, :], p_rows[:, b % 2, 0:g.dim],
                                  ALU.mult).then_inc(used, 1)
                if not (first and b == 0):
                    total(c - 1, (b - 1) % 2)

        def total(c, b):
            gate(dve, g, used, c + 1)
            dve.tensor_reduce(att[:, bass.ds(c, 1), :].rearrange("p o h -> p (o h)"),
                              prod[:, b, :].rearrange("p (h d) -> p h d", d=dk), AX,
                              ALU.add).then_inc(scored, 1)

        peeled(dve, loops, body)
        total(e.chunks - 1, 1)
        dve.wait_ge(scored, e.chunks)

    @block.scalar
    def _(act):
        def body(i, first):
            for b in range(SLOTS):
                copy(act, i * SLOTS + b, b, first)

        led(act, loops, body)

    @block.tensor
    def _(pe):
        def body(i, first, last):
            for b in range(SLOTS):
                c = i * SLOTS + b
                ahead(turn, pe, c, b, 2, first, last)
                find(pe, c, b, first, used)

        peeled(pe, loops, body)


@phase
def segment_softmax(g, e, att, tiny):
    nc = g.nc
    heads = att.shape[2]
    pieces = P // heads
    groups = e.chunks // pieces
    length = groups * P
    tag = f"{e.tag}_sm"
    ctx = g.scope
    def sb(name, shape):
        return ctx.enter_context(nc.sbuf_tensor(f"{tag}_{name}", shape, F32))

    turned = sb("turned", [P, 3, groups, P])
    value, keep_f, keep_b = (turned[:, n, :, :].rearrange("p g e -> p (g e)") for n in range(3))
    scan = sb("scan", [P, length])
    temp = sb("temp", [P, length])
    stage = sb("stage", [P, 3, P])
    stage_back = sb("stage_back", [P, P])
    least_f, least_b = sb("least_f", [P, 1]), sb("least_b", [P, 1])
    rows = sb("rows", [1, 2 * P])
    row_scan = sb("row_scan", [1, P])
    row_init = sb("row_init", [1, P])
    init = sb("init", [P, 1])
    p_turn = ctx.enter_context(nc.psum_tensor(f"{tag}_p_turn", [P, 3, P], F32))
    p_rows = ctx.enter_context(nc.psum_tensor(f"{tag}_p_rows", [P, 512], F32))
    p_init = ctx.enter_context(nc.psum_tensor(f"{tag}_p_init", [P, 512], F32))
    p_back = ctx.enter_context(nc.psum_tensor(f"{tag}_p_back", [P, 512], F32))
    names = ("staged", "turn_done", "turn_copied", "chain", "cols_ready", "rows_done", "init_ready", "init_done",
             "shifted", "exp_done", "weighed", "back_staged", "back_done", "back_copied")
    s = {n: g.sem(f"{tag}_{n}") for n in names}
    by_head = att[:, :, :].rearrange("p (c g) h -> p h c g", g=groups)
    rounds = 4

    def piece_of(keep, i):
        return keep[:, :].rearrange("p (c g) -> p c g", g=groups)[:, :, bass.ds(i, 1)].unsqueeze(1).to_broadcast(
            [P, heads, pieces, 1])

    block = g.block
    @block.vector
    def _(dve):
        def turn_body(i, first):
            if not first:
                dve.wait_ge(s["turn_done"], i)
            for n, of in enumerate((by_head[:, :, :, bass.ds(i, 1)], piece_of(e.keep_f, i),
                                    piece_of(e.keep_b, i))):
                dve.tensor_scalar(stage[:, n, :].rearrange("p (h c o) -> p h c o", h=heads, o=1), of, 1.0,
                                  None, ALU.mult).then_inc(s["staged"], 1)

        led(dve, groups, turn_body)
        dve.wait_ge(s["turn_copied"], groups)
        ch = Chain(dve, s["chain"])
        ch.inc(dve.tensor_reduce(least_f[:, :], keep_f, AX, ALU.min))
        ch.step(dve.tensor_reduce(least_b[:, :], keep_b, AX, ALU.min))
        turn = [0]

        def scan_pieces(data0, data1, op0, op1, least, neutral, back):
            turn[0] += 1
            r = turn[0]
            way = slice(None, None, -1) if back else slice(None)

            def run(initial):
                ch.step(dve.tensor_tensor_scan(scan[:, way], data0[:, way], data1[:, way], initial, op0, op1))

            run(neutral)
            dve.sem_inc(s["cols_ready"], 1)
            dve.wait_ge(s["rows_done"], r)
            ch.step(dve.tensor_copy(rows[:, :], p_rows[0:1, 0:2 * P]))
            goes_on = rows[:, P:2 * P]
            if neutral:
                ch.step(dve.tensor_scalar(goes_on, goes_on, -1.0, BIG, ALU.add, ALU.mult))
            edge = pieces - 1 if back else 0
            ch.step(dve.memset(goes_on.rearrange("o (h c) -> o h c", h=heads)[:, :, edge:edge + 1], neutral))
            ch.inc(dve.tensor_tensor_scan(row_scan[:, way], goes_on[:, way], rows[:, 0:P][:, way], neutral,
                                          op0, op1))
            ch.inc(dve.memset(row_init[:, :], neutral))
            ch.wait()
            to = row_init[:, :].rearrange("o (h c) -> o h c", h=heads)
            of = row_scan[:, :].rearrange("o (h c) -> o h c", h=heads)
            a, b = (slice(0, pieces - 1), slice(1, pieces)) if back else (slice(1, pieces),
                                                                        slice(0, pieces - 1))
            dve.tensor_copy(to[:, :, a], of[:, :, b]).then_inc(s["init_ready"], 1)
            dve.wait_ge(s["init_done"], r)
            ch.step(dve.tensor_copy(init[:, :], p_init[:, 0:1]))
            run(init[:, 0:1])

        def spread_back():
            ch.step(dve.tensor_tensor(temp[:, :], scan[:, :], keep_b, ALU.mult))
            ch.step(dve.tensor_tensor(temp[:, :], scan[:, :], temp[:, :], ALU.subtract))
            scan_pieces(keep_b, temp[:, :], ALU.mult, ALU.add, least_b, 0.0, True)

        ch.step(dve.tensor_scalar(temp[:, :], keep_f, -1.0, BIG, ALU.add, ALU.mult))
        scan_pieces(temp[:, :], value, ALU.add, ALU.max, least_f, -BIG, False)
        spread_back()
        dve.tensor_tensor(value, value, scan[:, :], ALU.subtract).then_inc(s["shifted"], 1)
        dve.wait_ge(s["exp_done"], 1)
        scan_pieces(keep_f, value, ALU.mult, ALU.add, least_f, 0.0, False)
        spread_back()
        if tiny:
            ch.step(dve.tensor_scalar(scan[:, :], scan[:, :], tiny, None, ALU.add))
        ch.step(dve.reciprocal(scan[:, :], scan[:, :]))
        dve.tensor_tensor(value, value, scan[:, :], ALU.mult).then_inc(s["weighed"], 1)
        dve.wait_ge(s["weighed"], 1)

        def back_body(i, first):
            if not first:
                dve.wait_ge(s["back_done"], i)
            dve.tensor_scalar(stage_back[:, :].unsqueeze(1), turned[:, 0, bass.ds(i, 1), :], 1.0, None,
                              ALU.mult).then_inc(s["back_staged"], 1)

        led(dve, groups, back_body)

    @block.scalar
    def _(act):
        def turn_body(i, first):
            gate(act, g, s["turn_done"], i + 1)
            act.copy(turned[:, :, bass.ds(i, 1), :], p_turn[:, :, :].unsqueeze(2)).then_inc(s["turn_copied"], 1)

        led(act, groups, turn_body)
        act.wait_ge(s["turn_copied"], groups)
        act.wait_ge(s["shifted"], 1)
        act.activation(value, value, ACT.Exp).then_inc(s["exp_done"], 1)

        def back_body(i, first):
            gate(act, g, s["back_done"], i + 1)
            act.copy(by_head[:, :, :, bass.ds(i, 1)],
                     p_back[:, 0:P].rearrange("p (h c o) -> p h c o", h=heads, o=1)).then_inc(s["back_copied"], 1)

        led(act, groups, back_body)
        act.wait_ge(s["back_copied"], groups)

    @block.tensor
    def _(pe):
        def turn_body(i, first):
            pe.wait_ge(s["staged"], i * 3 + 3)
            if not first:
                pe.wait_ge(s["turn_copied"], i)
            for n in range(3):
                mm = pe.transpose(p_turn[:, n, :], stage[:, n, :], g.ident[:, :])
            mm.then_inc(s["turn_done"], 1)

        led(pe, groups, turn_body)
        for r in range(1, rounds + 1):
            back = r % 2 == 0
            end = 0 if back else length - 1
            pe.wait_ge(s["cols_ready"], r)
            pe.transpose(p_rows[0:1, 0:P], scan[:, end:end + 1], g.ident[:, :])
            pe.transpose(p_rows[0:1, P:2 * P], (least_b if back else least_f)[:, :],
                         g.ident[:, :]).then_inc(s["rows_done"], 1)
            pe.wait_ge(s["init_ready"], r)
            pe.matmul(p_init[:, 0:1], row_init[:, :], g.ones[0:1, 0:1], start=True,
                      stop=True).then_inc(s["init_done"], 1)

        def back_body(i, first):
            pe.wait_ge(s["back_staged"], i + 1)
            if not first:
                pe.wait_ge(s["back_copied"], i)
            pe.transpose(p_back[:, 0:P], stage_back[:, :], g.ident[:, :]).then_inc(s["back_done"], 1)

        led(pe, groups, back_body)


@phase
def hgt_sum(g, e, v_table, att, sums):
    nc = g.nc
    heads = att.shape[2]
    dk = g.dim // heads
    wide = g.dim + 1
    ctx = g.scope
    def sb(name, shape, dt=F32):
        return ctx.enter_context(nc.sbuf_tensor(f"ha_{name}", shape, dt))

    values = sb("values", [P, SLOTS, g.dim])
    value_rows = sb("value_rows", [P, SLOTS], I32)
    begins = sb("begins", [P, e.chunks])
    hot = sb("hot", [P, 2, P])
    weighted = sb("weighted", [P, 2, wide])
    p_sum = ctx.enter_context(nc.psum_tensor("ha_p_sum", [P, 2, 512], F32))
    staged, used, hot_made, counted = g.sem("ha_staged"), g.sem("ha_used"), g.sem("ha_hot"), g.sem("ha_counted")
    summed, added, begun = g.sem("ha_summed"), g.sem("ha_added"), g.sem("ha_begun")
    got = [g.sem(f"ha_got{b}") for b in range(SLOTS)]
    n = e.chunks
    block = g.block
    @block.gpsimd
    def _(pool):
        led(pool, n // SLOTS, gather_rows(pool, g, n, [(e.table_row, value_rows, v_table, values, got)],
                                          staged, used))

    @block.vector
    def _(dve):
        dve.tensor_scalar(begins[:, :], e.keep_f[:, :], -1.0, 1.0, ALU.mult, ALU.add).then_inc(begun, 1)
        dve.memset(sums[:, :, :], 0.0).then_inc(begun, 1)
        dve.wait_ge(begun, 2)

        def add(c, b, first):
            tile = dve.value_load(e.tile[0:1, bass.ds(c, 1)], min_val=0, max_val=g.tiles - 1)
            dve.wait_ge(summed, c + 1)
            if not first:
                dve.wait_ge(added, c)
            to = sums[:, bass.ds(tile, 1), :]
            dve.tensor_tensor(to, to, p_sum[:, b:b + 1, 0:wide], ALU.add).then_inc(added, 1)

        def body(i, first):
            for b in range(SLOTS):
                c = i * SLOTS + b
                if not (first and b < 2):
                    dve.wait_ge(summed, c - 1)
                dve.tensor_scalar(hot[:, b % 2, :], g.count_f[:, 0:P], e.local[:, bass.ds(c, 1)], None,
                                  ALU.is_equal).then_inc(hot_made, 1)
                dve.tensor_scalar(weighted[:, b % 2, g.dim:wide], begins[:, bass.ds(c, 1)], 1.0, None,
                                  ALU.mult).then_inc(counted, 1)
                dve.wait_ge(got[b], i * 16 + 16)
                dve.tensor_tensor(weighted[:, b % 2, 0:g.dim].rearrange("p (h d) -> p h d", d=dk),
                                  values[:, b, :].rearrange("p (h d) -> p h d", d=dk),
                                  att[:, bass.ds(c, 1), :].rearrange("p o h -> p (o h)").unsqueeze(2)
                                  .to_broadcast([P, heads, dk]), ALU.mult).then_inc(used, 1)
                if not (first and b == 0):
                    add(c - 1, (b - 1) % 2, first and b == 1)

        led(dve, n // SLOTS, body)
        add(n - 1, 1, False)
        dve.wait_ge(added, n)

    @block.tensor
    def _(pe):
        def body(i, first):
            for b in range(SLOTS):
                c = i * SLOTS + b
                for ready in (hot_made, counted, used):
                    pe.wait_ge(ready, c + 1)
                if not (first and b < 2):
                    pe.wait_ge(added, c - 1)
                pe.matmul(p_sum[:, b % 2, 0:wide], hot[:, b % 2, :], weighted[:, b % 2, :],
                          start=True, stop=True).then_inc(summed, 1)

        led(pe, n // SLOTS, body)


@phase
def hgt_update(g, ins, sums, y, type_hot, nodes_x):
    nc = g.nc
    types, dim, _ = ins["L0_gnn_Wa"].shape
    halves = dim // P
    ctx = g.scope
    def sb(name, shape, dt=F32):
        return ctx.enter_context(nc.sbuf_tensor(f"hu_{name}", shape, dt))

    w = sb("w", [P, types, halves, dim])
    bias = sb("bias", [types, dim])
    skip = sb("skip", [P, types])
    mix_all = sb("mix_all", [P, g.tiles, types])
    mix = sb("mix", [P, g.tiles])
    share = sb("share", [P, g.tiles, 1])
    share_hot = sb("share_hot", [P, g.tiles, types])
    masked = sb("masked", [P, types, dim])
    hot = sb("hot", [P, types])
    xt = sb("xt", [P, types * halves, P])
    hot_t = sb("hot_t", [types, P])
    change = sb("change", [P, 1, dim])
    p_xt = ctx.enter_context(nc.psum_tensor("hu_p_xt", [P, types * halves, P], F32))
    p_hot = ctx.enter_context(nc.psum_tensor("hu_p_hot", [types, 512], F32))
    p_out = ctx.enter_context(nc.psum_tensor("hu_p_out", [P, 1, 512], F32))
    names = ("loaded", "sigmoid", "chain", "masked_ready", "xt_done", "xt_copied", "out_done", "out_read", "tail")
    s = {n: g.sem(f"hu_{n}") for n in names}
    shape = [P, g.tiles, types]
    block = g.block
    @block.sync
    def _(sp):
        for t in range(types):
            sp.dma_start(w[:, t, :, :], ins["L0_gnn_Wa"][t].rearrange("(h p) n -> p h n", p=P)).then_inc(
                s["loaded"], 16)
        sp.dma_start(bias[:, :], ins["L0_gnn_ba"]).then_inc(s["loaded"], 16)
        sp.dma_start(skip[:, :], ins["L0_gnn_skip"].rearrange("(o t) -> o t", o=1).to_broadcast(
            [P, types])).then_inc(s["loaded"], 16)

    @block.scalar
    def _(act):
        act.wait_ge(s["loaded"], 16 * (types + 2))
        act.activation(skip[:, :], skip[:, :], ACT.Sigmoid).then_inc(s["sigmoid"], 1)

        def body(t, first):
            act.wait_ge(s["xt_done"], t + 1)
            if not first:
                act.wait_ge(s["out_done"], t)
            act.copy(xt[:, :, :], p_xt[:, :, :]).then_inc(s["xt_copied"], 1)
            act.copy(hot_t[:, :], p_hot[:, 0:P]).then_inc(s["xt_copied"], 1)

        led(act, g.tiles, body)

    @block.vector
    def _(dve):
        ch = Chain(dve, s["chain"])
        ch.step(dve.tensor_scalar(share[:, :, :], sums[:, :, dim:dim + 1], 1.0, None, ALU.max))
        ch.step(dve.reciprocal(share[:, :, :], share[:, :, :]))
        ch.step(dve.tensor_tensor(share_hot[:, :, :], type_hot[:, :, :], share[:, :, :].to_broadcast(shape),
                                  ALU.mult))
        dve.wait_ge(s["sigmoid"], 1)
        ch.step(dve.tensor_tensor(mix_all[:, :, :], type_hot[:, :, :],
                                  skip[:, :].unsqueeze(1).to_broadcast(shape), ALU.mult))
        ch.step(dve.tensor_reduce(mix[:, :], mix_all[:, :, :], AX, ALU.add))

        def body(t, first):
            if not first:
                dve.wait_ge(s["xt_done"], t)
            dve.tensor_tensor(masked[:, :, :], sums[:, bass.ds(t, 1), 0:dim].to_broadcast([P, types, dim]),
                              share_hot[:, bass.ds(t, 1), :].rearrange("p o k -> p (o k)").unsqueeze(2)
                              .to_broadcast([P, types, dim]), ALU.mult).then_inc(s["masked_ready"], 1)
            dve.tensor_scalar(hot[:, :].unsqueeze(1), type_hot[:, bass.ds(t, 1), :], 1.0, None,
                              ALU.mult).then_inc(s["masked_ready"], 1)
            dve.wait_ge(s["out_done"], t + 1)
            row, x_row = y[:, bass.ds(t, 1), :], nodes_x[:, bass.ds(t, 1), :]
            dve.tensor_tensor(change[:, :, :], p_out[:, :, 0:dim], row, ALU.subtract).then_inc(s["out_read"], 1)
            dve.wait_ge(s["out_read"], t + 1)
            dve.scalar_tensor_tensor(out=x_row, in0=change[:, :, :], scalar=mix[:, bass.ds(t, 1)], in1=x_row,
                                     op0=ALU.mult, op1=ALU.add).then_inc(s["tail"], 1)
            dve.wait_ge(s["tail"], t * 2 + 1)
            dve.tensor_tensor(x_row, x_row, row, ALU.add).then_inc(s["tail"], 1)

        led(dve, g.tiles, body)
        dve.wait_ge(s["tail"], 2 * g.tiles)

    @block.tensor
    def _(pe):
        pe.wait_ge(s["loaded"], 16 * (types + 2))

        def body(t, first):
            pe.wait_ge(s["masked_ready"], t * 2 + 2)
            if not first:
                pe.wait_ge(s["xt_copied"], t * 2)
            for k in range(types):
                for h in range(halves):
                    pe.transpose(p_xt[:, k * halves + h, :], masked[:, k, h * P:(h + 1) * P], g.ident[:, :])
            pe.transpose(p_hot[:, 0:P], hot[:, :], g.ident[:, :]).then_inc(s["xt_done"], 1)
            pe.wait_ge(s["xt_copied"], t * 2 + 2)
            if not first:
                pe.wait_ge(s["out_read"], t)
            pe.matmul(p_out[:, 0, 0:dim], hot_t[:, :], bias[:, :], start=True, stop=False)
            for k in range(types):
                for h in range(halves):
                    mm = pe.matmul(p_out[:, 0, 0:dim], xt[:, k * halves + h, :], w[:, k, h, :],
                                   start=False, stop=k == types - 1 and h == halves - 1)
            mm.then_inc(s["out_done"], 1)

        led(pe, g.tiles, body)


@phase
def turn_nodes(g, tag, src, turned, weight, bias, product):
    nc = g.nc
    halves = g.dim // P
    n = weight.shape[1] if weight is not None else 0
    ctx = g.scope
    def sb(name, shape):
        return ctx.enter_context(nc.sbuf_tensor(f"{tag}_{name}", shape, F32))

    stage = sb("stage", [P, g.dim])
    now = sb("now", [P, halves, P])
    p_now = ctx.enter_context(nc.psum_tensor(f"{tag}_p_now", [P, halves, P], F32))
    names = ("loaded", "staged", "turn_done", "kept", "now_ready", "product_done", "product_read")
    s = {k: g.sem(f"{tag}_{k}") for k in names}
    if n:
        w = sb("w", [P, halves, n])
        b_row = sb("b_row", [1, n])
        p_prod = ctx.enter_context(nc.psum_tensor(f"{tag}_p_prod", [P, 1, 512], F32))
    block = g.block
    @block.sync
    def _(sp):
        if n:
            sp.dma_start(w[:, :, :], weight.rearrange("(h p) n -> p h n", p=P)).then_inc(s["loaded"], 16)
            if bias is not None:
                sp.dma_start(b_row[:, :], bias.rearrange("(o n) -> o n", o=1)).then_inc(s["loaded"], 16)

    @block.vector
    def _(dve):
        if n and bias is None:
            dve.memset(b_row[:, :], 0.0).then_inc(s["loaded"], 16)

        def body(t, first):
            if not first:
                dve.wait_ge(s["turn_done"], t)
            dve.tensor_scalar(stage[:, :].unsqueeze(1), src[:, bass.ds(t, 1), :], 1.0, None,
                              ALU.mult).then_inc(s["staged"], 1)
            if turned is not None:
                dve.wait_ge(s["turn_done"], t + 1)
                dve.tensor_scalar(turned[:, :, bass.ds(t * P, P)], p_now[:, :, :], 1.0, None,
                                  ALU.mult).then_inc(s["kept"], 1)
            if n:
                dve.wait_ge(s["product_done"], t + 1)
                dve.tensor_scalar(product[:, bass.ds(t, 1), :], p_prod[:, :, 0:n], 1.0, None,
                                  ALU.mult).then_inc(s["product_read"], 1)

        led(dve, g.tiles, body)
        if turned is not None:
            dve.wait_ge(s["kept"], g.tiles)
        if n:
            dve.wait_ge(s["product_read"], g.tiles)

    @block.scalar
    def _(act):
        if n:
            def body(t, first):
                act.wait_ge(s["turn_done"], t + 1)
                if not first:
                    act.wait_ge(s["product_done"], t)
                if turned is not None:
                    act.wait_ge(s["kept"], t + 1)
                act.copy(now[:, :, :], p_now[:, :, :]).then_inc(s["now_ready"], 1)

            led(act, g.tiles, body)

    @block.tensor
    def _(pe):
        if n:
            pe.wait_ge(s["loaded"], 32)

        def body(t, first):
            pe.wait_ge(s["staged"], t + 1)
            if not first:
                if n:
                    pe.wait_ge(s["now_ready"], t)
                if turned is not None:
                    pe.wait_ge(s["kept"], t)
            for h in range(halves):
                mm = pe.transpose(p_now[:, h, :], stage[:, h * P:(h + 1) * P], g.ident[:, :])
            mm.then_inc(s["turn_done"], 1)
            if n:
                pe.wait_ge(s["now_ready"], t + 1)
                if not first:
                    pe.wait_ge(s["product_read"], t)
                pe.matmul(p_prod[:, 0, 0:n], g.ones[0:1, 0:P], b_row[:, :], start=True, stop=False)
                for h in range(halves):
                    mm = pe.matmul(p_prod[:, 0, 0:n], now[:, h, :], w[:, h, :], start=False,
                                   stop=h == halves - 1)
                mm.then_inc(s["product_done"], 1)

        led(pe, g.tiles, body)


@phase
def top2_gates(g, tag, scores, gates):
    nc = g.nc
    n = scores.shape[2]
    shape = [P, g.tiles, n]
    ctx = g.scope
    def sb(name, width=n):
        return ctx.enter_context(nc.sbuf_tensor(f"{tag}_{name}", [P, g.tiles, width], F32))

    rest, is_top, pick = sb("rest"), sb("is_top"), [sb("pick0"), sb("pick1")]
    top, which = [sb("top0", 1), sb("top1", 1)], sb("which", 1)
    gap, ratio, first_w, second_w = sb("gap", 1), sb("ratio", 1), sb("first_w", 1), sb("second_w", 1)
    chain, gap_ready, ratio_ready = g.sem(f"{tag}_chain"), g.sem(f"{tag}_gap"), g.sem(f"{tag}_ratio")
    block = g.block
    @block.vector
    def _(dve):
        ch = Chain(dve, chain)
        count = g.count_f[:, 0:n].unsqueeze(1).to_broadcast(shape)
        of = scores
        for k in range(2):
            ch.step(dve.tensor_reduce(top[k][:, :, 0], of[:, :, :], AX, ALU.max))
            ch.step(dve.tensor_tensor(is_top[:, :, :], of[:, :, :], top[k][:, :, :].to_broadcast(shape),
                                      ALU.is_equal))
            ch.step(dve.scalar_tensor_tensor(out=is_top[:, :, :], in0=is_top[:, :, :], scalar=-2.0 * n,
                                             in1=count, op0=ALU.mult, op1=ALU.add))
            ch.step(dve.tensor_reduce(which[:, :, 0], is_top[:, :, :], AX, ALU.min))
            ch.step(dve.tensor_tensor(pick[k][:, :, :], is_top[:, :, :], which[:, :, :].to_broadcast(shape),
                                      ALU.is_equal))
            if k == 0:
                ch.step(dve.scalar_tensor_tensor(out=rest[:, :, :], in0=pick[0][:, :, :], scalar=-BIG,
                                                 in1=scores[:, :, :], op0=ALU.mult, op1=ALU.add))
                of = rest
        dve.tensor_tensor(gap[:, :, :], top[1][:, :, :], top[0][:, :, :], ALU.subtract).then_inc(gap_ready, 1)
        dve.wait_ge(ratio_ready, 1)
        ch.step(dve.tensor_scalar(first_w[:, :, :], ratio[:, :, :], 1.0, None, ALU.add))
        ch.step(dve.reciprocal(first_w[:, :, :], first_w[:, :, :]))
        ch.step(dve.tensor_tensor(second_w[:, :, :], ratio[:, :, :], first_w[:, :, :], ALU.mult))
        for k, wk in enumerate((first_w, second_w)):
            ch.step(dve.tensor_tensor(pick[k][:, :, :], pick[k][:, :, :], wk[:, :, :].to_broadcast(shape),
                                      ALU.mult))
        ch.step(dve.tensor_tensor(gates[:, :, :], pick[0][:, :, :], pick[1][:, :, :], ALU.add))

    @block.scalar
    def _(act):
        act.wait_ge(gap_ready, 1)
        act.activation(ratio[:, :, :], gap[:, :, :], ACT.Exp).then_inc(ratio_ready, 1)


@phase
def experts(g, tag, turned, gates, nodes_x, w1, b1, w2, b2, ln_g, ln_b):
    nc = g.nc
    count, dim, hidden = w1.shape
    halves, parts = dim // P, hidden // P
    span = 5
    groups = g.tiles // span
    wide = span * P
    cut = wide // 2
    assert groups * span == g.tiles and count % 2 == 0
    ctx = g.scope
    def sb(name, shape):
        return ctx.enter_context(nc.sbuf_tensor(f"{tag}_{name}", shape, F32))

    w1_sb, w2_sb = sb("w1", [P, 2, halves, hidden]), sb("w2", [P, 2, parts, dim])
    b1_sb, b2_sb = sb("b1", [P, 2, parts]), sb("b2", [1, 2, dim])
    norm = sb("norm", [P, 2, count * halves])
    xe = sb("xe", [P, halves, wide])
    hid = sb("hid", [P, parts, wide])
    p_hid = ctx.enter_context(nc.psum_tensor(f"{tag}_p_hid", [P, 2, 2, 512], F32))
    p_out = ctx.enter_context(nc.psum_tensor(f"{tag}_p_out", [P, 2, 512], F32))
    names = ("norm_loaded", "xe_ready", "hid_done", "hid_ready", "out_done", "added")
    s = {k: g.sem(f"{tag}_{k}") for k in names}
    loaded = [g.sem(f"{tag}_loaded{k}") for k in range(2)]
    gate_flat = gates[:, :, :].rearrange("p t e -> p (t e)")

    def each_group(eng, body):
        def pair(i, first):
            for b in range(2):
                def group(gr, lead):
                    body(i * (2 * groups) + (gr + b * groups), gr, b, i, first and b == 0 and lead)
                led(eng, groups, group)
        led(eng, count // 2, pair)

    block = g.block
    @block.sync
    def _(sp):
        if ln_g is not None:
            with nc.allow_non_contiguous_dma("a number per partition"):
                for k, v in enumerate((ln_g, ln_b)):
                    sp.dma_start(norm[:, k, :], v.rearrange("e (h p) -> p (e h)", p=P)).then_inc(
                        s["norm_loaded"], 16)

        def pair(i, first):
            for b in range(2):
                x = i * 2 + b
                if not first:
                    sp.wait_ge(s["added"], x * g.tiles - g.tiles)
                one = bass.ds(x, 1)
                sp.dma_start(w1_sb[:, b, :, :], w1[one].rearrange("o (h p) n -> p (o h) n", p=P)).then_inc(
                    loaded[b], 16)
                sp.dma_start(w2_sb[:, b, :, :], w2[one].rearrange("o (m p) n -> p (o m) n", p=P)).then_inc(
                    loaded[b], 16)
                with nc.allow_non_contiguous_dma("a number per partition"):
                    sp.dma_start(b1_sb[:, b, :], b1[one].rearrange("o (m p) -> p (o m)", p=P)).then_inc(
                        loaded[b], 16)
                sp.dma_start(b2_sb[:, b, :], b2[one]).then_inc(loaded[b], 16)
        led(sp, count // 2, pair)

    @block.vector
    def _(dve):
        if ln_g is not None:
            dve.wait_ge(s["norm_loaded"], 32)

        def body(n, gr, b, i, first):
            if ln_g is not None:
                if not first:
                    dve.wait_ge(s["hid_done"], n * parts)
                for h in range(halves):
                    at = bass.ds((i * 2 + b) * halves + h, 1)
                    dve.tensor_scalar(xe[:, h, :], turned[:, h, bass.ds(gr * wide, wide)], norm[:, 0, at],
                                      norm[:, 1, at], ALU.mult, ALU.add).then_inc(s["xe_ready"], 1)
            for j in range(span):
                t = gr * span + j
                dve.wait_ge(s["out_done"], n * span + (j + 1))
                if not (first and j == 0):
                    dve.wait_ge(s["added"], n * span + j)
                x_row = nodes_x[:, bass.ds(t, 1), :]
                dve.scalar_tensor_tensor(out=x_row, in0=p_out[:, j % 2:j % 2 + 1, 0:dim],
                                         scalar=gate_flat[:, bass.ds(t * count + (i * 2 + b), 1)],
                                         in1=x_row, op0=ALU.mult, op1=ALU.add).then_inc(s["added"], 1)

        each_group(dve, body)
        dve.wait_ge(s["added"], count * g.tiles)

    @block.scalar
    def _(act):
        def body(n, gr, b, i, first):
            for m in range(parts):
                act.wait_ge(s["hid_done"], n * parts + (m + 1))
                if m == 0 and not first:
                    act.wait_ge(s["out_done"], n * span)
                act.activation(hid[:, m, :].rearrange("p (k c) -> p k c", k=2), p_hid[:, m % 2, :, 0:cut],
                               ACT.Gelu, bias=b1_sb[:, b, m:m + 1]).then_inc(s["hid_ready"], 1)

        each_group(act, body)

    @block.tensor
    def _(pe):
        def body(n, gr, b, i, first):
            pe.wait_ge(loaded[b], i * 64 + 64)
            if ln_g is not None:
                pe.wait_ge(s["xe_ready"], n * halves + halves)
            for m in range(parts):
                if not (first and m < 2):
                    pe.wait_ge(s["hid_ready"], n * parts + (m - 1))
                for k in range(2):
                    for h in range(halves):
                        if ln_g is not None:
                            x = xe[:, h, k * cut:(k + 1) * cut]
                        else:
                            x = turned[:, h, bass.ds(gr * wide + k * cut, cut)]
                        mm = pe.matmul(p_hid[:, m % 2, k, 0:cut], w1_sb[:, b, h, m * P:(m + 1) * P], x,
                                       start=h == 0, stop=h == halves - 1)
                mm.then_inc(s["hid_done"], 1)
            for j in range(span):
                if j == 0:
                    pe.wait_ge(s["hid_ready"], n * parts + parts)
                if not (first and j < 2):
                    pe.wait_ge(s["added"], n * span + max(j - 1, 0))
                out = p_out[:, j % 2, 0:dim]
                pe.matmul(out, g.ones[0:1, 0:P], b2_sb[:, b, :], start=True, stop=False)
                for m in range(parts):
                    mm = pe.matmul(out, hid[:, m, j * P:(j + 1) * P], w2_sb[:, b, m, :], start=False,
                                   stop=m == parts - 1)
                mm.then_inc(s["out_done"], 1)

        each_group(pe, body)


@phase
def gated_graph(g, ins, e, state, steps, h_table):
    nc = g.nc
    dim, halves, tiles = g.dim, g.dim // P, g.tiles
    span = 5
    groups = tiles // span
    wide = span * P
    cut = wide // 2
    ends = 2 * groups
    loops = e.chunks // SLOTS
    mats = ((ins["L1_gnn_W1"], 1), (ins["L1_gnn_W2"], 1), (ins["L1_gnn_W_ih"], 3), (ins["L1_gnn_W_hh"], 3))
    blocks = sum(m for _, m in mats) * halves
    W1, W2, WI, WH = 0, dim, 2 * dim, 5 * dim
    ctx = g.scope
    def sb(name, shape, dt=F32):
        return ctx.enter_context(nc.sbuf_tensor(f"gg_{name}", shape, dt))

    def psum(name, shape):
        return ctx.enter_context(nc.psum_tensor(f"gg_{name}", shape, F32))

    plain = sb("plain", [P, blocks, dim])
    w = sb("w", [P, halves, blocks * P])
    b1 = sb("b1", [P, halves])
    b2 = sb("b2", [1, dim])
    b_in, b_state = sb("b_in", [P, 3 * halves]), sb("b_state", [P, 3 * halves])
    b_both = sb("b_both", [P, 3 * halves])
    message = sb("message", [P, halves, tiles * P])
    rows = sb("rows", [P, SLOTS, dim])
    row_ids = sb("row_ids", [P, SLOTS], I32)
    hot = sb("hot", [P, SLOTS, P])
    mid = sb("mid", [P, halves, wide])
    h_out = sb("h_out", [P, span, dim])
    gate_r, gate_z = sb("gate_r", [P, halves, cut]), sb("gate_z", [P, halves, cut])
    fresh, move = sb("fresh", [P, halves, cut]), sb("move", [P, halves, cut])
    p_big = psum("p_big", [P, 4, 512])
    p_h = psum("p_h", [P, 2, 512])
    p_msg = psum("p_msg", [P, 2, 512])

    names = ("loaded", "turned", "turn_read", "summed_bias", "mid_done", "mid_ready", "h_done", "h_ready",
             "h_stored", "staged", "used", "hot_made", "summed", "added", "cleared", "gru_done", "gates_made",
             "reset_made", "fresh_made", "chain", "updated", "new_made")
    s = {k: g.sem(f"gg_{k}") for k in names}
    got = [g.sem(f"gg_got{b}") for b in range(SLOTS)]
    per_round = 4

    block = g.block
    @block.sync
    def _(sp):
        at = 0
        for m, parts in mats:
            sp.dma_start(plain[:, at:at + parts * halves, :], m.rearrange("(o p) i -> p o i", p=P)).then_inc(
                s["loaded"], 16)
            at += parts * halves
        with nc.allow_non_contiguous_dma("a number per partition"):
            for to, of in ((b1, ins["L1_gnn_b1"]), (b_in, ins["L1_gnn_b_ih"]), (b_state, ins["L1_gnn_b_hh"])):
                sp.dma_start(to[:, :], of.rearrange("(o p) -> p o", p=P)).then_inc(s["loaded"], 16)
        sp.dma_start(b2[:, :], ins["L1_gnn_b2"].rearrange("(o n) -> o n", o=1)).then_inc(s["loaded"], 16)

        with sp.Fori(0, steps, 1) as step:
            with sp.Fori(0, groups, 1) as gr:
                sp.wait_ge(s["h_ready"], step * tiles + gr * span + span)
                sp.dma_start(h_table.rearrange("(n p) d -> p n d", p=P)[:, bass.ds(gr * span, span), :],
                             h_out[:, :, :]).then_inc(s["h_stored"], 16)
        sp.wait_ge(s["h_stored"], steps * groups * 16)

    @block.gpsimd
    def _(pool):
        with pool.Fori(0, steps, 1) as step:
            gate(pool, g, s["h_stored"], step * (groups * 16) + groups * 16)
            led(pool, loops, gather_rows(pool, g, e.chunks, [(e.src_row, row_ids, h_table, rows, got)],
                                         s["staged"], s["used"], step * (2 * loops), step * e.chunks))

    @block.tensor
    def _(pe):
        pe.wait_ge(s["loaded"], 16 * 8)
        for r in range(blocks // per_round):
            for h in range(halves):
                if r or h:
                    pe.wait_ge(s["turn_read"], r * halves + h)
                for k in range(per_round):
                    mm = pe.transpose(p_big[:, 0, k * P:(k + 1) * P],
                                      plain[:, r * per_round + k, h * P:(h + 1) * P], g.ident[:, :])
                mm.then_inc(s["turned"], 1)
        pe.wait_ge(s["turn_read"], blocks // per_round * halves)

        def mid_out(m):
            return p_big[:, 2 * m:2 * m + 2, 0:cut]

        def nodes_to_h(gr, first, step):
            n = step * groups + gr
            for m in range(halves):
                if not first:
                    pe.wait_ge(s["mid_ready"], (n - 1) * halves + (m + 1))
                for k in range(2):
                    for h in range(halves):
                        mm = pe.matmul(p_big[:, 2 * m + k, 0:cut], w[:, h, W1 + m * P:W1 + (m + 1) * P],
                                       state[:, h, bass.ds(gr * wide + k * cut, cut)], start=h == 0,
                                       stop=h == halves - 1)
                mm.then_inc(s["mid_done"], 1)
            pe.wait_ge(s["mid_ready"], n * halves + halves)
            for j in range(span):
                if not (first and j < 2):
                    pe.wait_ge(s["h_ready"], n * span + max(j - 1, 0))
                pe.matmul(p_h[:, j % 2, 0:dim], g.ones[0:1, 0:P], b2[:, :], start=True, stop=False)
                for h in range(halves):
                    mm = pe.matmul(p_h[:, j % 2, 0:dim], mid[:, h, j * P:(j + 1) * P],
                                   w[:, h, W2:W2 + dim], start=False, stop=h == halves - 1)
                mm.then_inc(s["h_done"], 1)

        def sum_edges(i, first, step):
            for b in range(SLOTS):
                c = step * e.chunks + i * SLOTS + b
                if b % HALF == 0:
                    pe.wait_ge(s["hot_made"], step * (2 * loops) + i * 2 + (b // HALF + 1))
                pe.wait_ge(got[b], step * (loops * 16) + i * 16 + 16)
                if not (first and b < 2):
                    pe.wait_ge(s["added"], c - 1)
                for h in range(halves):
                    mm = pe.matmul(p_msg[:, b % 2, h * P:(h + 1) * P], rows[:, b, h * P:(h + 1) * P],
                                   hot[:, b, :], start=True, stop=True)
                mm.then_inc(s["used"], 1)

        def gru(n, first, step):
            q = step * ends + n
            now = bass.ds(n * cut, cut)
            for k in range(halves):
                if not (first and k == 0):
                    pe.wait_ge(s["gates_made"], (q * halves + k) * 2)
                    pe.wait_ge(s["reset_made"], (q * halves + k) * 2)
                for bank, col, both in ((0, 0, True), (1, dim, True)):
                    for h in range(halves):
                        pe.matmul(p_big[:, bank, 0:cut], w[:, h, WI + col + k * P:WI + col + (k + 1) * P],
                                  message[:, h, now], start=h == 0, stop=False)
                    for h in range(halves):
                        pe.matmul(p_big[:, bank, 0:cut], w[:, h, WH + col + k * P:WH + col + (k + 1) * P],
                                  state[:, h, now], start=False, stop=h == halves - 1)
                col = 2 * dim + k * P
                for bank, of, first_col in ((2, message, WI), (3, state, WH)):
                    for h in range(halves):
                        mm = pe.matmul(p_big[:, bank, 0:cut], w[:, h, first_col + col:first_col + col + P],
                                       of[:, h, now], start=h == 0, stop=h == halves - 1)
                mm.then_inc(s["gru_done"], 1)

        with pe.Fori(0, steps, 1) as step:
            pe.wait_ge(s["updated"], step * (ends * halves) + 1)
            led(pe, groups, lambda gr, first: nodes_to_h(gr, first, step))
            led(pe, loops, lambda i, first: sum_edges(i, first, step))
            pe.wait_ge(s["added"], step * e.chunks + e.chunks)
            led(pe, ends, lambda n, first: gru(n, first, step))

    @block.scalar
    def _(act):
        for r in range(blocks // per_round):
            for h in range(halves):
                act.wait_ge(s["turned"], r * halves + h + 1)
                act.copy(w[:, h, r * per_round * P:(r + 1) * per_round * P], p_big[:, 0, :]).then_inc(
                    s["turn_read"], 1)
        act.wait_ge(s["summed_bias"], 1)

        def nodes_to_h(gr, first, step):
            n = step * groups + gr
            for m in range(halves):
                act.wait_ge(s["mid_done"], n * halves + (m + 1))
                if not first and m == 0:
                    act.wait_ge(s["h_done"], n * span)
                act.activation(mid[:, m, :].rearrange("p (k c) -> p k c", k=2),
                               p_big[:, 2 * m:2 * m + 2, 0:cut], ACT.Relu, bias=b1[:, m:m + 1]).then_inc(
                    s["mid_ready"], 1)

        def gru(n, first, step):
            q = step * ends + n
            for k in range(halves):
                act.wait_ge(s["gru_done"], q * halves + (k + 1))
                if not first and k == 0:
                    act.wait_ge(s["updated"], step * (ends * halves) + (n * halves + 1))
                act.activation(gate_r[:, k, :], p_big[:, 0, 0:cut], ACT.Sigmoid,
                               bias=b_both[:, k:k + 1]).then_inc(s["gates_made"], 1)
                act.activation(gate_z[:, k, :], p_big[:, 1, 0:cut], ACT.Sigmoid,
                               bias=b_both[:, halves + k:halves + k + 1]).then_inc(s["gates_made"], 1)
                act.wait_ge(s["reset_made"], (q * halves + k) * 2 + 2)
                act.activation(fresh[:, k, :], move[:, k, :], ACT.Tanh,
                               bias=b_in[:, 2 * halves + k:2 * halves + k + 1]).then_inc(s["fresh_made"], 1)

        with act.Fori(0, steps, 1) as step:
            led(act, groups, lambda gr, first: nodes_to_h(gr, first, step))
            led(act, ends, lambda n, first: gru(n, first, step))

    @block.vector
    def _(dve):
        dve.wait_ge(s["loaded"], 16 * 8)
        dve.tensor_tensor(b_both[:, :], b_in[:, :], b_state[:, :], ALU.add).then_inc(s["summed_bias"], 1)
        dve.sem_inc(s["updated"], 1)

        def nodes_to_h(gr, first, step):
            n = step * groups + gr
            if not first:
                dve.wait_ge(s["h_stored"], n * 16)
            for j in range(span):
                dve.wait_ge(s["h_done"], n * span + (j + 1))
                dve.tensor_copy(h_out[:, j, :], p_h[:, j % 2, 0:dim]).then_inc(s["h_ready"], 1)

        def add(i_c, tile, b, first, step):
            c = step * e.chunks + i_c
            dve.wait_ge(s["used"], c + 1)
            if not first:
                dve.wait_ge(s["added"], c)
            to = message[:, :, bass.ds(tile * P, P)]
            dve.tensor_tensor(to, to, p_msg[:, b, 0:halves * P].rearrange("p (h n) -> p h n", h=halves),
                              ALU.add).then_inc(s["added"], 1)

        def add_batch(i_c, first, step):
            _, at = nc.values_load_multi_w_load_instructions(
                e.tile[0:1, bass.ds(i_c, HALF)], engines=[mybir.EngineType.DVE], min_val=0, max_val=tiles - 1)
            for b in range(HALF):
                add(i_c + b, at[b], b % 2, first and b == 0, step)

        def sum_edges(i, first, step):
            for h in range(2):
                i_c = i * SLOTS + h * HALF
                if not first:
                    dve.wait_ge(s["used"], step * e.chunks + (i_c - HALF))
                dve.tensor_tensor(hot[:, h * HALF:(h + 1) * HALF, :],
                                  g.count_f[:, 0:P].unsqueeze(1).to_broadcast([P, HALF, P]),
                                  e.local[:, bass.ds(i_c, HALF)].unsqueeze(2).to_broadcast([P, HALF, P]),
                                  ALU.is_equal).then_inc(s["hot_made"], 1)
                if not (first and h == 0):
                    add_batch(i_c - HALF, first and h == 1, step)

        def gru(n, first, step):
            q = step * ends + n
            now = bass.ds(n * cut, cut)
            per = 4
            for k in range(halves):
                dve.wait_ge(s["gates_made"], (q * halves + k) * 2 + 2)
                dve.scalar_tensor_tensor(out=move[:, k, :], in0=p_big[:, 3, 0:cut],
                                         scalar=b_state[:, 2 * halves + k:2 * halves + k + 1],
                                         in1=gate_r[:, k, :], op0=ALU.add, op1=ALU.mult).then_inc(
                    s["reset_made"], 1)
                dve.wait_ge(s["reset_made"], (q * halves + k) * 2 + 1)
                dve.tensor_tensor(move[:, k, :], move[:, k, :], p_big[:, 2, 0:cut], ALU.add).then_inc(
                    s["reset_made"], 1)
            dve.wait_ge(s["fresh_made"], q * halves + halves)
            old = state[:, :, now]
            dve.tensor_tensor(move[:, :, :], old, fresh[:, :, :], ALU.subtract).then_inc(s["chain"], 1)
            dve.wait_ge(s["chain"], q * 2 + 1)
            dve.tensor_tensor(move[:, :, :], move[:, :, :], gate_z[:, :, :], ALU.mult).then_inc(s["chain"], 1)
            dve.wait_ge(s["chain"], q * 2 + 2)
            dve.tensor_tensor(old, fresh[:, :, :], move[:, :, :], ALU.add).then_inc(s["updated"], halves)

        with dve.Fori(0, steps, 1) as step:
            led(dve, groups, lambda gr, first: nodes_to_h(gr, first, step))
            dve.wait_ge(s["h_done"], step * tiles + tiles)
            dve.memset(message[:, :, :], 0.0).then_inc(s["cleared"], 1)
            dve.wait_ge(s["cleared"], step + 1)
            led(dve, loops, lambda i, first: sum_edges(i, first, step))
            add_batch(e.chunks - HALF, False, step)
            dve.wait_ge(s["added"], step * e.chunks + e.chunks)
            led(dve, ends, lambda n, first: gru(n, first, step))
        dve.wait_ge(s["updated"], steps * ends * halves + 1)


@phase
def add_turned(g, tag, turned, nodes_x):
    nc = g.nc
    halves = g.dim // P
    ctx = g.scope
    stage = ctx.enter_context(nc.sbuf_tensor(f"{tag}_stage", [P, halves, P], F32))
    p_back = ctx.enter_context(nc.psum_tensor(f"{tag}_p_back", [P, 1, 512], F32))
    staged, turn_done, added = g.sem(f"{tag}_staged"), g.sem(f"{tag}_turn_done"), g.sem(f"{tag}_added")
    block = g.block
    @block.vector
    def _(dve):
        def body(t, first):
            if not first:
                dve.wait_ge(turn_done, t)
            dve.tensor_scalar(stage[:, :, :], turned[:, :, bass.ds(t * P, P)], 1.0, None,
                              ALU.mult).then_inc(staged, 1)
            dve.wait_ge(turn_done, t + 1)
            row = nodes_x[:, bass.ds(t, 1), :]
            dve.tensor_tensor(row, row, p_back[:, :, 0:g.dim], ALU.add).then_inc(added, 1)

        led(dve, g.tiles, body)
        dve.wait_ge(added, g.tiles)

    @block.tensor
    def _(pe):
        def body(t, first):
            pe.wait_ge(staged, t + 1)
            if not first:
                pe.wait_ge(added, t)
            for h in range(halves):
                mm = pe.transpose(p_back[:, 0, h * P:(h + 1) * P], stage[:, h, :], g.ident[:, :])
            mm.then_inc(turn_done, 1)

        led(pe, g.tiles, body)


@phase
def gat_tables(g, ins, feats, src_table, dst_table):
    nc = g.nc
    heads, per = ins["L1_ffn_att_src"].shape
    n = heads * per
    ctx = g.scope
    def sb(name, shape):
        return ctx.enter_context(nc.sbuf_tensor(f"gt_{name}", shape, F32))

    a = sb("a", [P, 2, n])
    prod = sb("prod", [P, g.tiles, n])
    from_row = sb("from_row", [P, g.tiles, n + heads])
    to_row = sb("to_row", [P, g.tiles, heads])
    loaded, chain, stored = g.sem("gt_loaded"), g.sem("gt_chain"), g.sem("gt_stored")
    ready = g.sem("gt_ready")
    block = g.block
    @block.sync
    def _(sp):
        for k, v in enumerate((ins["L1_ffn_att_src"], ins["L1_ffn_att_dst"])):
            sp.dma_start(a[:, k, :], v.rearrange("(o h) x -> o (h x)", o=1).to_broadcast([P, n])).then_inc(
                loaded, 16)
        sp.wait_ge(ready, 1)
        sp.dma_start(src_table.rearrange("(t p) d -> p t d", p=P), from_row[:, :, :]).then_inc(stored, 16)
        sp.dma_start(dst_table.rearrange("(t p) d -> p t d", p=P), to_row[:, :, :]).then_inc(stored, 16)
        sp.wait_ge(stored, 32)

    @block.vector
    def _(dve):
        ch = Chain(dve, chain)
        dve.wait_ge(loaded, 32)
        ch.step(dve.tensor_copy(from_row[:, :, 0:n], feats[:, :, :]))
        for k, to in enumerate((from_row[:, :, n:n + heads], to_row[:, :, :])):
            ch.step(dve.tensor_tensor(prod[:, :, :], feats[:, :, :],
                                      a[:, k, :].unsqueeze(1).to_broadcast([P, g.tiles, n]), ALU.mult))
            ch.step(dve.tensor_reduce(to, prod[:, :, :].rearrange("p t (h x) -> p t h x", h=heads), AX,
                                      ALU.add))
        dve.sem_inc(ready, 1)


@phase
def gat_scores(g, e, src_table, dst_table, edge_feats, att):
    nc = g.nc
    heads = att.shape[2]
    n = edge_feats.shape[2]
    ctx = g.scope
    def sb(name, shape, dt=F32):
        return ctx.enter_context(nc.sbuf_tensor(f"gs_{name}", shape, dt))

    from_rows, to_rows = sb("from_rows", [P, SLOTS, n + heads]), sb("to_rows", [P, SLOTS, heads])
    from_ids, to_ids = sb("from_ids", [P, SLOTS], I32), sb("to_ids", [P, SLOTS], I32)
    both = sb("both", [P, 2, HALF, heads])
    staged, used, summed, scored = g.sem("gs_staged"), g.sem("gs_used"), g.sem("gs_summed"), g.sem("gs_scored")
    got_from = [g.sem(f"gs_from{b}") for b in range(SLOTS)]
    got_to = [g.sem(f"gs_to{b}") for b in range(SLOTS)]
    block = g.block
    @block.gpsimd
    def _(pool):
        led(pool, e.chunks // SLOTS,
            gather_rows(pool, g, e.chunks, [(e.src_row, from_ids, src_table, from_rows, got_from),
                                            (e.dst_row, to_ids, dst_table, to_rows, got_to)], staged, used))

    @block.vector
    def _(dve):
        def body(i, first):
            for h in range(2):
                at = bass.ds(i * SLOTS + h * HALF, HALF)
                slots = slice(h * HALF, (h + 1) * HALF)
                for b in range(h * HALF, (h + 1) * HALF):
                    dve.wait_ge(got_from[b], i * 16 + 16)
                    dve.wait_ge(got_to[b], i * 16 + 16)
                dve.tensor_scalar(edge_feats[:, at, :], from_rows[:, slots, 0:n], 1.0, None,
                                  ALU.mult).then_inc(used, HALF // 2)
                if not first:
                    dve.wait_ge(scored, i * 2 + (h - 1))
                dve.tensor_tensor(both[:, h, :, :], from_rows[:, slots, n:n + heads], to_rows[:, slots, :],
                                  ALU.add).then_inc(used, HALF // 2)
                dve.wait_ge(used, i * SLOTS + (h + 1) * HALF)
                dve.scalar_tensor_tensor(out=att[:, at, :], in0=both[:, h, :, :], scalar=0.2,
                                         in1=both[:, h, :, :], op0=ALU.mult, op1=ALU.max).then_inc(scored, 1)

        led(dve, e.chunks // SLOTS, body)
        dve.wait_ge(scored, 2 * (e.chunks // SLOTS))


@phase
def gat_sum(g, e, edge_feats, att, sums):
    nc = g.nc
    heads = att.shape[2]
    n = edge_feats.shape[2]
    ctx = g.scope
    hot = ctx.enter_context(nc.sbuf_tensor("gu_hot", [P, 2, P], F32))
    p_sum = ctx.enter_context(nc.psum_tensor("gu_p_sum", [P, 2, 512], F32))
    weighed, hot_made, summed, added = g.sem("gu_weighed"), g.sem("gu_hot_made"), g.sem("gu_summed"), g.sem("gu_added")
    block = g.block
    @block.vector
    def _(dve):
        by_head = edge_feats[:, :, :].rearrange("p c (h x) -> p (c h) x", h=heads)
        dve.tensor_tensor(by_head, by_head, att[:, :, :].rearrange("p c h -> p (c h)").unsqueeze(2)
                          .to_broadcast([P, e.chunks * heads, n // heads]), ALU.mult).then_inc(weighed, 1)
        dve.memset(sums[:, :, :], 0.0).then_inc(weighed, 1)
        dve.wait_ge(weighed, 2)

        def add(c, b, first):
            tile = dve.value_load(e.tile[0:1, bass.ds(c, 1)], min_val=0, max_val=g.tiles - 1)
            dve.wait_ge(summed, c + 1)
            if not first:
                dve.wait_ge(added, c)
            to = sums[:, bass.ds(tile, 1), :]
            dve.tensor_tensor(to, to, p_sum[:, b:b + 1, 0:n], ALU.add).then_inc(added, 1)

        def body(i, first):
            for b in range(SLOTS):
                c = i * SLOTS + b
                if not (first and b < 2):
                    dve.wait_ge(summed, c - 1)
                dve.tensor_scalar(hot[:, b % 2, :], g.count_f[:, 0:P], e.local[:, bass.ds(c, 1)], None,
                                  ALU.is_equal).then_inc(hot_made, 1)
                if not (first and b == 0):
                    add(c - 1, (b - 1) % 2, first and b == 1)

        led(dve, e.chunks // SLOTS, body)
        add(e.chunks - 1, 1, False)
        dve.wait_ge(added, e.chunks)

    @block.tensor
    def _(pe):
        pe.wait_ge(weighed, 2)

        def body(i, first):
            for b in range(SLOTS):
                c = i * SLOTS + b
                pe.wait_ge(hot_made, c + 1)
                if not (first and b < 2):
                    pe.wait_ge(added, c - 1)
                pe.matmul(p_sum[:, b % 2:b % 2 + 1, 0:n], hot[:, b % 2, :], edge_feats[:, bass.ds(c, 1), :],
                          start=True, stop=True).then_inc(summed, 1)

        led(pe, e.chunks // SLOTS, body)


@phase
def gat_router(g, ins, sums, scores):
    nc = g.nc
    heads, per = ins["L1_ffn_att_src"].shape
    n = heads * per
    shape = [P, g.tiles, n]
    ctx = g.scope
    def sb(name, s):
        return ctx.enter_context(nc.sbuf_tensor(f"gr_{name}", s, F32))

    par = sb("par", [P, 3, n])
    square = sb("square", shape)
    mean, var, std = sb("mean", [P, g.tiles, 1]), sb("var", [P, g.tiles, 1]), sb("std", [P, g.tiles, 1])
    loaded, chain, var_ready, std_ready = (g.sem(f"gr_{k}") for k in ("loaded", "chain", "var", "std_ready"))
    block = g.block
    @block.sync
    def _(sp):
        for k, v in enumerate((ins["L1_ffn_b_gat"], ins["L1_ffn_ln_gamma"], ins["L1_ffn_ln_beta"])):
            sp.dma_start(par[:, k, :], v.rearrange("(o n) -> o n", o=1).to_broadcast([P, n])).then_inc(
                loaded, 16)

    @block.vector
    def _(dve):
        ch = Chain(dve, chain)

        def par_all(k):
            return par[:, k, :].unsqueeze(1).to_broadcast(shape)

        x = sums[:, :, :]
        dve.wait_ge(loaded, 48)
        ch.step(dve.tensor_tensor(x, x, par_all(0), ALU.add))
        ch.step(dve.tensor_reduce(mean[:, :, 0], x, AX, ALU.add))
        ch.step(dve.tensor_scalar(mean[:, :, :], mean[:, :, :], 1.0 / n, None, ALU.mult))
        ch.step(dve.tensor_tensor(x, x, mean[:, :, :].to_broadcast(shape), ALU.subtract))
        ch.step(dve.tensor_tensor(square[:, :, :], x, x, ALU.mult))
        ch.step(dve.tensor_reduce(var[:, :, 0], square[:, :, :], AX, ALU.add))
        dve.tensor_scalar(var[:, :, :], var[:, :, :], 1.0 / n, EPS, ALU.mult, ALU.add).then_inc(var_ready, 1)
        dve.wait_ge(std_ready, 1)
        ch.step(dve.reciprocal(std[:, :, :], std[:, :, :]))
        ch.step(dve.tensor_tensor(x, x, std[:, :, :].to_broadcast(shape), ALU.mult))
        ch.step(dve.tensor_tensor(x, x, par_all(1), ALU.mult))
        ch.step(dve.tensor_tensor(x, x, par_all(2), ALU.add))
        ch.step(dve.tensor_reduce(scores[:, :, :], sums[:, :, :].rearrange("p t (h x) -> p t x h", h=heads),
                                  AX, ALU.add))
        ch.step(dve.tensor_scalar(scores[:, :, :], scores[:, :, :], 1.0 / heads, None, ALU.mult))

    @block.scalar
    def _(act):
        act.wait_ge(var_ready, 1)
        act.activation(std[:, :, :], var[:, :, :], ACT.Sqrt).then_inc(std_ready, 1)


@phase
def store_nodes(g, nodes_x, out):
    nc = g.nc
    whole = g.nodes // P
    stored = g.sem("out_stored")
    block = g.block
    @block.sync
    def _(sp):
        sp.dma_start(out[0:whole * P, :].rearrange("(t p) d -> p t d", p=P), nodes_x[:, 0:whole, :]).then_inc(
            stored, 16)
        sp.dma_start(out[whole * P:g.nodes, :], nodes_x[0:g.nodes - whole * P, whole, :]).then_inc(stored, 16)
        sp.wait_ge(stored, 32)


def build_rest(g, ins, out, hgt, gat):
    nc = g.nc
    padded = g.tiles * P
    halves = g.dim // P
    rels, heads = ins["L0_gnn_rel_pri"].shape
    types = ins["L0_gnn_skip"].shape[0]

    def table(name, shape):
        return nc.dram_tensor(name, shape, F32).ap()

    k_table, v_table = table("k_table", [rels * padded, g.dim]), table("v_table", [rels * padded, g.dim])
    h_table = table("h_table", [padded, g.dim])
    n_gat = ins["L1_ffn_W_gat"].shape[1]
    gat_heads = ins["L1_ffn_att_src"].shape[0]
    src_table, dst_table = table("src_table", [padded, n_gat + gat_heads]), table("dst_table", [padded, gat_heads])

    node_shape = [P, g.tiles, g.dim]
    x = g.sb("nodes", node_shape)

    def scoped(own, name, shape):
        return own.enter_context(nc.sbuf_tensor(name, shape, F32))

    edge_memory(g, hgt)
    edge_memory(g, gat)

    with ExitStack() as own:
        for e in (hgt, gat):
            e.packed, e.words, e.place = (
                own.enter_context(nc.sbuf_tensor(f"{e.tag}_{name}", [P, e.raw_chunks], I32))
                for name in ("packed", "words", "place"))
        y = scoped(own, "y0", node_shape)
        type_hot = scoped(own, "type_hot", [P, g.tiles, types])
        q = scoped(own, "q", node_shape)
        with together(g):
            load_nodes(g, ins["x"], x)
            load_types(g, ins["node_type_4"], type_hot)
            pack_typed(g, hgt, ins["src"], ins["dst"], ins["edge_type_8"])
            pack_looped(g, gat, ins["L1_ffn_edge_index"])
        rank_edges(g, hgt, 0)
        with together(g):
            scatter_edges(g, hgt, 0)
            rank_edges(g, gat, 0)
            layernorm(g, "ln0", x, y)
        with together(g):
            scatter_edges(g, gat, 0)
            rank_edges(g, hgt, 1)
        with together(g):
            scatter_edges(g, hgt, 1)
            rank_edges(g, gat, 1)
        with together(g):
            scatter_edges(g, gat, 1)
            hgt_project(g, ins, y, type_hot, q, k_table, v_table)
        derive_edges(g, hgt)
        att = scoped(own, "att0", [P, hgt.chunks, heads])
        hgt_scores(g, hgt, q, k_table, att)
        segment_softmax(g, hgt, att, 0.0)
        sums = scoped(own, "sums0", [P, g.tiles, g.dim + 1])
        hgt_sum(g, hgt, v_table, att, sums)
        hgt_update(g, ins, sums, y, type_hot, x)

    with ExitStack() as own:
        count = ins["L0_ffn_Wr"].shape[1]
        gates = scoped(own, "gates0", [P, g.tiles, count])
        turned = scoped(own, "turned0", [P, halves, padded])
        with ExitStack() as inner:
            y = scoped(inner, "y1", node_shape)
            logits = scoped(inner, "logits0", [P, g.tiles, count])
            layernorm(g, "ln1", x, y)
            turn_nodes(g, "ro", y, None, ins["L0_ffn_Wr"], ins["L0_ffn_br"], logits)
            top2_gates(g, "g0", logits, gates)
            layernorm(g, "ln2", y, y)
            turn_nodes(g, "t0", y, turned, None, None, None)
        experts(g, "e0", turned, gates, x, ins["L0_ffn_W1"], ins["L0_ffn_b1"], ins["L0_ffn_W2"], ins["L0_ffn_b2"],
                ins["L0_ffn_ln_g"], ins["L0_ffn_ln_b"])

    with ExitStack() as own:
        state = scoped(own, "state", [P, halves, padded])
        with ExitStack() as inner:
            y = scoped(inner, "y2", node_shape)
            layernorm(g, "ln3", x, y)
            turn_nodes(g, "t1", y, state, None, None, None)
        gated_graph(g, ins, hgt, state, 6, h_table)
        add_turned(g, "at", state, x)

    derive_edges(g, gat)
    with ExitStack() as own:
        turned = scoped(own, "turned1", [P, halves, padded])
        count = ins["L1_ffn_W1"].shape[0]
        gates = scoped(own, "gates1", [P, g.tiles, count])
        with ExitStack() as inner:
            y = scoped(inner, "y3", node_shape)
            feats = scoped(inner, "feats", [P, g.tiles, n_gat])
            layernorm(g, "ln4", x, y)
            turn_nodes(g, "t2", y, turned, ins["L1_ffn_W_gat"], None, feats)
            gat_tables(g, ins, feats, src_table, dst_table)
        with ExitStack() as inner:
            att = scoped(inner, "att1", [P, gat.chunks, gat_heads])
            edge_feats = scoped(inner, "edge_feats", [P, gat.chunks, n_gat])
            sums = scoped(inner, "sums1", [P, g.tiles, n_gat])
            scores = scoped(inner, "scores", [P, g.tiles, count])
            gat_scores(g, gat, src_table, dst_table, edge_feats, att)
            segment_softmax(g, gat, att, 1e-16)
            gat_sum(g, gat, edge_feats, att, sums)
            gat_router(g, ins, sums, scores)
            top2_gates(g, "g1", scores, gates)
        experts(g, "e1", turned, gates, x, ins["L1_ffn_W1"], ins["L1_ffn_b1"], ins["L1_ffn_W2"], ins["L1_ffn_b2"], None, None)
    store_nodes(g, x, out)


_INS = ['x', 'src', 'dst', 'edge_type_8', 'node_type_4', 'L0_gnn_Wk', 'L0_gnn_bk', 'L0_gnn_Wq', 'L0_gnn_bq',
        'L0_gnn_Wv', 'L0_gnn_bv', 'L0_gnn_Wa', 'L0_gnn_ba', 'L0_gnn_rel_att', 'L0_gnn_rel_msg', 'L0_gnn_rel_pri',
        'L0_gnn_skip', 'L0_ffn_Wr', 'L0_ffn_br', 'L0_ffn_ln_g', 'L0_ffn_ln_b', 'L0_ffn_W1', 'L0_ffn_b1',
        'L0_ffn_W2', 'L0_ffn_b2', 'L1_gnn_W1', 'L1_gnn_b1', 'L1_gnn_W2', 'L1_gnn_b2', 'L1_gnn_W_ih',
        'L1_gnn_b_ih', 'L1_gnn_W_hh', 'L1_gnn_b_hh', 'L1_ffn_W_gat', 'L1_ffn_att_src', 'L1_ffn_att_dst',
        'L1_ffn_b_gat', 'L1_ffn_ln_gamma', 'L1_ffn_ln_beta', 'L1_ffn_W1', 'L1_ffn_b1', 'L1_ffn_W2',
        'L1_ffn_b2', 'L1_ffn_edge_index']
_OUTS = [((3125, 256), 'float32')]


def kernel(**inputs):
    import numpy as _np
    import concourse.bacc as _bacc
    from concourse import mybir as _mybir
    from concourse.bass_utils import run_bass_kernel_spmd as _run

    nc = _bacc.Bacc("TRN2", target_bir_lowering=False, num_devices=1)
    arrays, ins, outs = {}, {}, []
    for name in _INS:
        a = _np.ascontiguousarray(inputs[name])
        arrays[f"in_{name}_dram"] = a
        ins[name] = nc.dram_tensor(f"in_{name}_dram", a.shape, _mybir.dt.from_np(a.dtype), kind="ExternalInput").ap()
    for i, (shape, dtype) in enumerate(_OUTS):
        dt = _mybir.dt.from_np(_np.dtype(dtype))
        outs.append(nc.dram_tensor(f"out_{i}_dram", shape, dt, kind="ExternalOutput").ap())
    build(nc, ins, outs[0])
    r = _run(nc, [arrays], core_ids=[0])
    got = tuple(r.results[0][f"out_{i}_dram"] for i in range(len(_OUTS)))
    return got[0]
```

```python
from contextlib import ExitStack, contextmanager

import numpy as np

import concourse.bass as bass
import concourse.mybir as mybir

F32 = mybir.dt.float32
BF16 = mybir.dt.bfloat16
I32 = mybir.dt.int32
U16 = mybir.dt.uint16
ALU = mybir.AluOpType
ACT = mybir.ActivationFunctionType
AX = mybir.AxisListType.X

P = 128
EPS = 1e-5
BIG = 1e30
PAD_NODE = 4095
NODE_BITS = 12
NODE_MASK = (1 << NODE_BITS) - 1
PAD_WORD = PAD_NODE << NODE_BITS
SLOTS = 8
HALF = SLOTS // 2


class Program:
    pass


class Graph:
    pass


def cdiv(a, b):
    return -(-a // b)


class Chain:

    def __init__(self, eng, sem, base=0):
        self.eng, self.sem, self.base, self.n = eng, sem, base, 0

    def inc(self, ins):
        ins.then_inc(self.sem, 1)
        self.n += 1

    def wait(self):
        self.eng.wait_ge(self.sem, self.base + self.n)

    def step(self, ins):
        self.inc(ins)
        self.wait()


def peeled(eng, n, body):
    body(0, True, n == 1)
    if n > 2:
        with eng.Fori(1, n - 1, 1) as i:
            body(i, False, False)
    if n > 1:
        body(n - 1, False, True)


def led(eng, n, body):
    body(0, True)
    if n > 1:
        with eng.Fori(1, n, 1) as i:
            body(i, False)


def gate(eng, g, sem, value):
    eng.wait_ge(sem, value)
    eng.sem_inc(g.passed[eng.engine], 1)


def phase(make):
    def run(g, *args):
        if g.shared:
            make(g, *args)
        else:
            with together(g):
                make(g, *args)
    return run


@contextmanager
def together(g):
    used = []

    def sem(name):
        used.append(g.nc.alloc_semaphore(name))
        return used[-1]

    with ExitStack() as scope, g.nc.Block() as block:
        g.shared, g.block, g.scope, outer, g.sem = True, block, scope, g.sem, sem
        yield
    g.shared, g.sem = False, outer
    g.nc.clear_and_free_semaphores(used)
    g.nc.all_engine_barrier()


@phase
def make_constants(g):
    nc = g.nc
    g.ident = g.sb("ident", [P, P])
    g.ones = g.sb("ones", [P, 256])
    g.ones_bf = g.sb("ones_bf", [P, P], BF16)
    g.before_bf = g.sb("before_bf", [P, P], BF16)
    g.from_bf = g.sb("from_bf", [P, P], BF16)
    g.count_f = g.sb("count_f", [P, 256])
    g.count_bf = g.sb("count_bf", [P, 256], BF16)
    count_i = g.sb("count_i", [P, 256], I32)
    blank = g.sem("blank")
    shaped = g.sem("shaped")
    counted = g.sem("counted")
    converted = g.sem("converted")
    block = g.block
    @block.gpsimd
    def _(pool):
        pool.memset(g.ident[:, :], 0.0).then_inc(blank, 1)
        pool.memset(g.ones[:, :], 1.0).then_inc(blank, 1)
        pool.memset(g.ones_bf[:, :], 1.0).then_inc(blank, 1)
        pool.iota(count_i[:, :], pattern=[[1, 256]], base=0, channel_multiplier=0).then_inc(counted, 1)
        pool.wait_ge(blank, 3)
        pool.affine_select(out=g.ident[:, :], in_=g.ident[:, :], compare_op=ALU.not_equal, fill=1.0,
                           base=0, pattern=[[-1, P]], channel_multiplier=1).then_inc(shaped, 1)
        pool.affine_select(out=g.before_bf[:, :], in_=g.ones_bf[:, :], compare_op=ALU.is_gt, fill=0.0,
                           base=0, pattern=[[1, P]], channel_multiplier=-1).then_inc(shaped, 1)
        pool.affine_select(out=g.from_bf[:, :], in_=g.ones_bf[:, :], compare_op=ALU.is_ge, fill=0.0,
                           base=0, pattern=[[-1, P]], channel_multiplier=1).then_inc(shaped, 1)
        pool.wait_ge(counted, 1)
        pool.wait_ge(shaped, 3)

    @block.vector
    def _(dve):
        dve.wait_ge(counted, 1)
        dve.tensor_copy(g.count_f[:, :], count_i[:, :]).then_inc(converted, 1)
        dve.tensor_copy(g.count_bf[:, :], count_i[:, :]).then_inc(converted, 1)
        dve.wait_ge(converted, 2)


@phase
def rank_words(g, tag, words, place_at, words_in, out_dram, chunks, out_chunks, digits, digit_ops, per_tile):
    nc = g.nc
    lanes = 4
    runs = chunks // lanes
    assert chunks % (2 * lanes) == 0 and chunks % SLOTS == 0 and digits <= 256
    ctx = g.scope
    def sb(name, shape, dt=F32):
        return ctx.enter_context(nc.sbuf_tensor(f"{tag}_{name}", shape, dt))

    t0 = place_at
    t1 = sb("t1", [P, chunks], I32)
    digit = sb("digit", [P, chunks], BF16)
    hot = sb("hot", [P, 2, lanes, digits], BF16)
    prod = sb("prod", [P, 2, lanes, digits])
    place = sb("place", [P, chunks])
    total = sb("total", [P, digits])
    incl = sb("incl", [P, digits])
    excl = sb("excl", [P, digits])
    start = sb("start", [P, lanes, digits])
    tiles = (digits - 1) // per_tile if per_tile else 1
    tile_total = sb("tile_total", [P, tiles])
    tile_int = sb("tile_int", [P, tiles], I32)
    tile_room = sb("tile_room", [P, tiles])
    tile_end = sb("tile_end", [P, tiles])
    tile_start = sb("tile_start", [P, tiles])
    fill = sb("fill", [P, out_chunks], I32)
    hist = ctx.enter_context(nc.psum_tensor(f"{tag}_hist", [P, lanes, 512], F32))
    rank = ctx.enter_context(nc.psum_tensor(f"{tag}_rank", [P, lanes, 512], F32))

    loaded = g.sem(f"{tag}_loaded")
    dchain = g.sem(f"{tag}_dchain")
    hot_ready = g.sem(f"{tag}_hot_ready")
    hist_done = g.sem(f"{tag}_hist_done")
    start_ready = g.sem(f"{tag}_start_ready")
    rank_ready = g.sem(f"{tag}_rank_ready")
    prod_ready = g.sem(f"{tag}_prod_ready")
    rank_moved = g.sem(f"{tag}_rank_moved")
    reduced = g.sem(f"{tag}_reduced")
    filled = g.sem(f"{tag}_filled")
    padded = g.sem(f"{tag}_padded")

    by_lane = digit[:, :].rearrange("p (q j) -> p q j", q=lanes)
    place_lane = place[:, :].rearrange("p (q j) -> p q j", q=lanes)
    count = g.count_bf[:, 0:digits].unsqueeze(1).to_broadcast([P, lanes, digits])

    block = g.block
    @block.sync
    def _(sp):
        sp.dma_start(words[:, :], words_in).then_inc(loaded, 16)
        sp.wait_ge(filled, 1)
        sp.dma_start(out_dram.rearrange("(p c) o -> p (c o)", p=P), fill[:, :]).then_inc(padded, 16)
        sp.wait_ge(padded, 16)

    @block.vector
    def _(dve):
        ch = Chain(dve, dchain)
        dve.wait_ge(loaded, 16)
        digit_ops(ch, words, t0, t1)
        ch.step(dve.tensor_copy(digit[:, :], t0[:, :]))

        def one_hot(j, b):
            dve.tensor_tensor(hot[:, b, :, :], by_lane[:, :, bass.ds(j, 1)].to_broadcast([P, lanes, digits]),
                              count, ALU.is_equal).then_inc(hot_ready, 1)

        def hist_body(i, first, last):
            for b in range(2):
                if not first:
                    dve.wait_ge(hist_done, i * 2 + (b - 1))
                one_hot(i * 2 + b, b)

        peeled(dve, runs // 2, hist_body)

        dve.wait_ge(hist_done, runs)
        ch.step(dve.tensor_reduce(total[:, :], hist[:, :, 0:digits].rearrange("p q d -> p d q"), AX, ALU.add))
        ch.step(dve.tensor_tensor_scan(incl[:, :], g.ones[:, 0:digits], total[:, :], 0.0, ALU.mult, ALU.add))
        ch.step(dve.tensor_tensor(excl[:, :], incl[:, :], total[:, :], ALU.subtract))
        if per_tile:
            real = tiles * per_tile
            by_tile = [P, tiles, per_tile]
            ch.step(dve.tensor_reduce(tile_total[:, :], total[:, 0:real].rearrange(
                "p (t d) -> p t d", d=per_tile), AX, ALU.add))
            ch.step(dve.tensor_scalar(tile_int[:, :], tile_total[:, :], float(P - 1), None, ALU.add))
            ch.step(dve.tensor_scalar(tile_int[:, :], tile_int[:, :], 7, 7, ALU.logical_shift_right,
                                      ALU.logical_shift_left))
            ch.step(dve.tensor_copy(tile_room[:, :], tile_int[:, :]))
            ch.step(dve.tensor_tensor_scan(tile_end[:, :], g.ones[:, 0:tiles], tile_room[:, :], 0.0,
                                           ALU.mult, ALU.add))
            ch.step(dve.tensor_tensor(tile_start[:, :], tile_end[:, :], tile_room[:, :], ALU.subtract))
            ex = excl[:, 0:real].rearrange("p (t d) -> p t d", d=per_tile)
            st = start[:, 0, 0:real].rearrange("p (t d) -> p t d", d=per_tile)
            ch.step(dve.tensor_tensor(st, ex, ex[:, :, 0:1].to_broadcast(by_tile), ALU.subtract))
            ch.step(dve.tensor_tensor(st, st, tile_start[:, :].unsqueeze(2).to_broadcast(by_tile), ALU.add))
            ch.step(dve.tensor_copy(start[:, 0, real:digits], tile_end[:, tiles - 1:tiles]))
        else:
            ch.step(dve.tensor_copy(start[:, 0, :], excl[:, :]))
        for q in range(1, lanes):
            ch.step(dve.tensor_tensor(start[:, q, :], start[:, q - 1, :], hist[:, q - 1, 0:digits], ALU.add))
        dve.sem_inc(start_ready, 1)

        def rank_body(i, first, last):
            for b in range(2):
                j = i * 2 + b
                if not (last and b == 1):
                    if not (first and b == 0):
                        dve.wait_ge(rank_moved, j)
                    one_hot(j + 1, 1 - b)
                dve.wait_ge(rank_ready, j + 1)
                dve.tensor_tensor(prod[:, b, :, :], rank[:, :, 0:digits], hot[:, b, :, :],
                                  ALU.mult).then_inc(prod_ready, 1)
                gate(dve, g, prod_ready, j + 1)
                dve.tensor_reduce(place_lane[:, :, bass.ds(j, 1)], prod[:, b, :, :].unsqueeze(2), AX,
                                  ALU.add).then_inc(reduced, 1)

        one_hot(0, 0)
        peeled(dve, runs // 2, rank_body)

        dve.wait_ge(reduced, runs)
        ch.step(dve.tensor_copy(t0[:, :], place[:, :]))
        ch.inc(dve.tensor_scalar(t1[:, :], t0[:, :], P - 1, None, ALU.bitwise_and))
        ch.wait()
        ch.step(dve.tensor_scalar(t0[:, :], t0[:, :], 7, None, ALU.logical_shift_right))
        ch.step(dve.scalar_tensor_tensor(out=t0[:, :], in0=t1[:, :], scalar=float(out_chunks), in1=t0[:, :],
                                         op0=ALU.mult, op1=ALU.add))

    @block.tensor
    def _(pe):
        def hist_body(i, first, last):
            for b in range(2):
                pe.wait_ge(hot_ready, i * 2 + (b + 1))
                for q in range(lanes):
                    mm = pe.matmul(hist[:, q, 0:digits], g.ones_bf[:, :], hot[:, b, q, :],
                                   start=first and b == 0, stop=last and b == 1)
                mm.then_inc(hist_done, 1)

        peeled(pe, runs // 2, hist_body)
        pe.wait_ge(start_ready, 1)
        for q in range(lanes):
            pe.matmul(rank[:, q, 0:digits], g.ones[0:1, 0:P], start[0:1, q, :], start=True, stop=True)

        def rank_body(i, first, last):
            for b in range(2):
                pe.wait_ge(hot_ready, i * 2 + (b + 1 + runs))
                for q in range(lanes):
                    mm = pe.matmul(rank[:, q, 0:digits], g.before_bf[:, :], hot[:, b, q, :],
                                   start=False, stop=True, skip_group_check=True)
                mm.then_inc(rank_ready, 1)
                pe.wait_ge(prod_ready, i * 2 + (b + 1))
                for q in range(lanes):
                    mm = pe.matmul(rank[:, q, 0:digits], g.from_bf[:, :], hot[:, b, q, :],
                                   start=False, stop=True, skip_group_check=True)
                mm.then_inc(rank_moved, 1)

        peeled(pe, runs // 2, rank_body)

    @block.gpsimd
    def _(pool):
        pool.memset(fill[:, :], PAD_WORD).then_inc(filled, 1)


@phase
def scatter_words(g, tag, words, place_at, out_dram, since, chunks):
    ctx = g.scope
    at = ctx.enter_context(g.nc.sbuf_tensor(f"{tag}_at", [P, SLOTS], I32))
    what = ctx.enter_context(g.nc.sbuf_tensor(f"{tag}_what", [P, SLOTS], I32))
    staged = g.sem(f"{tag}_staged")
    scattered = [g.sem(f"{tag}_scattered{b}") for b in range(SLOTS)]
    block = g.block

    @block.gpsimd
    def _(pool):
        def body(i, first):
            for h in range(2):
                half = slice(h * HALF, (h + 1) * HALF)
                if not first:
                    for b in range(h * HALF, (h + 1) * HALF):
                        pool.wait_ge(scattered[b], i * 16)
                now = bass.ds(i * SLOTS + (since + h * HALF), HALF)
                pool.tensor_copy(at[:, half].bitcast(U16), place_at[:, now].bitcast(U16)).then_inc(staged, 1)
                pool.tensor_copy(what[:, half].bitcast(U16), words[:, now].bitcast(U16)).then_inc(staged, 1)
                gate(pool, g, staged, i * 4 + (h * 2 + 2))
                for b in range(h * HALF, (h + 1) * HALF):
                    pool.indirect_dma_start(
                        out=out_dram, out_offset=bass.IndirectOffsetOnAxis(ap=at[:, b:b + 1], axis=0),
                        in_=what[:, b:b + 1], in_offset=None).then_inc(scattered[b], 16)

        led(pool, chunks // SLOTS, body)
        for b in range(SLOTS):
            pool.wait_ge(scattered[b], 16 * (chunks // SLOTS))


def sort_plan(g, e):
    def bits(ch, out, a, shift, mask):
        ch.step(ch.eng.tensor_scalar(out[:, :], a[:, :], shift, mask, ALU.logical_shift_right, ALU.bitwise_and))

    if e.typed:
        def low_digit(ch, words, t0, t1):
            bits(ch, t0, words, NODE_BITS - 3, 0x78)
            bits(ch, t1, words, 2 * NODE_BITS, 7)
            ch.step(ch.eng.tensor_tensor(t0[:, :], t0[:, :], t1[:, :], ALU.bitwise_or))
        low, shift = 128, 4
    else:
        def low_digit(ch, words, t0, t1):
            bits(ch, t0, words, NODE_BITS, 63)
        low, shift = 64, 6
    high = g.tiles * P >> shift

    def high_digit(ch, words, t0, t1):
        bits(ch, t0, words, NODE_BITS + shift, NODE_MASK >> shift)
        ch.step(ch.eng.tensor_scalar(t0[:, :], t0[:, :], float(high), None, ALU.min))

    return ((low, low_digit, None), (high + 1, high_digit, P >> shift))


def rank_edges(g, e, n):
    digits, digit_ops, per_tile = sort_plan(g, e)[n]
    words_in = e.once.rearrange("(p c) o -> p (c o)", p=P) if n else e.packed[:, :]
    rank_words(g, f"{e.tag}_rank{n}", e.words, e.place, words_in, e.sorted if n else e.once, e.raw_chunks,
               e.room if n else e.raw_chunks, digits, digit_ops, per_tile)


def scatter_edges(g, e, n, since=0, until=None):
    scatter_words(g, f"{e.tag}_scatter{n}_{since}", e.words, e.place, e.sorted if n else e.once, since,
                  (until or e.raw_chunks) - since)


@phase
def pack_typed(g, e, src, dst, etype):
    nc = g.nc
    edges = src.shape[0]
    rows = edges // e.raw_chunks
    assert rows * e.raw_chunks == edges and rows <= P
    ctx = g.scope
    def sb(name):
        return ctx.enter_context(nc.sbuf_tensor(f"{e.tag}_{name}", [P, e.raw_chunks], I32))

    s, d, t = sb("src"), sb("dst"), sb("typ")
    blank = g.sem(f"{e.tag}_blank")
    loaded = g.sem(f"{e.tag}_in")
    chain = g.sem(f"{e.tag}_pack")
    block = g.block
    @block.sync
    def _(sp):
        sp.wait_ge(blank, 3)
        for to, of in ((s, src), (d, dst), (t, etype)):
            sp.dma_start(to[0:rows, :], of.rearrange("(p c) -> p c", p=rows)).then_inc(loaded, 16)

    @block.vector
    def _(dve):
        dve.memset(s[:, :], 0).then_inc(blank, 1)
        dve.memset(d[:, :], PAD_NODE).then_inc(blank, 1)
        dve.memset(t[:, :], 0).then_inc(blank, 1)
        dve.wait_ge(loaded, 48)
        ch = Chain(dve, chain)
        ch.inc(dve.tensor_scalar(d[:, :], d[:, :], NODE_BITS, None, ALU.logical_shift_left))
        ch.inc(dve.tensor_scalar(t[:, :], t[:, :], 2 * NODE_BITS, None, ALU.logical_shift_left))
        ch.wait()
        ch.step(dve.tensor_tensor(s[:, :], s[:, :], d[:, :], ALU.bitwise_or))
        ch.step(dve.tensor_tensor(e.packed[:, :], s[:, :], t[:, :], ALU.bitwise_or))


@phase
def pack_looped(g, e, edge_index):
    nc = g.nc
    edges = edge_index.shape[1]
    cols = edges // P
    assert cols * P == edges and cols + g.tiles <= e.raw_chunks
    ctx = g.scope
    def sb(name):
        return ctx.enter_context(nc.sbuf_tensor(f"{e.tag}_{name}", [P, e.raw_chunks], I32))

    s, d = sb("src"), sb("dst")
    blank = g.sem(f"{e.tag}_blank")
    loaded = g.sem(f"{e.tag}_in")
    looped = g.sem(f"{e.tag}_looped")
    chain = g.sem(f"{e.tag}_pack")
    block = g.block
    @block.sync
    def _(sp):
        sp.wait_ge(blank, 2)
        for to, k in ((s, 0), (d, 1)):
            sp.dma_start(to[:, 0:cols], edge_index[k, :].rearrange("(p c) -> p c", p=P)).then_inc(loaded, 16)

    @block.gpsimd
    def _(pool):
        pool.wait_ge(blank, 2)
        for x in (s, d):
            pool.iota(x[:, cols:cols + g.tiles], pattern=[[1, g.tiles]], base=0,
                      channel_multiplier=g.tiles).then_inc(looped, 1)

    @block.vector
    def _(dve):
        dve.memset(s[:, :], 0).then_inc(blank, 1)
        dve.memset(d[:, :], PAD_NODE).then_inc(blank, 1)
        dve.wait_ge(loaded, 32)
        dve.wait_ge(looped, 2)
        ch = Chain(dve, chain)
        ch.step(dve.tensor_scalar(d[:, :], d[:, :], NODE_BITS, None, ALU.logical_shift_left))
        ch.step(dve.tensor_tensor(e.packed[:, :], s[:, :], d[:, :], ALU.bitwise_or))


def make_graph(g, tag, edges, raw_chunks, typed):
    nc = g.nc
    e = Graph()
    e.tag, e.typed, e.raw_chunks = tag, typed, raw_chunks
    used = (edges + g.tiles * (P - 1)) // P
    heads_step = 2 * SLOTS if typed else 4 * SLOTS
    e.chunks = cdiv(used, heads_step) * heads_step
    pads = raw_chunks * P - edges
    e.room = max(e.chunks, cdiv(edges + pads + g.tiles * (P - 1), P))
    e.room = cdiv(e.room, 16) * 16
    e.once = nc.dram_tensor(f"{tag}_once", [P * raw_chunks, 1], I32).ap()
    e.sorted = nc.dram_tensor(f"{tag}_sorted", [P * e.room, 1], I32).ap()
    return e


def build(nc, ins, out):
    nodes, dim = ins["x"].shape
    g = Program()
    g.shared = False
    g.nc, g.nodes, g.dim, g.tiles = nc, nodes, dim, cdiv(nodes, P)
    with ExitStack() as ctx:
        g.sb = lambda name, shape, dt=F32: ctx.enter_context(nc.sbuf_tensor(name, shape, dt))
        g.sem = lambda name: ctx.enter_context(nc.semaphore(name))
        g.passed = {nc.vector.engine: g.sem("passed_dve"), nc.gpsimd.engine: g.sem("passed_pool"),
                    nc.scalar.engine: g.sem("passed_act"), nc.tensor.engine: g.sem("passed_pe")}
        make_constants(g)

        hgt = make_graph(g, "hgt", ins["src"].shape[0], 400, True)
        gat = make_graph(g, "gat", ins["L1_ffn_edge_index"].shape[1] + g.tiles * P, 288, False)
        build_rest(g, ins, out, hgt, gat)


def edge_memory(g, e):
    n = e.chunks
    e.src_row = g.sb(f"{e.tag}_src_row", [P, n], I32)
    e.table_row = g.sb(f"{e.tag}_table_row", [P, n], I32) if e.typed else e.src_row
    e.local = g.sb(f"{e.tag}_local", [P, n])
    e.keep_f = g.sb(f"{e.tag}_keep_f", [P, n])
    e.keep_b = g.sb(f"{e.tag}_keep_b", [P, n])
    e.tile = g.sb(f"{e.tag}_tile", [1, n], I32)


@phase
def derive_edges(g, e):
    nc = g.nc
    n = e.chunks
    words = e.sorted.rearrange("(p c) o -> p (c o)", p=P)
    ctx = g.scope
    def sb(name):
        return ctx.enter_context(nc.sbuf_tensor(f"{e.tag}_{name}", [P, n], I32))

    w, before, after, dst, t0 = sb("w"), sb("before"), sb("after"), sb("dsts"), sb("dt0")
    far = ctx.enter_context(nc.sbuf_tensor(f"{e.tag}_far", [P, n], F32))
    blank = g.sem(f"{e.tag}_edge_blank")
    loaded = g.sem(f"{e.tag}_edge_loaded")
    chain = g.sem(f"{e.tag}_derive")
    block = g.block
    @block.sync
    def _(sp):
        sp.dma_start(w[:, :], words[:, 0:n]).then_inc(loaded, 16)
        sp.wait_ge(blank, 2)
        sp.dma_start(before[1:P, :], words[0:P - 1, 0:n]).then_inc(loaded, 16)
        sp.dma_start(before[0:1, 1:n], words[P - 1:P, 0:n - 1]).then_inc(loaded, 16)
        sp.dma_start(after[0:P - 1, :], words[1:P, 0:n]).then_inc(loaded, 16)
        sp.dma_start(after[P - 1:P, 0:n - 1], words[0:1, 1:n]).then_inc(loaded, 16)

    @block.vector
    def _(dve):
        dve.memset(before[:, :], 0x7fff0000).then_inc(blank, 1)
        dve.memset(after[:, :], 0x7fff0000).then_inc(blank, 1)
        dve.wait_ge(loaded, 80)
        ch = Chain(dve, chain)
        ch.inc(dve.tensor_scalar(e.src_row[:, :], w[:, :], NODE_MASK, None, ALU.bitwise_and))
        ch.inc(dve.tensor_scalar(dst[:, :], w[:, :], NODE_BITS, NODE_MASK, ALU.logical_shift_right,
                                 ALU.bitwise_and))
        for x in (w, before, after):
            ch.inc(dve.tensor_scalar(x[:, :], x[:, :], NODE_BITS, None, ALU.logical_shift_right))
        ch.wait()
        ch.inc(dve.tensor_tensor(e.keep_f[:, :], w[:, :], before[:, :], ALU.is_equal))
        ch.inc(dve.tensor_tensor(e.keep_b[:, :], w[:, :], after[:, :], ALU.is_equal))
        if e.typed:
            ch.step(dve.tensor_scalar(t0[:, :], w[:, :], NODE_BITS, None, ALU.logical_shift_right))
            ch.step(dve.scalar_tensor_tensor(out=e.table_row[:, :], in0=t0[:, :], scalar=float(g.tiles * P),
                                             in1=e.src_row[:, :], op0=ALU.mult, op1=ALU.add))
        ch.step(dve.tensor_scalar(far[:, :], dst[:, :], float(g.tiles * P), 1024.0, ALU.is_ge, ALU.mult))
        ch.step(dve.tensor_scalar(t0[:, :], dst[:, :], P - 1, None, ALU.bitwise_and))
        ch.step(dve.tensor_tensor(e.local[:, :], t0[:, :], far[:, :], ALU.add))
        ch.step(dve.tensor_scalar(t0[:, :], dst[:, :], 7, None, ALU.logical_shift_right))
        ch.step(dve.tensor_scalar(e.tile[:, :], t0[0:1, :], float(g.tiles - 1), None, ALU.min))


@phase
def load_nodes(g, x, to):
    nc = g.nc
    whole = g.nodes // P
    blank = g.sem("x_blank")
    loaded = g.sem("x_loaded")
    block = g.block
    @block.vector
    def _(dve):
        dve.memset(to[:, whole:g.tiles, :], 0.0).then_inc(blank, 1)

    @block.sync
    def _(sp):
        sp.dma_start(to[:, 0:whole, :], x[0:whole * P, :].rearrange("(t p) d -> p t d", p=P)).then_inc(loaded, 16)
        sp.wait_ge(blank, 1)
        sp.dma_start(to[0:g.nodes - whole * P, whole, :], x[whole * P:g.nodes, :]).then_inc(loaded, 16)
        sp.wait_ge(loaded, 32)


@phase
def layernorm(g, tag, src, dst):
    nc = g.nc
    tiles = g.tiles
    ctx = g.scope
    def sb(name, shape):
        return ctx.enter_context(nc.sbuf_tensor(f"{tag}_{name}", shape, F32))

    stats = sb("stats", [P, tiles, 6])
    mean, diff, var, std, rstd = (sb(n, [P, tiles, 1]) for n in ("mean", "diff", "var", "std", "rstd"))
    counted = g.sem(f"{tag}_stats")
    chain = g.sem(f"{tag}_chain")
    var_ready = g.sem(f"{tag}_var_ready")
    std_ready = g.sem(f"{tag}_std_ready")
    done = g.sem(f"{tag}_done")
    block = g.block
    @block.vector
    def _(dve):
        with dve.Fori(0, tiles, 1) as t:
            dve.bn_stats(stats[:, bass.ds(t, 1), :], src[:, bass.ds(t, 1), :]).then_inc(counted, 1)
        dve.wait_ge(counted, tiles)
        ch = Chain(dve, chain)
        even, odd = stats[:, :, 1:2], stats[:, :, 4:5]
        ch.inc(dve.tensor_tensor(mean[:, :, :], even, odd, ALU.add))
        ch.inc(dve.tensor_tensor(diff[:, :, :], even, odd, ALU.subtract))
        ch.step(dve.tensor_tensor(var[:, :, :], stats[:, :, 2:3], stats[:, :, 5:6], ALU.add))
        ch.inc(dve.tensor_scalar(mean[:, :, :], mean[:, :, :], 0.5, None, ALU.mult))
        ch.step(dve.scalar_tensor_tensor(out=diff[:, :, :], in0=diff[:, :, :], scalar=0.25,
                                         in1=diff[:, :, :], op0=ALU.mult, op1=ALU.mult))
        ch.step(dve.scalar_tensor_tensor(out=var[:, :, :], in0=var[:, :, :], scalar=1.0 / g.dim,
                                         in1=diff[:, :, :], op0=ALU.mult, op1=ALU.add))
        dve.tensor_scalar(var[:, :, :], var[:, :, :], EPS, None, ALU.add).then_inc(var_ready, 1)
        dve.wait_ge(std_ready, 1)
        ch.step(dve.reciprocal(rstd[:, :, :], std[:, :, :]))
        with dve.Fori(0, tiles, 1) as t:
            dve.tensor_scalar(dst[:, bass.ds(t, 1), :], src[:, bass.ds(t, 1), :],
                              mean[:, bass.ds(t, 1), 0], rstd[:, bass.ds(t, 1), 0],
                              ALU.subtract, ALU.mult).then_inc(done, 1)
        dve.wait_ge(done, tiles)

    @block.scalar
    def _(act):
        act.wait_ge(var_ready, 1)
        act.activation(std[:, :, :], var[:, :, :], ACT.Sqrt).then_inc(std_ready, 1)


@phase
def load_types(g, node_type, type_hot):
    nc = g.nc
    types = type_hot.shape[2]
    whole = g.nodes // P
    ctx = g.scope
    kind = ctx.enter_context(nc.sbuf_tensor("kind", [P, g.tiles], I32))
    blank, loaded, made = g.sem("kind_blank"), g.sem("kind_loaded"), g.sem("kind_made")
    shape = [P, g.tiles, types]
    block = g.block
    @block.sync
    def _(sp):
        sp.wait_ge(blank, 1)
        with nc.allow_non_contiguous_dma("one word per node"):
            sp.dma_start(kind[:, 0:whole], node_type[0:whole * P].rearrange("(t p) -> p t", p=P)).then_inc(
                loaded, 16)
            sp.dma_start(kind[0:g.nodes - whole * P, whole:whole + 1],
                         node_type[whole * P:g.nodes].rearrange("(p o) -> p o", o=1)).then_inc(loaded, 16)

    @block.vector
    def _(dve):
        dve.memset(kind[:, :], 0).then_inc(blank, 1)
        dve.wait_ge(loaded, 32)
        dve.tensor_tensor(type_hot[:, :, :], kind[:, :].unsqueeze(2).to_broadcast(shape),
                          g.count_f[:, 0:types].unsqueeze(1).to_broadcast(shape),
                          ALU.is_equal).then_inc(made, 1)
        dve.wait_ge(made, 1)


@phase
def hgt_project(g, ins, y, type_hot, q, k_table, v_table, since, until):
    nc = g.nc
    tiles = until - since
    types, dim, _ = ins["L0_gnn_Wk"].shape
    rels, heads, dk, _ = ins["L0_gnn_rel_att"].shape
    halves = dim // P
    hh = heads // halves
    wide = 3 * dim
    ctx = g.scope
    def sb(name, shape, dt=F32):
        return ctx.enter_context(nc.sbuf_tensor(f"hp{since}_{name}", shape, dt))

    def psum(name, shape):
        return ctx.enter_context(nc.psum_tensor(f"hp{since}_{name}", shape, F32))

    w = sb("w", [P, types, halves, wide])
    bias = sb("bias", [types, wide])
    rel = sb("rel", [P, 2, halves, rels, P])
    pri = sb("pri", [P, rels * heads])
    masked = sb("masked", [P, types, dim])
    hot = sb("hot", [P, types])
    xt = sb("xt", [P, types * halves, P])
    hot_t = sb("hot_t", [types, P])
    kv = sb("kv", [P, 2 * dim])
    kvt = sb("kvt", [P, 2 * halves, P])
    kr = sb("kr", [P, 2, rels, dim])
    p_xt = psum("p_xt", [P, types * halves, P])
    p_qkv = psum("p_qkv", [P, 1024])
    p_hot = p_qkv[0:types, wide:wide + P]
    p_kvt = psum("p_kvt", [P, 2 * halves, P])
    p_rel = psum("p_rel", [P, 2, 512])

    names = ("w_loaded", "rel_blank", "rel_loaded", "rel_ready", "chain", "masked_ready", "xt_done", "xt_copied",
             "qkv_done", "qkv_copied", "kvt_done", "kvt_copied", "rel_done", "rel_even", "rel_odd",
             "kv_stored")
    s = {n: g.sem(f"hp{since}_{n}") for n in names}
    steps = 2 * halves * 2
    half_rels = rels // 2

    def rel_out(i):
        return kr[:, i // (2 * halves), (i % 2) * half_rels:(i % 2 + 1) * half_rels,
                  (i // 2 % halves) * P:(i // 2 % halves + 1) * P]

    block = g.block
    @block.sync
    def _(sp):
        for n, (wt, b) in enumerate(((ins["L0_gnn_Wq"], ins["L0_gnn_bq"]), (ins["L0_gnn_Wk"], ins["L0_gnn_bk"]),
                                     (ins["L0_gnn_Wv"], ins["L0_gnn_bv"]))):
            for t in range(types):
                sp.dma_start(w[:, t, :, n * dim:(n + 1) * dim],
                             wt[t].rearrange("(h p) n -> p h n", p=P)).then_inc(s["w_loaded"], 16)
            sp.dma_start(bias[:, n * dim:(n + 1) * dim], b).then_inc(s["w_loaded"], 16)
        sp.dma_start(pri[:, :], ins["L0_gnn_rel_pri"].rearrange("(o r) h -> o (r h)", o=1).to_broadcast(
            [P, rels * heads])).then_inc(s["w_loaded"], 16)
        sp.wait_ge(s["rel_blank"], 1)
        for n, m in enumerate((ins["L0_gnn_rel_att"], ins["L0_gnn_rel_msg"])):
            for h in range(heads):
                at = h % hh * dk
                sp.dma_start(rel[at:at + dk, n, h // hh, :, at:at + dk],
                             m[:, h].rearrange("r d e -> d r e")).then_inc(s["rel_loaded"], 16)

        def body(t, first):
            sp.wait_ge(s["rel_even"], t * (steps // 2) + steps // 2)
            sp.wait_ge(s["rel_odd"], t * (steps // 2) + steps // 2)
            for n, table in enumerate((k_table, v_table)):
                sp.dma_start(table.rearrange("(r n) d -> n r d", r=rels)[bass.ds(t * P + since * P, P), :, :],
                             kr[:, n, :, :]).then_inc(s["kv_stored"], 16)

        led(sp, tiles, body)
        sp.wait_ge(s["kv_stored"], 32 * tiles)

    @block.vector
    def _(dve):
        dve.memset(rel[:, :, :, :, :], 0.0).then_inc(s["rel_blank"], 1)
        dve.wait_ge(s["w_loaded"], 16 * (3 * (types + 1) + 1))
        dve.wait_ge(s["rel_loaded"], 16 * 2 * heads)
        ch = Chain(dve, s["chain"])
        ch.step(dve.tensor_scalar(pri[:, :], pri[:, :], float(1.0 / np.sqrt(dk)), None, ALU.mult))
        pr = pri[:, :].rearrange("p (r h) -> p r h", h=heads)
        for k in range(halves):
            for h in range(hh):
                block_cols = rel[:, 0, k, :, h * dk:(h + 1) * dk]
                ch.inc(dve.tensor_tensor(block_cols, block_cols,
                                         pr[:, :, k * hh + h:k * hh + h + 1].to_broadcast([P, rels, dk]),
                                         ALU.mult))
        ch.wait()
        dve.sem_inc(s["rel_ready"], 1)

        def body(t, first):
            if not first:
                dve.wait_ge(s["xt_done"], t)
            dve.tensor_tensor(masked[:, :, :], y[:, bass.ds(t + since, 1), :].to_broadcast([P, types, dim]),
                              type_hot[:, bass.ds(t + since, 1), :].rearrange("p o k -> p (o k)").unsqueeze(2)
                              .to_broadcast([P, types, dim]), ALU.mult).then_inc(s["masked_ready"], 1)
            dve.tensor_scalar(hot[:, :].unsqueeze(1), type_hot[:, bass.ds(t + since, 1), :], 1.0, None,
                              ALU.mult).then_inc(s["masked_ready"], 1)
            dve.wait_ge(s["qkv_done"], t + 1)
            if not first:
                dve.wait_ge(s["kvt_done"], t)
            dve.tensor_copy(kv[:, :], p_qkv[:, dim:wide]).then_inc(s["qkv_copied"], 1)
            dve.tensor_scalar(q[:, bass.ds(t + since, 1), :], p_qkv[:, 0:dim].unsqueeze(1), 1.0, None,
                              ALU.mult).then_inc(s["qkv_copied"], 1)
            if not first:
                dve.wait_ge(s["kv_stored"], t * 32)
            for i in range(0, steps, 2):
                dve.wait_ge(s["rel_done"], t * steps + (i + 1))
                dve.tensor_copy(rel_out(i), p_rel[:, 0, :].rearrange("p (r e) -> p r e", e=P)).then_inc(
                    s["rel_even"], 1)

        led(dve, tiles, body)
        dve.wait_ge(s["qkv_copied"], 2 * tiles)

    @block.scalar
    def _(act):
        def body(t, first):
            act.wait_ge(s["xt_done"], t + 1)
            if not first:
                act.wait_ge(s["qkv_done"], t)
            act.copy(xt[:, :, :], p_xt[:, :, :]).then_inc(s["xt_copied"], 1)
            act.copy(hot_t[:, :], p_hot).then_inc(s["xt_copied"], 1)
            act.wait_ge(s["kvt_done"], t + 1)
            act.copy(kvt[:, :, :], p_kvt[:, :, :]).then_inc(s["kvt_copied"], 1)
            if not first:
                act.wait_ge(s["kv_stored"], t * 32)
            for i in range(1, steps, 2):
                act.wait_ge(s["rel_done"], t * steps + (i + 1))
                act.copy(rel_out(i), p_rel[:, 1, :].rearrange("p (r e) -> p r e", e=P)).then_inc(s["rel_odd"], 1)

        led(act, tiles, body)

    @block.tensor
    def _(pe):
        pe.wait_ge(s["rel_ready"], 1)

        def body(t, first):
            pe.wait_ge(s["masked_ready"], t * 2 + 2)
            if not first:
                pe.wait_ge(s["xt_copied"], t * 2)
                pe.wait_ge(s["qkv_copied"], t * 2)
            for k in range(types):
                for h in range(halves):
                    pe.transpose(p_xt[:, k * halves + h, :], masked[:, k, h * P:(h + 1) * P], g.ident[:, :])
            pe.transpose(p_hot, hot[:, :], g.ident[:, :]).then_inc(s["xt_done"], 1)
            pe.wait_ge(s["xt_copied"], t * 2 + 2)
            for c0, c1 in ((0, 512), (512, wide)):
                pe.matmul(p_qkv[:, c0:c1], hot_t[:, :], bias[:, c0:c1], start=True, stop=False)
                for k in range(types):
                    for h in range(halves):
                        last = k == types - 1 and h == halves - 1
                        mm = pe.matmul(p_qkv[:, c0:c1], xt[:, k * halves + h, :], w[:, k, h, c0:c1],
                                       start=False, stop=last)
            mm.then_inc(s["qkv_done"], 1)
            pe.wait_ge(s["qkv_copied"], t * 2 + 1)
            if not first:
                pe.wait_ge(s["kvt_copied"], t)
            for k in range(2 * halves):
                mm = pe.transpose(p_kvt[:, k, :], kv[:, k * P:(k + 1) * P], g.ident[:, :])
            mm.then_inc(s["kvt_done"], 1)
            pe.wait_ge(s["kvt_copied"], t + 1)
            for i in range(steps):
                m, h, r = i // (2 * halves), i // 2 % halves, i % 2
                seen = s["rel_odd"] if i % 2 else s["rel_even"]
                if not (first and i < 2):
                    pe.wait_ge(seen, t * (steps // 2) + i // 2)
                pe.matmul(p_rel[:, i % 2, :], kvt[:, m * halves + h, :],
                          rel[:, m, h, r * half_rels:(r + 1) * half_rels, :],
                          start=True, stop=True).then_inc(s["rel_done"], 1)

        led(pe, tiles, body)


def gather_rows(pool, g, chunks, sources, staged, used, stage_base=0, used_base=0):
    k = len(sources)

    def body(i, first):
        for h in range(2):
            if not first:
                gate(pool, g, used, i * SLOTS + (used_base + (h + 1) * HALF - SLOTS))
            for rows, stage, _, _, _ in sources:
                pool.tensor_copy(stage[:, h * HALF:(h + 1) * HALF].bitcast(U16),
                                 rows[:, bass.ds(i * SLOTS + h * HALF, HALF)].bitcast(U16)).then_inc(staged, 1)
            gate(pool, g, staged, i * (2 * k) + (stage_base + (h + 1) * k))
            for b in range(h * HALF, (h + 1) * HALF):
                for _, stage, table, slots, gathered in sources:
                    pool.indirect_dma_start(
                        out=slots[:, b, :], out_offset=None, in_=table,
                        in_offset=bass.IndirectOffsetOnAxis(ap=stage[:, b:b + 1], axis=0)).then_inc(gathered[b], 16)

    return body


def load_tiles(g, engine, e, c):
    return g.nc.values_load_multi_w_load_instructions(e.tile[0:1, bass.ds(c, HALF)], engines=[engine], min_val=0,
                                                      max_val=g.tiles - 1)[1]


def batch_hot(dve, g, e, c, hot):
    return dve.tensor_tensor(hot, g.count_f[:, 0:P].unsqueeze(1).to_broadcast([P, HALF, P]),
                             e.local[:, bass.ds(c, HALF)].unsqueeze(2).to_broadcast([P, HALF, P]), ALU.is_equal)


def dst_rows(g, tag, e, values, width):
    deep = 4
    ctx = g.scope
    hot = ctx.enter_context(g.nc.sbuf_tensor(f"{tag}_hot", [P, deep, P], F32))
    hot_t = ctx.enter_context(g.nc.sbuf_tensor(f"{tag}_hot_t", [P, deep, P], F32))
    p_hot = ctx.enter_context(g.nc.psum_tensor(f"{tag}_p_hot", [P, 2, 512], F32))
    p_rows = ctx.enter_context(g.nc.psum_tensor(f"{tag}_p_rows", [P, 2, 512], F32))
    hot_made, turned, copied, found = (g.sem(f"{tag}_{k}") for k in ("hot_made", "turned", "copied", "found"))

    def make_hot(dve, c, k, first):
        if not (first and k < deep):
            dve.wait_ge(turned, c + (1 - deep))
        dve.tensor_scalar(hot[:, k % deep, :], g.count_f[:, 0:P], e.local[:, bass.ds(c, 1)], None,
                          ALU.is_equal).then_inc(hot_made, 1)

    def turn(pe, c, k, first):
        pe.wait_ge(hot_made, c + 1)
        if not (first and k < 2):
            pe.wait_ge(copied, c - 1)
        pe.transpose(p_hot[:, k % 2, 0:P], hot[:, k % deep, :], g.ident[:, :]).then_inc(turned, 1)

    def copy(act, c, k, first):
        act.wait_ge(turned, c + 1)
        if not (first and k < deep):
            act.wait_ge(found, c + (1 - deep))
        act.copy(hot_t[:, k % deep, :], p_hot[:, k % 2, 0:P]).then_inc(copied, 1)

    def find(pe, tile, c, k, first, read):
        pe.wait_ge(copied, c + 1)
        if not (first and k < 2):
            pe.wait_ge(read, c - 1)
        pe.matmul(p_rows[:, k % 2:k % 2 + 1, 0:width], hot_t[:, k % deep, :], values[:, bass.ds(tile, 1), :],
                  start=True, stop=True).then_inc(found, 1)

    return make_hot, turn, copy, find, found, p_rows


def ahead(step, eng, c, b, lead, first, last):
    for n in (range(lead + 1) if first and b == 0 else (lead,)):
        if not (last and b + n >= SLOTS):
            step(eng, c + n, b + n, first)


@phase
def hgt_scores(g, e, q, k_table, att):
    nc = g.nc
    heads = att.shape[2]
    dk = g.dim // heads
    ctx = g.scope
    keys = ctx.enter_context(nc.sbuf_tensor("hs_keys", [P, SLOTS, g.dim], F32))
    key_rows = ctx.enter_context(nc.sbuf_tensor("hs_key_rows", [P, SLOTS], I32))
    prod = ctx.enter_context(nc.sbuf_tensor("hs_prod", [P, 2, g.dim], F32))
    staged, used, scored = g.sem("hs_staged"), g.sem("hs_used"), g.sem("hs_scored")
    got = [g.sem(f"hs_got{b}") for b in range(SLOTS)]
    make_hot, turn, copy, find, found, p_rows = dst_rows(g, "hq", e, q, g.dim)
    loops = e.chunks // SLOTS
    block = g.block

    @block.gpsimd
    def _(pool):
        led(pool, loops, gather_rows(pool, g, e.chunks, [(e.table_row, key_rows, k_table, keys, got)], staged, used))

    @block.vector
    def _(dve):
        def body(i, first, last):
            for b in range(SLOTS):
                c = i * SLOTS + b
                ahead(make_hot, dve, c, b, 3, first, last)
                dve.wait_ge(got[b], i * 16 + 16)
                dve.wait_ge(found, c + 1)
                if not (first and b < 2):
                    dve.wait_ge(scored, c - 1)
                dve.tensor_tensor(prod[:, b % 2, :], keys[:, b, :], p_rows[:, b % 2, 0:g.dim],
                                  ALU.mult).then_inc(used, 1)
                if not (first and b == 0):
                    total(c - 1, (b - 1) % 2)

        def total(c, b):
            gate(dve, g, used, c + 1)
            dve.tensor_reduce(att[:, bass.ds(c, 1), :].rearrange("p o h -> p (o h)"),
                              prod[:, b, :].rearrange("p (h d) -> p h d", d=dk), AX,
                              ALU.add).then_inc(scored, 1)

        peeled(dve, loops, body)
        total(e.chunks - 1, 1)
        dve.wait_ge(scored, e.chunks)

    @block.scalar
    def _(act):
        def body(i, first):
            for b in range(SLOTS):
                copy(act, i * SLOTS + b, b, first)

        led(act, loops, body)

    @block.tensor
    def _(pe):
        def body(i, first, last):
            for b in range(SLOTS):
                c = i * SLOTS + b
                ahead(turn, pe, c, b, 2, first, last)
                if b % HALF == 0:
                    tiles = load_tiles(g, mybir.EngineType.PE, e, c)
                find(pe, tiles[b % HALF], c, b, first, used)

        peeled(pe, loops, body)


@phase
def segment_softmax(g, e, att, tiny):
    nc = g.nc
    heads = att.shape[2]
    pieces = P // heads
    groups = e.chunks // pieces
    length = groups * P
    tag = f"{e.tag}_sm"
    ctx = g.scope
    def sb(name, shape):
        return ctx.enter_context(nc.sbuf_tensor(f"{tag}_{name}", shape, F32))

    turned = sb("turned", [P, 3, groups, P])
    value, keep_f, keep_b = (turned[:, n, :, :].rearrange("p g e -> p (g e)") for n in range(3))
    scan = sb("scan", [P, length])
    temp = sb("temp", [P, length])
    stage = sb("stage", [P, 3, P])
    stage_back = sb("stage_back", [P, P])
    least_f, least_b = sb("least_f", [P, 1]), sb("least_b", [P, 1])
    rows = sb("rows", [1, 2 * P])
    row_scan = sb("row_scan", [1, P])
    row_init = sb("row_init", [1, P])
    init = sb("init", [P, 1])
    p_turn = ctx.enter_context(nc.psum_tensor(f"{tag}_p_turn", [P, 3, P], F32))
    p_rows = ctx.enter_context(nc.psum_tensor(f"{tag}_p_rows", [P, 512], F32))
    p_init = ctx.enter_context(nc.psum_tensor(f"{tag}_p_init", [P, 512], F32))
    p_back = ctx.enter_context(nc.psum_tensor(f"{tag}_p_back", [P, 512], F32))
    names = ("staged", "turn_done", "turn_copied", "chain", "cols_ready", "rows_done", "init_ready", "init_done",
             "shifted", "exp_done", "weighed", "back_staged", "back_done", "back_copied")
    s = {n: g.sem(f"{tag}_{n}") for n in names}
    by_head = att[:, :, :].rearrange("p (c g) h -> p h c g", g=groups)
    rounds = 4

    def piece_of(keep, i):
        return keep[:, :].rearrange("p (c g) -> p c g", g=groups)[:, :, bass.ds(i, 1)].unsqueeze(1).to_broadcast(
            [P, heads, pieces, 1])

    block = g.block
    @block.vector
    def _(dve):
        def turn_body(i, first):
            if not first:
                dve.wait_ge(s["turn_done"], i)
            for n, of in enumerate((by_head[:, :, :, bass.ds(i, 1)], piece_of(e.keep_f, i),
                                    piece_of(e.keep_b, i))):
                dve.tensor_scalar(stage[:, n, :].rearrange("p (h c o) -> p h c o", h=heads, o=1), of, 1.0,
                                  None, ALU.mult).then_inc(s["staged"], 1)

        led(dve, groups, turn_body)
        dve.wait_ge(s["turn_copied"], groups)
        ch = Chain(dve, s["chain"])
        ch.inc(dve.tensor_reduce(least_f[:, :], keep_f, AX, ALU.min))
        ch.step(dve.tensor_reduce(least_b[:, :], keep_b, AX, ALU.min))
        turn = [0]

        def scan_pieces(data0, data1, op0, op1, least, neutral, back):
            turn[0] += 1
            r = turn[0]
            way = slice(None, None, -1) if back else slice(None)

            def run(initial):
                ch.step(dve.tensor_tensor_scan(scan[:, way], data0[:, way], data1[:, way], initial, op0, op1))

            run(neutral)
            dve.sem_inc(s["cols_ready"], 1)
            dve.wait_ge(s["rows_done"], r)
            ch.step(dve.tensor_copy(rows[:, :], p_rows[0:1, 0:2 * P]))
            goes_on = rows[:, P:2 * P]
            if neutral:
                ch.step(dve.tensor_scalar(goes_on, goes_on, -1.0, BIG, ALU.add, ALU.mult))
            edge = pieces - 1 if back else 0
            ch.step(dve.memset(goes_on.rearrange("o (h c) -> o h c", h=heads)[:, :, edge:edge + 1], neutral))
            ch.inc(dve.tensor_tensor_scan(row_scan[:, way], goes_on[:, way], rows[:, 0:P][:, way], neutral,
                                          op0, op1))
            ch.inc(dve.memset(row_init[:, :], neutral))
            ch.wait()
            to = row_init[:, :].rearrange("o (h c) -> o h c", h=heads)
            of = row_scan[:, :].rearrange("o (h c) -> o h c", h=heads)
            a, b = (slice(0, pieces - 1), slice(1, pieces)) if back else (slice(1, pieces),
                                                                        slice(0, pieces - 1))
            dve.tensor_copy(to[:, :, a], of[:, :, b]).then_inc(s["init_ready"], 1)
            dve.wait_ge(s["init_done"], r)
            ch.step(dve.tensor_copy(init[:, :], p_init[:, 0:1]))
            run(init[:, 0:1])

        def spread_back():
            ch.step(dve.tensor_tensor(temp[:, :], scan[:, :], keep_b, ALU.mult))
            ch.step(dve.tensor_tensor(temp[:, :], scan[:, :], temp[:, :], ALU.subtract))
            scan_pieces(keep_b, temp[:, :], ALU.mult, ALU.add, least_b, 0.0, True)

        ch.step(dve.tensor_scalar(temp[:, :], keep_f, -1.0, BIG, ALU.add, ALU.mult))
        scan_pieces(temp[:, :], value, ALU.add, ALU.max, least_f, -BIG, False)
        spread_back()
        dve.tensor_tensor(value, value, scan[:, :], ALU.subtract).then_inc(s["shifted"], 1)
        dve.wait_ge(s["exp_done"], 1)
        scan_pieces(keep_f, value, ALU.mult, ALU.add, least_f, 0.0, False)
        spread_back()
        if tiny:
            ch.step(dve.tensor_scalar(scan[:, :], scan[:, :], tiny, None, ALU.add))
        ch.step(dve.reciprocal(scan[:, :], scan[:, :]))
        dve.tensor_tensor(value, value, scan[:, :], ALU.mult).then_inc(s["weighed"], 1)
        dve.wait_ge(s["weighed"], 1)

        def back_body(i, first):
            if not first:
                dve.wait_ge(s["back_done"], i)
            dve.tensor_scalar(stage_back[:, :].unsqueeze(1), turned[:, 0, bass.ds(i, 1), :], 1.0, None,
                              ALU.mult).then_inc(s["back_staged"], 1)

        led(dve, groups, back_body)

    @block.scalar
    def _(act):
        def turn_body(i, first):
            gate(act, g, s["turn_done"], i + 1)
            act.copy(turned[:, :, bass.ds(i, 1), :], p_turn[:, :, :].unsqueeze(2)).then_inc(s["turn_copied"], 1)

        led(act, groups, turn_body)
        act.wait_ge(s["turn_copied"], groups)
        act.wait_ge(s["shifted"], 1)
        act.activation(value, value, ACT.Exp).then_inc(s["exp_done"], 1)

        def back_body(i, first):
            gate(act, g, s["back_done"], i + 1)
            act.copy(by_head[:, :, :, bass.ds(i, 1)],
                     p_back[:, 0:P].rearrange("p (h c o) -> p h c o", h=heads, o=1)).then_inc(s["back_copied"], 1)

        led(act, groups, back_body)
        act.wait_ge(s["back_copied"], groups)

    @block.tensor
    def _(pe):
        def turn_body(i, first):
            pe.wait_ge(s["staged"], i * 3 + 3)
            if not first:
                pe.wait_ge(s["turn_copied"], i)
            for n in range(3):
                mm = pe.transpose(p_turn[:, n, :], stage[:, n, :], g.ident[:, :])
            mm.then_inc(s["turn_done"], 1)

        led(pe, groups, turn_body)
        for r in range(1, rounds + 1):
            back = r % 2 == 0
            end = 0 if back else length - 1
            pe.wait_ge(s["cols_ready"], r)
            pe.transpose(p_rows[0:1, 0:P], scan[:, end:end + 1], g.ident[:, :])
            pe.transpose(p_rows[0:1, P:2 * P], (least_b if back else least_f)[:, :],
                         g.ident[:, :]).then_inc(s["rows_done"], 1)
            pe.wait_ge(s["init_ready"], r)
            pe.matmul(p_init[:, 0:1], row_init[:, :], g.ones[0:1, 0:1], start=True,
                      stop=True).then_inc(s["init_done"], 1)

        def back_body(i, first):
            pe.wait_ge(s["back_staged"], i + 1)
            if not first:
                pe.wait_ge(s["back_copied"], i)
            pe.transpose(p_back[:, 0:P], stage_back[:, :], g.ident[:, :]).then_inc(s["back_done"], 1)

        led(pe, groups, back_body)


@phase
def hgt_sum(g, e, v_table, att, sums):
    nc = g.nc
    heads = att.shape[2]
    dk = g.dim // heads
    wide = g.dim + 1
    ctx = g.scope
    def sb(name, shape, dt=F32):
        return ctx.enter_context(nc.sbuf_tensor(f"ha_{name}", shape, dt))

    values = sb("values", [P, SLOTS, g.dim])
    value_rows = sb("value_rows", [P, SLOTS], I32)
    begins = sb("begins", [P, e.chunks])
    hot = sb("hot", [P, SLOTS, P])
    weighted = sb("weighted", [P, SLOTS, wide])
    p_sum = ctx.enter_context(nc.psum_tensor("ha_p_sum", [P, 2, 512], F32))
    staged, used, hot_made, counted = g.sem("ha_staged"), g.sem("ha_used"), g.sem("ha_hot"), g.sem("ha_counted")
    summed, added, begun = g.sem("ha_summed"), g.sem("ha_added"), g.sem("ha_begun")
    got = [g.sem(f"ha_got{b}") for b in range(SLOTS)]
    n = e.chunks
    block = g.block
    @block.gpsimd
    def _(pool):
        led(pool, n // SLOTS, gather_rows(pool, g, n, [(e.table_row, value_rows, v_table, values, got)],
                                          staged, used))

    @block.vector
    def _(dve):
        dve.tensor_scalar(begins[:, :], e.keep_f[:, :], -1.0, 1.0, ALU.mult, ALU.add).then_inc(begun, 1)
        dve.memset(sums[:, :, :], 0.0).then_inc(begun, 1)
        dve.wait_ge(begun, 2)

        def add_batch(c, first):
            at = load_tiles(g, mybir.EngineType.DVE, e, c)
            for b in range(HALF):
                dve.wait_ge(summed, c + (b + 1))
                if not (first and b == 0):
                    dve.wait_ge(added, c + b)
                to = sums[:, bass.ds(at[b], 1), :]
                dve.tensor_tensor(to, to, p_sum[:, b % 2:b % 2 + 1, 0:wide], ALU.add).then_inc(added, 1)

        def body(i, first):
            for h in range(2):
                c = i * SLOTS + h * HALF
                slots = slice(h * HALF, (h + 1) * HALF)
                if not first:
                    dve.wait_ge(summed, c - HALF)
                batch_hot(dve, g, e, c, hot[:, slots, :]).then_inc(hot_made, 1)
                dve.tensor_scalar(weighted[:, slots, g.dim:wide], begins[:, bass.ds(c, HALF)].unsqueeze(2), 1.0,
                                  None, ALU.mult).then_inc(counted, 1)
                for b in range(h * HALF, (h + 1) * HALF):
                    dve.wait_ge(got[b], i * 16 + 16)
                    dve.tensor_tensor(weighted[:, b, 0:g.dim].rearrange("p (h d) -> p h d", d=dk),
                                      values[:, b, :].rearrange("p (h d) -> p h d", d=dk),
                                      att[:, bass.ds(i * SLOTS + b, 1), :].rearrange("p o h -> p (o h)")
                                      .unsqueeze(2).to_broadcast([P, heads, dk]), ALU.mult).then_inc(used, 1)
                if not (first and h == 0):
                    add_batch(c - HALF, first and h == 1)

        led(dve, n // SLOTS, body)
        add_batch(n - HALF, False)
        dve.wait_ge(added, n)

    @block.tensor
    def _(pe):
        def body(i, first):
            for b in range(SLOTS):
                c = i * SLOTS + b
                if b % HALF == 0:
                    for ready in (hot_made, counted):
                        pe.wait_ge(ready, i * 2 + (b // HALF + 1))
                pe.wait_ge(used, c + 1)
                if not (first and b < 2):
                    pe.wait_ge(added, c - 1)
                pe.matmul(p_sum[:, b % 2, 0:wide], hot[:, b, :], weighted[:, b, :],
                          start=True, stop=True).then_inc(summed, 1)

        led(pe, n // SLOTS, body)


@phase
def hgt_update(g, ins, sums, y, type_hot, nodes_x):
    nc = g.nc
    types, dim, _ = ins["L0_gnn_Wa"].shape
    halves = dim // P
    ctx = g.scope
    def sb(name, shape, dt=F32):
        return ctx.enter_context(nc.sbuf_tensor(f"hu_{name}", shape, dt))

    w = sb("w", [P, types, halves, dim])
    bias = sb("bias", [types, dim])
    skip = sb("skip", [P, types])
    mix_all = sb("mix_all", [P, g.tiles, types])
    mix = sb("mix", [P, g.tiles])
    share = sb("share", [P, g.tiles, 1])
    share_hot = sb("share_hot", [P, g.tiles, types])
    masked = sb("masked", [P, types, dim])
    hot = sb("hot", [P, types])
    xt = sb("xt", [P, types * halves, P])
    hot_t = sb("hot_t", [types, P])
    change = sb("change", [P, 1, dim])
    p_xt = ctx.enter_context(nc.psum_tensor("hu_p_xt", [P, types * halves, P], F32))
    p_hot = ctx.enter_context(nc.psum_tensor("hu_p_hot", [types, 512], F32))
    p_out = ctx.enter_context(nc.psum_tensor("hu_p_out", [P, 1, 512], F32))
    names = ("loaded", "sigmoid", "chain", "masked_ready", "xt_done", "xt_copied", "out_done", "out_read", "tail")
    s = {n: g.sem(f"hu_{n}") for n in names}
    shape = [P, g.tiles, types]
    block = g.block
    @block.sync
    def _(sp):
        for t in range(types):
            sp.dma_start(w[:, t, :, :], ins["L0_gnn_Wa"][t].rearrange("(h p) n -> p h n", p=P)).then_inc(
                s["loaded"], 16)
        sp.dma_start(bias[:, :], ins["L0_gnn_ba"]).then_inc(s["loaded"], 16)
        sp.dma_start(skip[:, :], ins["L0_gnn_skip"].rearrange("(o t) -> o t", o=1).to_broadcast(
            [P, types])).then_inc(s["loaded"], 16)

    @block.scalar
    def _(act):
        act.wait_ge(s["loaded"], 16 * (types + 2))
        act.activation(skip[:, :], skip[:, :], ACT.Sigmoid).then_inc(s["sigmoid"], 1)

        def body(t, first):
            act.wait_ge(s["xt_done"], t + 1)
            if not first:
                act.wait_ge(s["out_done"], t)
            act.copy(xt[:, :, :], p_xt[:, :, :]).then_inc(s["xt_copied"], 1)
            act.copy(hot_t[:, :], p_hot[:, 0:P]).then_inc(s["xt_copied"], 1)

        led(act, g.tiles, body)

    @block.vector
    def _(dve):
        ch = Chain(dve, s["chain"])
        ch.step(dve.tensor_scalar(share[:, :, :], sums[:, :, dim:dim + 1], 1.0, None, ALU.max))
        ch.step(dve.reciprocal(share[:, :, :], share[:, :, :]))
        ch.step(dve.tensor_tensor(share_hot[:, :, :], type_hot[:, :, :], share[:, :, :].to_broadcast(shape),
                                  ALU.mult))
        dve.wait_ge(s["sigmoid"], 1)
        ch.step(dve.tensor_tensor(mix_all[:, :, :], type_hot[:, :, :],
                                  skip[:, :].unsqueeze(1).to_broadcast(shape), ALU.mult))
        ch.step(dve.tensor_reduce(mix[:, :], mix_all[:, :, :], AX, ALU.add))

        def body(t, first):
            if not first:
                dve.wait_ge(s["xt_done"], t)
            dve.tensor_tensor(masked[:, :, :], sums[:, bass.ds(t, 1), 0:dim].to_broadcast([P, types, dim]),
                              share_hot[:, bass.ds(t, 1), :].rearrange("p o k -> p (o k)").unsqueeze(2)
                              .to_broadcast([P, types, dim]), ALU.mult).then_inc(s["masked_ready"], 1)
            dve.tensor_scalar(hot[:, :].unsqueeze(1), type_hot[:, bass.ds(t, 1), :], 1.0, None,
                              ALU.mult).then_inc(s["masked_ready"], 1)
            dve.wait_ge(s["out_done"], t + 1)
            row, x_row = y[:, bass.ds(t, 1), :], nodes_x[:, bass.ds(t, 1), :]
            dve.tensor_tensor(change[:, :, :], p_out[:, :, 0:dim], row, ALU.subtract).then_inc(s["out_read"], 1)
            dve.wait_ge(s["out_read"], t + 1)
            dve.scalar_tensor_tensor(out=x_row, in0=change[:, :, :], scalar=mix[:, bass.ds(t, 1)], in1=x_row,
                                     op0=ALU.mult, op1=ALU.add).then_inc(s["tail"], 1)
            dve.wait_ge(s["tail"], t * 2 + 1)
            dve.tensor_tensor(x_row, x_row, row, ALU.add).then_inc(s["tail"], 1)

        led(dve, g.tiles, body)
        dve.wait_ge(s["tail"], 2 * g.tiles)

    @block.tensor
    def _(pe):
        pe.wait_ge(s["loaded"], 16 * (types + 2))

        def body(t, first):
            pe.wait_ge(s["masked_ready"], t * 2 + 2)
            if not first:
                pe.wait_ge(s["xt_copied"], t * 2)
            for k in range(types):
                for h in range(halves):
                    pe.transpose(p_xt[:, k * halves + h, :], masked[:, k, h * P:(h + 1) * P], g.ident[:, :])
            pe.transpose(p_hot[:, 0:P], hot[:, :], g.ident[:, :]).then_inc(s["xt_done"], 1)
            pe.wait_ge(s["xt_copied"], t * 2 + 2)
            if not first:
                pe.wait_ge(s["out_read"], t)
            pe.matmul(p_out[:, 0, 0:dim], hot_t[:, :], bias[:, :], start=True, stop=False)
            for k in range(types):
                for h in range(halves):
                    mm = pe.matmul(p_out[:, 0, 0:dim], xt[:, k * halves + h, :], w[:, k, h, :],
                                   start=False, stop=k == types - 1 and h == halves - 1)
            mm.then_inc(s["out_done"], 1)

        led(pe, g.tiles, body)


@phase
def turn_nodes(g, tag, src, turned, weight, bias, product):
    nc = g.nc
    halves = g.dim // P
    n = weight.shape[1] if weight is not None else 0
    ctx = g.scope
    def sb(name, shape):
        return ctx.enter_context(nc.sbuf_tensor(f"{tag}_{name}", shape, F32))

    stage = sb("stage", [P, g.dim])
    now = sb("now", [P, halves, P])
    p_now = ctx.enter_context(nc.psum_tensor(f"{tag}_p_now", [P, halves, P], F32))
    names = ("loaded", "staged", "turn_done", "kept", "now_ready", "product_done", "product_read")
    s = {k: g.sem(f"{tag}_{k}") for k in names}
    if n:
        w = sb("w", [P, halves, n])
        b_row = sb("b_row", [1, n])
        p_prod = ctx.enter_context(nc.psum_tensor(f"{tag}_p_prod", [P, 1, 512], F32))
    block = g.block
    @block.sync
    def _(sp):
        if n:
            sp.dma_start(w[:, :, :], weight.rearrange("(h p) n -> p h n", p=P)).then_inc(s["loaded"], 16)
            if bias is not None:
                sp.dma_start(b_row[:, :], bias.rearrange("(o n) -> o n", o=1)).then_inc(s["loaded"], 16)

    @block.vector
    def _(dve):
        if n and bias is None:
            dve.memset(b_row[:, :], 0.0).then_inc(s["loaded"], 16)

        def body(t, first):
            if not first:
                dve.wait_ge(s["turn_done"], t)
            dve.tensor_scalar(stage[:, :].unsqueeze(1), src[:, bass.ds(t, 1), :], 1.0, None,
                              ALU.mult).then_inc(s["staged"], 1)
            if turned is not None:
                dve.wait_ge(s["turn_done"], t + 1)
                dve.tensor_scalar(turned[:, :, bass.ds(t * P, P)], p_now[:, :, :], 1.0, None,
                                  ALU.mult).then_inc(s["kept"], 1)
            if n:
                dve.wait_ge(s["product_done"], t + 1)
                dve.tensor_scalar(product[:, bass.ds(t, 1), :], p_prod[:, :, 0:n], 1.0, None,
                                  ALU.mult).then_inc(s["product_read"], 1)

        led(dve, g.tiles, body)
        if turned is not None:
            dve.wait_ge(s["kept"], g.tiles)
        if n:
            dve.wait_ge(s["product_read"], g.tiles)

    @block.scalar
    def _(act):
        if n:
            def body(t, first):
                act.wait_ge(s["turn_done"], t + 1)
                if not first:
                    act.wait_ge(s["product_done"], t)
                if turned is not None:
                    act.wait_ge(s["kept"], t + 1)
                act.copy(now[:, :, :], p_now[:, :, :]).then_inc(s["now_ready"], 1)

            led(act, g.tiles, body)

    @block.tensor
    def _(pe):
        if n:
            pe.wait_ge(s["loaded"], 32)

        def body(t, first):
            pe.wait_ge(s["staged"], t + 1)
            if not first:
                if n:
                    pe.wait_ge(s["now_ready"], t)
                if turned is not None:
                    pe.wait_ge(s["kept"], t)
            for h in range(halves):
                mm = pe.transpose(p_now[:, h, :], stage[:, h * P:(h + 1) * P], g.ident[:, :])
            mm.then_inc(s["turn_done"], 1)
            if n:
                pe.wait_ge(s["now_ready"], t + 1)
                if not first:
                    pe.wait_ge(s["product_read"], t)
                pe.matmul(p_prod[:, 0, 0:n], g.ones[0:1, 0:P], b_row[:, :], start=True, stop=False)
                for h in range(halves):
                    mm = pe.matmul(p_prod[:, 0, 0:n], now[:, h, :], w[:, h, :], start=False,
                                   stop=h == halves - 1)
                mm.then_inc(s["product_done"], 1)

        led(pe, g.tiles, body)


@phase
def top2_gates(g, tag, scores, gates):
    nc = g.nc
    n = scores.shape[2]
    shape = [P, g.tiles, n]
    ctx = g.scope
    def sb(name, width=n):
        return ctx.enter_context(nc.sbuf_tensor(f"{tag}_{name}", [P, g.tiles, width], F32))

    rest, is_top, pick = sb("rest"), sb("is_top"), [sb("pick0"), sb("pick1")]
    top, which = [sb("top0", 1), sb("top1", 1)], sb("which", 1)
    gap, ratio, first_w, second_w = sb("gap", 1), sb("ratio", 1), sb("first_w", 1), sb("second_w", 1)
    chain, gap_ready, ratio_ready = g.sem(f"{tag}_chain"), g.sem(f"{tag}_gap"), g.sem(f"{tag}_ratio")
    block = g.block
    @block.vector
    def _(dve):
        ch = Chain(dve, chain)
        count = g.count_f[:, 0:n].unsqueeze(1).to_broadcast(shape)
        of = scores
        for k in range(2):
            ch.step(dve.tensor_reduce(top[k][:, :, 0], of[:, :, :], AX, ALU.max))
            ch.step(dve.tensor_tensor(is_top[:, :, :], of[:, :, :], top[k][:, :, :].to_broadcast(shape),
                                      ALU.is_equal))
            ch.step(dve.scalar_tensor_tensor(out=is_top[:, :, :], in0=is_top[:, :, :], scalar=-2.0 * n,
                                             in1=count, op0=ALU.mult, op1=ALU.add))
            ch.step(dve.tensor_reduce(which[:, :, 0], is_top[:, :, :], AX, ALU.min))
            ch.step(dve.tensor_tensor(pick[k][:, :, :], is_top[:, :, :], which[:, :, :].to_broadcast(shape),
                                      ALU.is_equal))
            if k == 0:
                ch.step(dve.scalar_tensor_tensor(out=rest[:, :, :], in0=pick[0][:, :, :], scalar=-BIG,
                                                 in1=scores[:, :, :], op0=ALU.mult, op1=ALU.add))
                of = rest
        dve.tensor_tensor(gap[:, :, :], top[1][:, :, :], top[0][:, :, :], ALU.subtract).then_inc(gap_ready, 1)
        dve.wait_ge(ratio_ready, 1)
        ch.step(dve.tensor_scalar(first_w[:, :, :], ratio[:, :, :], 1.0, None, ALU.add))
        ch.step(dve.reciprocal(first_w[:, :, :], first_w[:, :, :]))
        ch.step(dve.tensor_tensor(second_w[:, :, :], ratio[:, :, :], first_w[:, :, :], ALU.mult))
        for k, wk in enumerate((first_w, second_w)):
            ch.step(dve.tensor_tensor(pick[k][:, :, :], pick[k][:, :, :], wk[:, :, :].to_broadcast(shape),
                                      ALU.mult))
        ch.step(dve.tensor_tensor(gates[:, :, :], pick[0][:, :, :], pick[1][:, :, :], ALU.add))

    @block.scalar
    def _(act):
        act.wait_ge(gap_ready, 1)
        act.activation(ratio[:, :, :], gap[:, :, :], ACT.Exp).then_inc(ratio_ready, 1)


@phase
def experts(g, tag, turned, gates, nodes_x, w1, b1, w2, b2, ln_g, ln_b):
    nc = g.nc
    count, dim, hidden = w1.shape
    halves, parts = dim // P, hidden // P
    span = 5
    groups = g.tiles // span
    wide = span * P
    cut = wide // 2
    assert groups * span == g.tiles and count % 2 == 0
    ctx = g.scope
    def sb(name, shape):
        return ctx.enter_context(nc.sbuf_tensor(f"{tag}_{name}", shape, F32))

    w1_sb, w2_sb = sb("w1", [P, 2, halves, hidden]), sb("w2", [P, 2, parts, dim])
    b1_sb, b2_sb = sb("b1", [P, 2, parts]), sb("b2", [1, 2, dim])
    norm = sb("norm", [P, 2, count * halves])
    xe = sb("xe", [P, halves, wide])
    hid = sb("hid", [P, parts, wide])
    p_hid = ctx.enter_context(nc.psum_tensor(f"{tag}_p_hid", [P, 2, 2, 512], F32))
    p_out = ctx.enter_context(nc.psum_tensor(f"{tag}_p_out", [P, 2, 512], F32))
    names = ("norm_loaded", "xe_ready", "hid_done", "hid_ready", "out_done", "added")
    s = {k: g.sem(f"{tag}_{k}") for k in names}
    loaded = [g.sem(f"{tag}_loaded{k}") for k in range(2)]
    gate_flat = gates[:, :, :].rearrange("p t e -> p (t e)")

    def each_group(eng, body):
        def pair(i, first):
            for b in range(2):
                def group(gr, lead):
                    body(i * (2 * groups) + (gr + b * groups), gr, b, i, first and b == 0 and lead)
                led(eng, groups, group)
        led(eng, count // 2, pair)

    block = g.block
    @block.sync
    def _(sp):
        if ln_g is not None:
            with nc.allow_non_contiguous_dma("a number per partition"):
                for k, v in enumerate((ln_g, ln_b)):
                    sp.dma_start(norm[:, k, :], v.rearrange("e (h p) -> p (e h)", p=P)).then_inc(
                        s["norm_loaded"], 16)

        def pair(i, first):
            for b in range(2):
                x = i * 2 + b
                if not first:
                    sp.wait_ge(s["added"], x * g.tiles - g.tiles)
                one = bass.ds(x, 1)
                sp.dma_start(w1_sb[:, b, :, :], w1[one].rearrange("o (h p) n -> p (o h) n", p=P)).then_inc(
                    loaded[b], 16)
                sp.dma_start(w2_sb[:, b, :, :], w2[one].rearrange("o (m p) n -> p (o m) n", p=P)).then_inc(
                    loaded[b], 16)
                with nc.allow_non_contiguous_dma("a number per partition"):
                    sp.dma_start(b1_sb[:, b, :], b1[one].rearrange("o (m p) -> p (o m)", p=P)).then_inc(
                        loaded[b], 16)
                sp.dma_start(b2_sb[:, b, :], b2[one]).then_inc(loaded[b], 16)
        led(sp, count // 2, pair)

    @block.vector
    def _(dve):
        if ln_g is not None:
            dve.wait_ge(s["norm_loaded"], 32)

        def body(n, gr, b, i, first):
            if ln_g is not None:
                if not first:
                    dve.wait_ge(s["hid_done"], n * parts)
                for h in range(halves):
                    at = bass.ds((i * 2 + b) * halves + h, 1)
                    dve.tensor_scalar(xe[:, h, :], turned[:, h, bass.ds(gr * wide, wide)], norm[:, 0, at],
                                      norm[:, 1, at], ALU.mult, ALU.add).then_inc(s["xe_ready"], 1)
            for j in range(span):
                t = gr * span + j
                dve.wait_ge(s["out_done"], n * span + (j + 1))
                if not (first and j == 0):
                    dve.wait_ge(s["added"], n * span + j)
                x_row = nodes_x[:, bass.ds(t, 1), :]
                dve.scalar_tensor_tensor(out=x_row, in0=p_out[:, j % 2:j % 2 + 1, 0:dim],
                                         scalar=gate_flat[:, bass.ds(t * count + (i * 2 + b), 1)],
                                         in1=x_row, op0=ALU.mult, op1=ALU.add).then_inc(s["added"], 1)

        each_group(dve, body)
        dve.wait_ge(s["added"], count * g.tiles)

    @block.scalar
    def _(act):
        def body(n, gr, b, i, first):
            for m in range(parts):
                act.wait_ge(s["hid_done"], n * parts + (m + 1))
                if m == 0 and not first:
                    act.wait_ge(s["out_done"], n * span)
                act.activation(hid[:, m, :].rearrange("p (k c) -> p k c", k=2), p_hid[:, m % 2, :, 0:cut],
                               ACT.Gelu, bias=b1_sb[:, b, m:m + 1]).then_inc(s["hid_ready"], 1)

        each_group(act, body)

    @block.tensor
    def _(pe):
        def body(n, gr, b, i, first):
            pe.wait_ge(loaded[b], i * 64 + 64)
            if ln_g is not None:
                pe.wait_ge(s["xe_ready"], n * halves + halves)
            for m in range(parts):
                if not (first and m < 2):
                    pe.wait_ge(s["hid_ready"], n * parts + (m - 1))
                for k in range(2):
                    for h in range(halves):
                        if ln_g is not None:
                            x = xe[:, h, k * cut:(k + 1) * cut]
                        else:
                            x = turned[:, h, bass.ds(gr * wide + k * cut, cut)]
                        mm = pe.matmul(p_hid[:, m % 2, k, 0:cut], w1_sb[:, b, h, m * P:(m + 1) * P], x,
                                       start=h == 0, stop=h == halves - 1)
                mm.then_inc(s["hid_done"], 1)
            for j in range(span):
                if j == 0:
                    pe.wait_ge(s["hid_ready"], n * parts + parts)
                if not (first and j < 2):
                    pe.wait_ge(s["added"], n * span + max(j - 1, 0))
                out = p_out[:, j % 2, 0:dim]
                pe.matmul(out, g.ones[0:1, 0:P], b2_sb[:, b, :], start=True, stop=False)
                for m in range(parts):
                    mm = pe.matmul(out, hid[:, m, j * P:(j + 1) * P], w2_sb[:, b, m, :], start=False,
                                   stop=m == parts - 1)
                mm.then_inc(s["out_done"], 1)

        each_group(pe, body)


@phase
def gated_graph(g, ins, e, state, steps, h_table, nodes_x, x_saved):
    nc = g.nc
    dim, halves, tiles = g.dim, g.dim // P, g.tiles
    span = 5
    groups = tiles // span
    wide = span * P
    cut = wide // 2
    ends = 2 * groups
    units = ends * halves
    outs = 3 * halves
    part = 400
    parts = tiles * P // part
    loops = e.chunks // SLOTS
    extra = loops - parts * outs
    assert parts * part == tiles * P and extra >= 0
    mats = ((ins["L1_gnn_W1"], 1), (ins["L1_gnn_W2"], 1), (ins["L1_gnn_W_ih"], 3), (ins["L1_gnn_W_hh"], 3))
    blocks = sum(m for _, m in mats) * halves
    W1, W2, WI, WH = 0, dim, 2 * dim, 5 * dim
    ctx = g.scope
    def sb(name, shape, dt=F32):
        return ctx.enter_context(nc.sbuf_tensor(f"gg_{name}", shape, dt))

    w = sb("w", [P, halves, blocks * P])
    b1 = sb("b1", [P, halves])
    b2 = sb("b2", [P, dim])
    b_in, b_state = sb("b_in", [P, outs]), sb("b_state", [P, outs])
    b_both = sb("b_both", [P, outs])
    from_state = sb("from_state", [P, outs, tiles * P])
    row_ids = sb("row_ids", [P, SLOTS], I32)
    hot = sb("hot", [P, SLOTS, P])
    mid = sb("mid", [P, 2, halves, wide])
    shared = sb("shared", [P, 2 * span, dim])
    rows = shared[:, 0:SLOTS, :]
    gates = sb("gates", [P, 2, 2, cut])
    fresh, move = sb("fresh", [P, 2, cut]), sb("move", [P, 2, cut])
    p_all = ctx.enter_context(nc.psum_tensor("gg_p_all", [P, 6, 512], F32))
    p_msg = ctx.enter_context(nc.psum_tensor("gg_p_msg", [P, 2, 512], F32))
    in_x = nodes_x[:, :, :].rearrange("p t d -> p (t d)")
    message = in_x.rearrange("p (h n) -> p h n", h=halves)
    plain = nodes_x[:, 0:blocks, :]

    names = ("saved", "loaded", "turned", "turn_read", "summed_bias", "mid_done", "mid_ready", "h_done", "h_ready",
             "staged", "used", "hot_made", "added", "cleared", "state_done", "state_ready", "gru_done",
             "gates_summed", "gates_made", "reset_made", "fresh_made", "chain", "updated", "restored")
    s = {k: g.sem(f"gg_{k}") for k in names}
    got = [g.sem(f"gg_got{b}") for b in range(SLOTS)]
    stored = [g.sem(f"gg_stored{b}") for b in range(2)]
    stores = [16 * cdiv(groups, 2), 16 * (groups // 2)]
    per_round = 4

    block = g.block
    @block.sync
    def _(sp):
        sp.dma_start(x_saved.rearrange("(t p) d -> p t d", p=P), nodes_x[:, :, :]).then_inc(s["saved"], 16)
        sp.wait_ge(s["saved"], 16)
        at = 0
        for m, n in mats:
            sp.dma_start(plain[:, at:at + n * halves, :], m.rearrange("(o p) i -> p o i", p=P)).then_inc(
                s["loaded"], 16)
            at += n * halves
        with nc.allow_non_contiguous_dma("a number per partition"):
            for to, of in ((b1, ins["L1_gnn_b1"]), (b_in, ins["L1_gnn_b_ih"]), (b_state, ins["L1_gnn_b_hh"])):
                sp.dma_start(to[:, :], of.rearrange("(o p) -> p o", p=P)).then_inc(s["loaded"], 16)
        sp.dma_start(b2[:, :], ins["L1_gnn_b2"].rearrange("(o n) -> o n", o=1).to_broadcast([P, dim])).then_inc(
            s["loaded"], 16)

        with sp.Fori(0, steps, 1) as step:
            for gr in range(groups):
                sp.wait_ge(s["h_ready"], step * tiles + (gr + 1) * span)
                sp.dma_start(h_table.rearrange("(n p) d -> p n d", p=P)[:, gr * span:(gr + 1) * span, :],
                             shared[:, gr % 2 * span:(gr % 2 + 1) * span, :]).then_inc(stored[gr % 2], 16)
        for b in range(2):
            sp.wait_ge(stored[b], steps * stores[b])
        sp.wait_ge(s["updated"], steps * units + units)
        sp.dma_start(nodes_x[:, :, :], x_saved.rearrange("(t p) d -> p t d", p=P)).then_inc(s["restored"], 16)
        sp.wait_ge(s["restored"], 16)

    @block.gpsimd
    def _(pool):
        pool.wait_ge(s["turn_read"], blocks // per_round * halves)
        with pool.Fori(0, steps, 1) as step:
            gate(pool, g, s["updated"], step * units + units)
            pool.memset(in_x, 0.0).then_inc(s["cleared"], 1)
            for b in range(2):
                gate(pool, g, stored[b], step * stores[b] + stores[b])
            led(pool, loops, gather_rows(pool, g, e.chunks, [(e.src_row, row_ids, h_table, rows, got)],
                                         s["staged"], s["used"], step * (2 * loops), step * e.chunks))

    @block.tensor
    def _(pe):
        pe.wait_ge(s["loaded"], 16 * 8)
        for r in range(blocks // per_round):
            for h in range(halves):
                if r or h:
                    pe.wait_ge(s["turn_read"], r * halves + h)
                for k in range(per_round):
                    mm = pe.transpose(p_all[:, 0, k * P:(k + 1) * P],
                                      plain[:, r * per_round + k, h * P:(h + 1) * P], g.ident[:, :])
                mm.then_inc(s["turned"], 1)
        pe.wait_ge(s["turn_read"], blocks // per_round * halves)

        def to_mid(gr, step):
            pe.wait_ge(s["updated"], step * units + (2 * gr + 2) * halves)
            for m in range(halves):
                if gr:
                    pe.wait_ge(s["mid_ready"], step * (groups * halves) + ((gr - 1) * halves + m + 1))
                for k in range(2):
                    at = gr * wide + k * cut
                    for h in range(halves):
                        mm = pe.matmul(p_all[:, 2 * m + k, 0:cut], w[:, h, W1 + m * P:W1 + (m + 1) * P],
                                       state[:, h, at:at + cut], start=h == 0, stop=h == halves - 1)
                mm.then_inc(s["mid_done"], 1)

        def to_h(gr, step):
            pe.wait_ge(s["mid_ready"], step * (groups * halves) + (gr + 1) * halves)
            for j in range(span):
                n = gr * span + j
                if n >= 2:
                    pe.wait_ge(s["h_ready"], step * tiles + (n - 1))
                for h in range(halves):
                    mm = pe.matmul(p_all[:, 4 + n % 2, 0:dim], mid[:, gr % 2, h, j * P:(j + 1) * P],
                                   w[:, h, W2:W2 + dim], start=h == 0, stop=h == halves - 1)
                mm.then_inc(s["h_done"], 1)

        def sum_edges(i, first, step, beside=None):
            for b in range(SLOTS):
                c = step * e.chunks + i * SLOTS + b
                if b % HALF == 0:
                    if beside:
                        beside(b // HALF)
                    pe.wait_ge(s["hot_made"], step * (2 * loops) + i * 2 + (b // HALF + 1))
                pe.wait_ge(got[b], step * (loops * 16) + i * 16 + 16)
                if not (first and b < 2):
                    pe.wait_ge(s["added"], c - 1)
                for h in range(halves):
                    mm = pe.matmul(p_msg[:, b % 2, h * P:(h + 1) * P], rows[:, b, h * P:(h + 1) * P],
                                   hot[:, b, :], start=True, stop=True)
                mm.then_inc(s["used"], 1)

        def of_state(n, m, h, first, step):
            if not first and h == 0:
                pe.wait_ge(s["state_ready"], step * (parts * outs) + n * outs + (m + 1 - outs))
            mm = pe.matmul(p_all[:, m, 0:part], w[:, h, WH + m * P:WH + (m + 1) * P],
                           state[:, h, bass.ds(n * part, part)], start=h == 0, stop=h == halves - 1)
            if h == halves - 1:
                mm.then_inc(s["state_done"], 1)

        def gru(n, first, step):
            for k in range(halves):
                if not first:
                    pe.wait_ge(s["reset_made"], step * (2 * units) + n * (2 * halves) + (2 * k - 1))
                for i in range(3):
                    col = WI + i * dim + k * P
                    for h in range(halves):
                        mm = pe.matmul(p_all[:, 3 * k + i, 0:cut], w[:, h, col:col + P],
                                       message[:, h, bass.ds(n * cut, cut)], start=h == 0, stop=h == halves - 1)
                mm.then_inc(s["gru_done"], 1)

        with pe.Fori(0, steps, 1) as step:
            pe.wait_ge(s["reset_made"], step * (2 * units) + 1)
            to_mid(0, step)
            for gr in range(groups):
                if gr + 1 < groups:
                    to_mid(gr + 1, step)
                to_h(gr, step)
            pe.wait_ge(s["h_ready"], step * tiles + tiles)

            def beside(n, first):
                for m in range(outs):
                    sum_edges(n * outs + m, first and m == 0, step, lambda h: of_state(n, m, h, first, step))

            led(pe, parts, beside)
            if extra:
                with pe.Fori(0, extra, 1) as i:
                    sum_edges(i + parts * outs, False, step)
            pe.wait_ge(s["added"], step * e.chunks + e.chunks)
            pe.wait_ge(s["state_ready"], step * (parts * outs) + parts * outs)
            led(pe, ends, lambda n, first: gru(n, first, step))

    @block.scalar
    def _(act):
        for r in range(blocks // per_round):
            for h in range(halves):
                act.wait_ge(s["turned"], r * halves + h + 1)
                act.copy(w[:, h, r * per_round * P:(r + 1) * per_round * P], p_all[:, 0, :]).then_inc(
                    s["turn_read"], 1)
        act.wait_ge(s["summed_bias"], 2)

        def keep_state(n, m, step):
            act.wait_ge(s["state_done"], step * (parts * outs) + n * outs + (m + 1))
            act.activation(from_state[:, m, bass.ds(n * part, part)], p_all[:, m, 0:part], ACT.Identity,
                           bias=b_both[:, m:m + 1]).then_inc(s["state_ready"], 1)

        def make_gates(n, k, step):
            act.wait_ge(s["gates_summed"], step * units + n * halves + (k + 1))
            act.activation(gates[:, k, :, :], gates[:, k, :, :], ACT.Sigmoid).then_inc(s["gates_made"], 1)

        def make_fresh(n, k, back, step):
            act.wait_ge(s["reset_made"], step * (2 * units) + n * (2 * halves) + (2 * k + 3 - 2 * back))
            k = (k - back) % halves
            act.activation(fresh[:, k, :], move[:, k, :], ACT.Tanh,
                           bias=b_in[:, 2 * halves + k:2 * halves + k + 1]).then_inc(s["fresh_made"], 1)

        def gru(n, first, step):
            for k in range(halves):
                make_gates(n, k, step)
                if not (first and k == 0):
                    make_fresh(n, k, 1, step)

        with act.Fori(0, steps, 1) as step:
            for gr in range(groups):
                for m in range(halves):
                    act.wait_ge(s["mid_done"], step * (groups * halves) + (gr * halves + m + 1))
                    if gr >= 2 and m == 0:
                        act.wait_ge(s["h_done"], step * tiles + (gr - 1) * span)
                    act.activation(mid[:, gr % 2, m, :].rearrange("p (k c) -> p k c", k=2),
                                   p_all[:, 2 * m:2 * m + 2, 0:cut], ACT.Relu, bias=b1[:, m:m + 1]).then_inc(
                        s["mid_ready"], 1)
            with act.Fori(0, parts, 1) as n:
                for m in range(outs):
                    keep_state(n, m, step)
            led(act, ends, lambda n, first: gru(n, first, step))
            make_fresh(ends - 1, halves - 1, 0, step)

    @block.vector
    def _(dve):
        dve.wait_ge(s["loaded"], 16 * 8)
        rz, n_part = slice(0, 2 * halves), slice(2 * halves, outs)
        dve.tensor_tensor(b_both[:, rz], b_in[:, rz], b_state[:, rz], ALU.add).then_inc(s["summed_bias"], 1)
        dve.tensor_scalar(b_both[:, n_part], b_state[:, n_part], 1.0, None, ALU.mult).then_inc(s["summed_bias"], 1)
        dve.sem_inc(s["updated"], units)
        dve.sem_inc(s["reset_made"], 1)

        def add(i_c, tile, b, first, step):
            c = step * e.chunks + i_c
            dve.wait_ge(s["used"], c + 1)
            if not first:
                dve.wait_ge(s["added"], c)
            to = message[:, :, bass.ds(tile * P, P)]
            dve.tensor_tensor(to, to, p_msg[:, b, 0:halves * P].rearrange("p (h n) -> p h n", h=halves),
                              ALU.add).then_inc(s["added"], 1)

        def add_batch(i_c, first, step):
            at = load_tiles(g, mybir.EngineType.DVE, e, i_c)
            for b in range(HALF):
                add(i_c + b, at[b], b % 2, first and b == 0, step)

        def sum_edges(i, first, step):
            for h in range(2):
                i_c = i * SLOTS + h * HALF
                if not first:
                    dve.wait_ge(s["used"], step * e.chunks + (i_c - HALF))
                batch_hot(dve, g, e, i_c, hot[:, h * HALF:(h + 1) * HALF, :]).then_inc(s["hot_made"], 1)
                if not (first and h == 0):
                    add_batch(i_c - HALF, first and h == 1, step)

        def sum_gates(n, k, step):
            dve.wait_ge(s["gru_done"], step * units + n * halves + (k + 1))
            both = from_state[:, 0:2 * halves, :].rearrange("p (i k) n -> p k i n", k=halves)
            dve.tensor_tensor(gates[:, k, :, :], p_all[:, 3 * k:3 * k + 2, 0:cut],
                              both[:, k, :, bass.ds(n * cut, cut)], ALU.add).then_inc(s["gates_summed"], 1)

        def reset(n, k, step):
            dve.wait_ge(s["gates_made"], step * units + n * halves + (k + 1))
            to = move[:, k:k + 1, :]
            dve.tensor_tensor(to, gates[:, k:k + 1, 0, :],
                              from_state[:, 2 * halves + k:2 * halves + k + 1, bass.ds(n * cut, cut)],
                              ALU.mult).then_inc(s["reset_made"], 1)
            dve.wait_ge(s["reset_made"], step * (2 * units) + n * (2 * halves) + (2 * k + 2))
            dve.tensor_tensor(to, to, p_all[:, 3 * k + 2:3 * k + 3, 0:cut], ALU.add).then_inc(s["reset_made"], 1)

        def update(n, k, step):
            done = step * (2 * units) + n * (2 * halves) + 2 * k
            old = state[:, k, bass.ds(n * cut, cut)]
            dve.wait_ge(s["fresh_made"], step * units + n * halves + (k + 1))
            dve.tensor_tensor(move[:, k, :], old, fresh[:, k, :], ALU.subtract).then_inc(s["chain"], 1)
            dve.wait_ge(s["chain"], done + 1)
            dve.tensor_tensor(move[:, k, :], move[:, k, :], gates[:, k, 1, :], ALU.mult).then_inc(s["chain"], 1)
            dve.wait_ge(s["chain"], done + 2)
            dve.tensor_tensor(old, fresh[:, k, :], move[:, k, :], ALU.add).then_inc(s["updated"], 1)

        def gru(n, first, step):
            for k in range(halves):
                if not first:
                    update(n - 1, k, step)
                if k:
                    reset(n, k - 1, step)
                elif not first:
                    reset(n - 1, halves - 1, step)
                sum_gates(n, k, step)

        with dve.Fori(0, steps, 1) as step:
            for n in range(tiles):
                gr = n // span
                if n % span == 0 and gr >= 2:
                    dve.wait_ge(stored[gr % 2], step * stores[gr % 2] + gr // 2 * 16)
                dve.wait_ge(s["h_done"], step * tiles + (n + 1))
                dve.tensor_tensor(shared[:, n % (2 * span), :], p_all[:, 4 + n % 2, 0:dim], b2[:, :],
                                  ALU.add).then_inc(s["h_ready"], 1)
            dve.wait_ge(s["cleared"], step + 1)
            led(dve, loops, lambda i, first: sum_edges(i, first, step))
            add_batch(e.chunks - HALF, False, step)
            dve.wait_ge(s["added"], step * e.chunks + e.chunks)
            dve.wait_ge(s["state_ready"], step * (parts * outs) + parts * outs)
            led(dve, ends, lambda n, first: gru(n, first, step))
            reset(ends - 1, halves - 1, step)
            for k in range(halves):
                update(ends - 1, k, step)
        dve.wait_ge(s["updated"], steps * units + units)


@phase
def add_turned(g, tag, turned, nodes_x):
    nc = g.nc
    halves = g.dim // P
    ctx = g.scope
    stage = ctx.enter_context(nc.sbuf_tensor(f"{tag}_stage", [P, halves, P], F32))
    p_back = ctx.enter_context(nc.psum_tensor(f"{tag}_p_back", [P, 1, 512], F32))
    staged, turn_done, added = g.sem(f"{tag}_staged"), g.sem(f"{tag}_turn_done"), g.sem(f"{tag}_added")
    block = g.block
    @block.vector
    def _(dve):
        def body(t, first):
            if not first:
                dve.wait_ge(turn_done, t)
            dve.tensor_scalar(stage[:, :, :], turned[:, :, bass.ds(t * P, P)], 1.0, None,
                              ALU.mult).then_inc(staged, 1)
            dve.wait_ge(turn_done, t + 1)
            row = nodes_x[:, bass.ds(t, 1), :]
            dve.tensor_tensor(row, row, p_back[:, :, 0:g.dim], ALU.add).then_inc(added, 1)

        led(dve, g.tiles, body)
        dve.wait_ge(added, g.tiles)

    @block.tensor
    def _(pe):
        def body(t, first):
            pe.wait_ge(staged, t + 1)
            if not first:
                pe.wait_ge(added, t)
            for h in range(halves):
                mm = pe.transpose(p_back[:, 0, h * P:(h + 1) * P], stage[:, h, :], g.ident[:, :])
            mm.then_inc(turn_done, 1)

        led(pe, g.tiles, body)


@phase
def gat_tables(g, ins, feats, src_table, to_row):
    nc = g.nc
    heads, per = ins["L1_ffn_att_src"].shape
    n = heads * per
    ctx = g.scope
    def sb(name, shape):
        return ctx.enter_context(nc.sbuf_tensor(f"gt_{name}", shape, F32))

    a = sb("a", [P, 2, n])
    prod = sb("prod", [P, g.tiles, n])
    from_row = sb("from_row", [P, g.tiles, n + heads])
    loaded, chain, stored = g.sem("gt_loaded"), g.sem("gt_chain"), g.sem("gt_stored")
    ready = g.sem("gt_ready")
    block = g.block
    @block.sync
    def _(sp):
        for k, v in enumerate((ins["L1_ffn_att_src"], ins["L1_ffn_att_dst"])):
            sp.dma_start(a[:, k, :], v.rearrange("(o h) x -> o (h x)", o=1).to_broadcast([P, n])).then_inc(
                loaded, 16)
        sp.wait_ge(ready, 1)
        sp.dma_start(src_table.rearrange("(t p) d -> p t d", p=P), from_row[:, :, :]).then_inc(stored, 16)
        sp.wait_ge(stored, 16)

    @block.vector
    def _(dve):
        ch = Chain(dve, chain)
        dve.wait_ge(loaded, 32)
        ch.step(dve.tensor_copy(from_row[:, :, 0:n], feats[:, :, :]))
        for k, to in enumerate((from_row[:, :, n:n + heads], to_row[:, :, :])):
            ch.step(dve.tensor_tensor(prod[:, :, :], feats[:, :, :],
                                      a[:, k, :].unsqueeze(1).to_broadcast([P, g.tiles, n]), ALU.mult))
            ch.step(dve.tensor_reduce(to, prod[:, :, :].rearrange("p t (h x) -> p t h x", h=heads), AX,
                                      ALU.add))
        dve.sem_inc(ready, 1)


@phase
def gat_scores(g, e, src_table, to_row, edge_feats, att):
    nc = g.nc
    heads = att.shape[2]
    n = edge_feats.shape[2]
    ctx = g.scope
    def sb(name, shape, dt=F32):
        return ctx.enter_context(nc.sbuf_tensor(f"gs_{name}", shape, dt))

    from_rows = sb("from_rows", [P, SLOTS, n + heads])
    from_ids = sb("from_ids", [P, SLOTS], I32)
    both = sb("both", [P, SLOTS, heads])
    staged, used, kept, scored = g.sem("gs_staged"), g.sem("gs_used"), g.sem("gs_kept"), g.sem("gs_scored")
    got_from = [g.sem(f"gs_from{b}") for b in range(SLOTS)]
    make_hot, turn, copy, find, found, p_rows = dst_rows(g, "gd", e, to_row, heads)
    loops = e.chunks // SLOTS
    block = g.block
    @block.gpsimd
    def _(pool):
        led(pool, loops, gather_rows(pool, g, e.chunks, [(e.src_row, from_ids, src_table, from_rows, got_from)],
                                     staged, kept))

    @block.vector
    def _(dve):
        def body(i, first, last):
            for b in range(SLOTS):
                c = i * SLOTS + b
                ahead(make_hot, dve, c, b, 3, first, last)
                dve.wait_ge(got_from[b], i * 16 + 16)
                dve.wait_ge(found, c + 1)
                if not first and b % HALF == 0:
                    dve.wait_ge(scored, i * 2 + (b // HALF - 1))
                dve.tensor_tensor(both[:, b, :], from_rows[:, b, n:n + heads], p_rows[:, b % 2, 0:heads],
                                  ALU.add).then_inc(used, 1)
                if b % HALF == HALF - 1:
                    slots = slice(b + 1 - HALF, b + 1)
                    at = bass.ds(i * SLOTS + (b + 1 - HALF), HALF)
                    dve.tensor_scalar(edge_feats[:, at, :], from_rows[:, slots, 0:n], 1.0, None,
                                      ALU.mult).then_inc(kept, HALF)
                    dve.wait_ge(used, c + 1)
                    dve.scalar_tensor_tensor(out=att[:, at, :], in0=both[:, slots, :], scalar=0.2,
                                             in1=both[:, slots, :], op0=ALU.mult, op1=ALU.max).then_inc(scored, 1)

        peeled(dve, loops, body)
        dve.wait_ge(scored, 2 * loops)
        dve.wait_ge(kept, e.chunks)

    @block.scalar
    def _(act):
        def body(i, first):
            for b in range(SLOTS):
                copy(act, i * SLOTS + b, b, first)

        led(act, loops, body)

    @block.tensor
    def _(pe):
        def body(i, first, last):
            for b in range(SLOTS):
                c = i * SLOTS + b
                ahead(turn, pe, c, b, 2, first, last)
                if b % HALF == 0:
                    tiles = load_tiles(g, mybir.EngineType.PE, e, c)
                find(pe, tiles[b % HALF], c, b, first, used)

        peeled(pe, loops, body)


@phase
def gat_sum(g, e, edge_feats, att, sums):
    nc = g.nc
    heads = att.shape[2]
    n = edge_feats.shape[2]
    ctx = g.scope
    hot = ctx.enter_context(nc.sbuf_tensor("gu_hot", [P, SLOTS, P], F32))
    p_sum = ctx.enter_context(nc.psum_tensor("gu_p_sum", [P, SLOTS, 512], F32))
    weighed, hot_made, summed, added = g.sem("gu_weighed"), g.sem("gu_hot_made"), g.sem("gu_summed"), g.sem("gu_added")
    block = g.block
    @block.vector
    def _(dve):
        by_head = edge_feats[:, :, :].rearrange("p c (h x) -> p (c h) x", h=heads)
        dve.tensor_tensor(by_head, by_head, att[:, :, :].rearrange("p c h -> p (c h)").unsqueeze(2)
                          .to_broadcast([P, e.chunks * heads, n // heads]), ALU.mult).then_inc(weighed, 1)
        dve.memset(sums[:, :, :], 0.0).then_inc(weighed, 1)
        dve.wait_ge(weighed, 2)

        def add_batch(c, h, first):
            at = load_tiles(g, mybir.EngineType.DVE, e, c)
            for b in range(HALF):
                dve.wait_ge(summed, c + (b + 1))
                if not (first and b == 0):
                    dve.wait_ge(added, c + b)
                to = sums[:, bass.ds(at[b], 1), :]
                bank = h * HALF + b
                dve.tensor_tensor(to, to, p_sum[:, bank:bank + 1, 0:n], ALU.add).then_inc(added, 1)

        def body(i, first):
            for h in range(2):
                c = i * SLOTS + h * HALF
                if not first:
                    dve.wait_ge(summed, c - HALF)
                batch_hot(dve, g, e, c, hot[:, h * HALF:(h + 1) * HALF, :]).then_inc(hot_made, 1)
                if not (first and h == 0):
                    add_batch(c - HALF, 1 - h, first and h == 1)

        led(dve, e.chunks // SLOTS, body)
        add_batch(e.chunks - HALF, 1, False)
        dve.wait_ge(added, e.chunks)

    @block.tensor
    def _(pe):
        pe.wait_ge(weighed, 2)

        def body(i, first):
            for b in range(SLOTS):
                c = i * SLOTS + b
                if b % HALF == 0:
                    pe.wait_ge(hot_made, i * 2 + (b // HALF + 1))
                    if not first:
                        pe.wait_ge(added, c - HALF)
                pe.matmul(p_sum[:, b:b + 1, 0:n], hot[:, b, :], edge_feats[:, bass.ds(c, 1), :],
                          start=True, stop=True).then_inc(summed, 1)

        led(pe, e.chunks // SLOTS, body)


@phase
def gat_router(g, ins, sums, scores):
    nc = g.nc
    heads, per = ins["L1_ffn_att_src"].shape
    n = heads * per
    shape = [P, g.tiles, n]
    ctx = g.scope
    def sb(name, s):
        return ctx.enter_context(nc.sbuf_tensor(f"gr_{name}", s, F32))

    par = sb("par", [P, 3, n])
    square = sb("square", shape)
    mean, var, std = sb("mean", [P, g.tiles, 1]), sb("var", [P, g.tiles, 1]), sb("std", [P, g.tiles, 1])
    loaded, chain, var_ready, std_ready = (g.sem(f"gr_{k}") for k in ("loaded", "chain", "var", "std_ready"))
    block = g.block
    @block.sync
    def _(sp):
        for k, v in enumerate((ins["L1_ffn_b_gat"], ins["L1_ffn_ln_gamma"], ins["L1_ffn_ln_beta"])):
            sp.dma_start(par[:, k, :], v.rearrange("(o n) -> o n", o=1).to_broadcast([P, n])).then_inc(
                loaded, 16)

    @block.vector
    def _(dve):
        ch = Chain(dve, chain)

        def par_all(k):
            return par[:, k, :].unsqueeze(1).to_broadcast(shape)

        x = sums[:, :, :]
        dve.wait_ge(loaded, 48)
        ch.step(dve.tensor_tensor(x, x, par_all(0), ALU.add))
        ch.step(dve.tensor_reduce(mean[:, :, 0], x, AX, ALU.add))
        ch.step(dve.tensor_scalar(mean[:, :, :], mean[:, :, :], 1.0 / n, None, ALU.mult))
        ch.step(dve.tensor_tensor(x, x, mean[:, :, :].to_broadcast(shape), ALU.subtract))
        ch.step(dve.tensor_tensor(square[:, :, :], x, x, ALU.mult))
        ch.step(dve.tensor_reduce(var[:, :, 0], square[:, :, :], AX, ALU.add))
        dve.tensor_scalar(var[:, :, :], var[:, :, :], 1.0 / n, EPS, ALU.mult, ALU.add).then_inc(var_ready, 1)
        dve.wait_ge(std_ready, 1)
        ch.step(dve.reciprocal(std[:, :, :], std[:, :, :]))
        ch.step(dve.tensor_tensor(x, x, std[:, :, :].to_broadcast(shape), ALU.mult))
        ch.step(dve.tensor_tensor(x, x, par_all(1), ALU.mult))
        ch.step(dve.tensor_tensor(x, x, par_all(2), ALU.add))
        ch.step(dve.tensor_reduce(scores[:, :, :], sums[:, :, :].rearrange("p t (h x) -> p t x h", h=heads),
                                  AX, ALU.add))
        ch.step(dve.tensor_scalar(scores[:, :, :], scores[:, :, :], 1.0 / heads, None, ALU.mult))

    @block.scalar
    def _(act):
        act.wait_ge(var_ready, 1)
        act.activation(std[:, :, :], var[:, :, :], ACT.Sqrt).then_inc(std_ready, 1)


@phase
def store_nodes(g, nodes_x, out):
    nc = g.nc
    whole = g.nodes // P
    stored = g.sem("out_stored")
    block = g.block
    @block.sync
    def _(sp):
        sp.dma_start(out[0:whole * P, :].rearrange("(t p) d -> p t d", p=P), nodes_x[:, 0:whole, :]).then_inc(
            stored, 16)
        sp.dma_start(out[whole * P:g.nodes, :], nodes_x[0:g.nodes - whole * P, whole, :]).then_inc(stored, 16)
        sp.wait_ge(stored, 32)


def build_rest(g, ins, out, hgt, gat):
    nc = g.nc
    padded = g.tiles * P
    halves = g.dim // P
    rels, heads = ins["L0_gnn_rel_pri"].shape
    types = ins["L0_gnn_skip"].shape[0]

    def table(name, shape):
        return nc.dram_tensor(name, shape, F32).ap()

    k_table, v_table = table("k_table", [rels * padded, g.dim]), table("v_table", [rels * padded, g.dim])
    h_table = table("h_table", [padded, g.dim])
    n_gat = ins["L1_ffn_W_gat"].shape[1]
    gat_heads = ins["L1_ffn_att_src"].shape[0]
    src_table = table("src_table", [padded, n_gat + gat_heads])

    node_shape = [P, g.tiles, g.dim]
    x = g.sb("nodes", node_shape)

    def scoped(own, name, shape):
        return own.enter_context(nc.sbuf_tensor(name, shape, F32))

    edge_memory(g, hgt)
    edge_memory(g, gat)

    with ExitStack() as own:
        for e in (hgt, gat):
            e.packed, e.words, e.place = (
                own.enter_context(nc.sbuf_tensor(f"{e.tag}_{name}", [P, e.raw_chunks], I32))
                for name in ("packed", "words", "place"))
        y = scoped(own, "y0", node_shape)
        type_hot = scoped(own, "type_hot", [P, g.tiles, types])
        q = scoped(own, "q", node_shape)
        with together(g):
            load_nodes(g, ins["x"], x)
            load_types(g, ins["node_type_4"], type_hot)
            pack_typed(g, hgt, ins["src"], ins["dst"], ins["edge_type_8"])
            pack_looped(g, gat, ins["L1_ffn_edge_index"])
        rank_edges(g, hgt, 0)
        with together(g):
            scatter_edges(g, hgt, 0, 0, 160)
            rank_edges(g, gat, 0)
            layernorm(g, "ln0", x, y)
        with together(g):
            scatter_edges(g, hgt, 0, 160)
            hgt_project(g, ins, y, type_hot, q, k_table, v_table, 0, 9)
        with together(g):
            scatter_edges(g, gat, 0)
            rank_edges(g, hgt, 1)
        with together(g):
            scatter_edges(g, hgt, 1, 0, 96)
            rank_edges(g, gat, 1)
        with together(g):
            scatter_edges(g, hgt, 1, 96)
            hgt_project(g, ins, y, type_hot, q, k_table, v_table, 9, 20)
        with together(g):
            scatter_edges(g, gat, 1)
            hgt_project(g, ins, y, type_hot, q, k_table, v_table, 20, g.tiles)
        derive_edges(g, hgt)
        att = scoped(own, "att0", [P, hgt.chunks, heads])
        hgt_scores(g, hgt, q, k_table, att)
        segment_softmax(g, hgt, att, 0.0)
        sums = scoped(own, "sums0", [P, g.tiles, g.dim + 1])
        hgt_sum(g, hgt, v_table, att, sums)
        hgt_update(g, ins, sums, y, type_hot, x)

    with ExitStack() as own:
        count = ins["L0_ffn_Wr"].shape[1]
        gates = scoped(own, "gates0", [P, g.tiles, count])
        turned = scoped(own, "turned0", [P, halves, padded])
        with ExitStack() as inner:
            y = scoped(inner, "y1", node_shape)
            logits = scoped(inner, "logits0", [P, g.tiles, count])
            layernorm(g, "ln1", x, y)
            turn_nodes(g, "ro", y, None, ins["L0_ffn_Wr"], ins["L0_ffn_br"], logits)
            top2_gates(g, "g0", logits, gates)
            layernorm(g, "ln2", y, y)
            turn_nodes(g, "t0", y, turned, None, None, None)
        experts(g, "e0", turned, gates, x, ins["L0_ffn_W1"], ins["L0_ffn_b1"], ins["L0_ffn_W2"], ins["L0_ffn_b2"],
                ins["L0_ffn_ln_g"], ins["L0_ffn_ln_b"])

    with ExitStack() as own:
        state = scoped(own, "state", [P, halves, padded])
        with ExitStack() as inner:
            y = scoped(inner, "y2", node_shape)
            layernorm(g, "ln3", x, y)
            turn_nodes(g, "t1", y, state, None, None, None)
        gated_graph(g, ins, hgt, state, 6, h_table, x, table("x_saved", [padded, g.dim]))
        add_turned(g, "at", state, x)

    derive_edges(g, gat)
    with ExitStack() as own:
        turned = scoped(own, "turned1", [P, halves, padded])
        count = ins["L1_ffn_W1"].shape[0]
        gates = scoped(own, "gates1", [P, g.tiles, count])
        to_row = scoped(own, "to_row", [P, g.tiles, gat_heads])
        with ExitStack() as inner:
            y = scoped(inner, "y3", node_shape)
            feats = scoped(inner, "feats", [P, g.tiles, n_gat])
            layernorm(g, "ln4", x, y)
            turn_nodes(g, "t2", y, turned, ins["L1_ffn_W_gat"], None, feats)
            gat_tables(g, ins, feats, src_table, to_row)
        with ExitStack() as inner:
            att = scoped(inner, "att1", [P, gat.chunks, gat_heads])
            edge_feats = scoped(inner, "edge_feats", [P, gat.chunks, n_gat])
            sums = scoped(inner, "sums1", [P, g.tiles, n_gat])
            scores = scoped(inner, "scores", [P, g.tiles, count])
            gat_scores(g, gat, src_table, to_row, edge_feats, att)
            segment_softmax(g, gat, att, 1e-16)
            gat_sum(g, gat, edge_feats, att, sums)
            gat_router(g, ins, sums, scores)
            top2_gates(g, "g1", scores, gates)
        experts(g, "e1", turned, gates, x, ins["L1_ffn_W1"], ins["L1_ffn_b1"], ins["L1_ffn_W2"], ins["L1_ffn_b2"], None, None)
    store_nodes(g, x, out)


_INS = ['x', 'src', 'dst', 'edge_type_8', 'node_type_4', 'L0_gnn_Wk', 'L0_gnn_bk', 'L0_gnn_Wq', 'L0_gnn_bq',
        'L0_gnn_Wv', 'L0_gnn_bv', 'L0_gnn_Wa', 'L0_gnn_ba', 'L0_gnn_rel_att', 'L0_gnn_rel_msg', 'L0_gnn_rel_pri',
        'L0_gnn_skip', 'L0_ffn_Wr', 'L0_ffn_br', 'L0_ffn_ln_g', 'L0_ffn_ln_b', 'L0_ffn_W1', 'L0_ffn_b1',
        'L0_ffn_W2', 'L0_ffn_b2', 'L1_gnn_W1', 'L1_gnn_b1', 'L1_gnn_W2', 'L1_gnn_b2', 'L1_gnn_W_ih',
        'L1_gnn_b_ih', 'L1_gnn_W_hh', 'L1_gnn_b_hh', 'L1_ffn_W_gat', 'L1_ffn_att_src', 'L1_ffn_att_dst',
        'L1_ffn_b_gat', 'L1_ffn_ln_gamma', 'L1_ffn_ln_beta', 'L1_ffn_W1', 'L1_ffn_b1', 'L1_ffn_W2',
        'L1_ffn_b2', 'L1_ffn_edge_index']
_OUTS = [((3125, 256), 'float32')]


def kernel(**inputs):
    import numpy as _np
    import concourse.bacc as _bacc
    from concourse import mybir as _mybir
    from concourse.bass_utils import run_bass_kernel_spmd as _run

    nc = _bacc.Bacc("TRN2", target_bir_lowering=False, num_devices=1)
    arrays, ins, outs = {}, {}, []
    for name in _INS:
        a = _np.ascontiguousarray(inputs[name])
        arrays[f"in_{name}_dram"] = a
        ins[name] = nc.dram_tensor(f"in_{name}_dram", a.shape, _mybir.dt.from_np(a.dtype), kind="ExternalInput").ap()
    for i, (shape, dtype) in enumerate(_OUTS):
        dt = _mybir.dt.from_np(_np.dtype(dtype))
        outs.append(nc.dram_tensor(f"out_{i}_dram", shape, dt, kind="ExternalOutput").ap())
    build(nc, ins, outs[0])
    r = _run(nc, [arrays], core_ids=[0])
    got = tuple(r.results[0][f"out_{i}_dram"] for i in range(len(_OUTS)))
    return got[0]
```
